# Optimizing a Trainium2 kernel written in Bass

```python
import numpy as np
import jax
import jax.numpy as jnp

def _softmax(x, axis=-1):
    return jax.nn.softmax(x, axis=axis)

def _gelu(x):
    return jax.nn.gelu(x, approximate=True)

def _silu(x):
    return jax.nn.silu(x)

def _sigmoid(x):
    return jax.nn.sigmoid(x)

def _layernorm(x, axis=-1, eps=1e-05):
    m = jnp.mean(x, axis=axis, keepdims=True)
    v = jnp.var(x, axis=axis, keepdims=True)
    return (x - m) / jnp.sqrt(v + eps)

def _scatter_add(tgt, idx, src, axis=0):
    return tgt.at[idx].add(src)

def _segment_sum(src, seg, n):
    return jax.ops.segment_sum(src, seg, n)
kernel_name = 'mk_xattn_ffn_d2_seqx_r4_a01c77'

def setup_inputs(seed: int=0):
    np.random.seed(seed)
    _w = jnp.asarray

    def _rec_inputs():
        import jax
        import jax.numpy as jnp
        _rk = jax.random.key(seed)
        x = -0.0002928 + 1 * jax.random.normal(jax.random.fold_in(_rk, 1), (1, 2048, 256), jnp.float32)
        _lenS = 2048 - jax.random.randint(jax.random.fold_in(_rk, 7), (1,), 0, max(1, 2048 // 4) + 1, jnp.int32)
        _lenS2 = 1601 - jax.random.randint(jax.random.fold_in(_rk, 8), (1,), 0, max(1, 1601 // 4) + 1, jnp.int32)
        _ctx_1024P = jax.random.normal(jax.random.fold_in(_rk, 11), (1, 16, 256), jnp.float32)
        _ctx_1024c = jax.random.dirichlet(jax.random.fold_in(_rk, 511), 0.3 * jnp.ones((16,), jnp.float32), (1, 1601))
        _ctx_1024t = jnp.einsum('bsk,bkd->bsd', _ctx_1024c, _ctx_1024P)
        _ctx_1024t = _ctx_1024t * jax.lax.rsqrt(jnp.mean(jnp.square(_ctx_1024t)) + 1e-12) * 0.953939
        ctx_1024 = -1.39393e-06 + 0.999914 * (_ctx_1024t + 0.3 * jax.random.normal(jax.random.fold_in(_rk, 611), (1, 1601, 256), jnp.float32))
        _validS = jnp.arange(2048)[None, :] < _lenS[:, None]
        _validS2 = jnp.arange(1601)[None, :] < _lenS2[:, None]
        _causal = jnp.tril(jnp.ones((2048, 2048), dtype=bool))
        mask_Bx1xSxS2_bk1 = jnp.broadcast_to(_validS2[:, None, None, :], (1, 1, 2048, 1601))
        return (x, ctx_1024, mask_Bx1xSxS2_bk1)
    x, ctx_1024, mask_Bx1xSxS2_bk1 = _rec_inputs()

    def _L0_xattn_setup():
        import jax, jax.numpy as jnp
        import numpy as np
        B, L, D, H = (2, 512, 256, 16)
        DH = D // H
        NEG_INF = 1000000000000.0

        def _split_heads(x):
            b, l, _ = x.shape
            return x.reshape(b, l, H, DH).transpose(0, 2, 1, 3)
        key = jax.random.key(seed)
        ks = jax.random.split(key, 12)
        s_in = 1.0 / np.sqrt(D)
        inp = {'q': jax.random.normal(ks[0], (B, L, D), jnp.float32), 'k': jax.random.normal(ks[1], (B, L, D), jnp.float32), 'v': jax.random.normal(ks[2], (B, L, D), jnp.float32), 'mask': jnp.broadcast_to(jnp.triu(jnp.ones((L, L), jnp.bool_), k=1)[None, None], (B, 1, L, L)), 'Wq': jax.random.normal(ks[3], (D, D), jnp.float32) * s_in, 'bq': jnp.zeros((D,), jnp.float32), 'Wk': jax.random.normal(ks[4], (D, D), jnp.float32) * s_in, 'bk': jnp.zeros((D,), jnp.float32), 'Wv': jax.random.normal(ks[5], (D, D), jnp.float32) * s_in, 'bv': jnp.zeros((D,), jnp.float32), 'Wo': jax.random.normal(ks[6], (D, D), jnp.float32) * s_in, 'bo': jnp.zeros((D,), jnp.float32)}
        return inp
    _L0_xattn_all = _L0_xattn_setup()
    _L0_xattn_in = {k: v for k, v in _L0_xattn_all.items() if k in ('Wq', 'bq', 'Wk', 'bk', 'Wv', 'bv', 'Wo', 'bo')}
    del _L0_xattn_all

    def _L0_ffn_setup():
        import jax, jax.numpy as jnp
        import numpy as np
        key = jax.random.key(seed)
        ks = jax.random.split(key, 5)
        B, T, D, E = (4, 512, 256, 8)
        inputs = jax.random.normal(ks[0], (B, T, D), dtype=jnp.float32)
        Wr = jax.random.normal(ks[1], (D, E), dtype=jnp.float32) * 0.02
        br = jnp.zeros((E,), dtype=jnp.float32)
        W1 = jax.random.normal(ks[2], (E, D, D), dtype=jnp.float32) * 0.02
        b1 = jnp.zeros((E, D), dtype=jnp.float32)
        W2 = jax.random.normal(ks[3], (E, D, D), dtype=jnp.float32) * 0.02
        b2 = jnp.zeros((E, D), dtype=jnp.float32)
        return {'inputs': inputs, 'Wr': Wr, 'br': br, 'W1': W1, 'b1': b1, 'W2': W2, 'b2': b2}
    _L0_ffn_all = _L0_ffn_setup()
    _L0_ffn_in = {k: v for k, v in _L0_ffn_all.items() if k in ('Wr', 'br', 'W1', 'b1', 'W2', 'b2')}
    del _L0_ffn_all

    def _L1_xattn_setup():
        import jax, jax.numpy as jnp
        import numpy as np
        EMBED_DIM = 256
        NUM_HEADS = 16
        HEAD_DIM = EMBED_DIM // NUM_HEADS
        key = jax.random.key(seed)
        ks = jax.random.split(key, 11)
        s = 1.0 / np.sqrt(EMBED_DIM)
        inp = {'query': jax.random.normal(ks[0], (4, 512, EMBED_DIM), jnp.float32), 'key': jax.random.normal(ks[1], (4, 512, EMBED_DIM), jnp.float32), 'value': jax.random.normal(ks[2], (4, 512, EMBED_DIM), jnp.float32), 'Wq': jax.random.uniform(ks[3], (EMBED_DIM, EMBED_DIM), jnp.float32, -s, s), 'bq': jax.random.uniform(ks[4], (EMBED_DIM,), jnp.float32, -s, s), 'Wk': jax.random.uniform(ks[5], (EMBED_DIM, EMBED_DIM), jnp.float32, -s, s), 'bk': jax.random.uniform(ks[6], (EMBED_DIM,), jnp.float32, -s, s), 'Wv': jax.random.uniform(ks[7], (EMBED_DIM, EMBED_DIM), jnp.float32, -s, s), 'bv': jax.random.uniform(ks[8], (EMBED_DIM,), jnp.float32, -s, s), 'Wo': jax.random.uniform(ks[9], (EMBED_DIM, EMBED_DIM), jnp.float32, -s, s), 'bo': jax.random.uniform(ks[10], (EMBED_DIM,), jnp.float32, -s, s)}
        return inp
    _L1_xattn_all = _L1_xattn_setup()
    _L1_xattn_in = {k: v for k, v in _L1_xattn_all.items() if k in ('Wq', 'bq', 'Wk', 'bk', 'Wv', 'bv', 'Wo', 'bo')}
    del _L1_xattn_all

    def _L1_ffn_setup():
        import jax, jax.numpy as jnp
        import numpy as np
        BS, L, D = (4, 512, 256)
        H, E, K = (8, 16, 2)
        HD = D // H
        I = 1024 // H
        key = jax.random.key(seed)
        ks = jax.random.split(key, 10)
        s = lambda k, shp, fan: jax.random.normal(k, shp, jnp.float32) / np.sqrt(fan)
        return {'x': jax.random.normal(ks[0], (BS, L, D), jnp.float32), 'Wm': s(ks[1], (D, D), D), 'bm': jnp.zeros((D,), jnp.float32), 'expert_emb': jax.random.normal(ks[2], (HD, E), jnp.float32), 'W1': s(ks[3], (E, HD, I), HD), 'b1': jnp.zeros((E, I), jnp.float32), 'W2': s(ks[4], (E, I, HD), I), 'b2': jnp.zeros((E, HD), jnp.float32), 'Wo': s(ks[5], (D, D), D), 'bo': jnp.zeros((D,), jnp.float32)}
    _L1_ffn_all = _L1_ffn_setup()
    _L1_ffn_in = {k: v for k, v in _L1_ffn_all.items() if k in ('Wm', 'bm', 'expert_emb', 'W1', 'b1', 'W2', 'b2', 'Wo', 'bo')}
    del _L1_ffn_all
    return {'x': x, 'ctx_1024': ctx_1024, 'mask_Bx1xSxS2_bk1': mask_Bx1xSxS2_bk1, 'L0_xattn_Wq': _L0_xattn_in['Wq'], 'L0_xattn_bq': _L0_xattn_in['bq'], 'L0_xattn_Wk': _L0_xattn_in['Wk'], 'L0_xattn_bk': _L0_xattn_in['bk'], 'L0_xattn_Wv': _L0_xattn_in['Wv'], 'L0_xattn_bv': _L0_xattn_in['bv'], 'L0_xattn_Wo': _L0_xattn_in['Wo'], 'L0_xattn_bo': _L0_xattn_in['bo'], 'L0_ffn_Wr': _L0_ffn_in['Wr'], 'L0_ffn_br': _L0_ffn_in['br'], 'L0_ffn_W1': _L0_ffn_in['W1'], 'L0_ffn_b1': _L0_ffn_in['b1'], 'L0_ffn_W2': _L0_ffn_in['W2'], 'L0_ffn_b2': _L0_ffn_in['b2'], 'L1_xattn_Wq': _L1_xattn_in['Wq'], 'L1_xattn_bq': _L1_xattn_in['bq'], 'L1_xattn_Wk': _L1_xattn_in['Wk'], 'L1_xattn_bk': _L1_xattn_in['bk'], 'L1_xattn_Wv': _L1_xattn_in['Wv'], 'L1_xattn_bv': _L1_xattn_in['bv'], 'L1_xattn_Wo': _L1_xattn_in['Wo'], 'L1_xattn_bo': _L1_xattn_in['bo'], 'L1_ffn_Wm': _L1_ffn_in['Wm'], 'L1_ffn_bm': _L1_ffn_in['bm'], 'L1_ffn_expert_emb': _L1_ffn_in['expert_emb'], 'L1_ffn_W1': _L1_ffn_in['W1'], 'L1_ffn_b1': _L1_ffn_in['b1'], 'L1_ffn_W2': _L1_ffn_in['W2'], 'L1_ffn_b2': _L1_ffn_in['b2'], 'L1_ffn_Wo': _L1_ffn_in['Wo'], 'L1_ffn_bo': _L1_ffn_in['bo']}

def reference(x, ctx_1024, mask_Bx1xSxS2_bk1, L0_xattn_Wq, L0_xattn_bq, L0_xattn_Wk, L0_xattn_bk, L0_xattn_Wv, L0_xattn_bv, L0_xattn_Wo, L0_xattn_bo, L0_ffn_Wr, L0_ffn_br, L0_ffn_W1, L0_ffn_b1, L0_ffn_W2, L0_ffn_b2, L1_xattn_Wq, L1_xattn_bq, L1_xattn_Wk, L1_xattn_bk, L1_xattn_Wv, L1_xattn_bv, L1_xattn_Wo, L1_xattn_bo, L1_ffn_Wm, L1_ffn_bm, L1_ffn_expert_emb, L1_ffn_W1, L1_ffn_b1, L1_ffn_W2, L1_ffn_b2, L1_ffn_Wo, L1_ffn_bo):
    import jax
    import jax.numpy as jnp

    def _L0_xattn_ref(q, k, v, mask, Wq, bq, Wk, bk, Wv, bv, Wo, bo):
        import jax, jax.numpy as jnp
        import numpy as np
        B, L, D, H = (2, 512, 256, 16)
        DH = D // H
        NEG_INF = 1000000000000.0

        def _split_heads(x):
            b, l, _ = x.shape
            return x.reshape(b, l, H, DH).transpose(0, 2, 1, 3)
        Q = _split_heads(q @ Wq + bq)
        K = _split_heads(k @ Wk + bk)
        V = _split_heads(v @ Wv + bv)
        scale = 1.0 / np.sqrt(DH)
        dots = jnp.einsum('bhqd,bhkd->bhqk', Q, K) * scale
        dots = jnp.where(mask, -NEG_INF, dots)
        attn = jax.nn.softmax(dots, axis=-1)
        out = jnp.einsum('bhqk,bhkd->bhqd', attn, V)
        out = out.transpose(0, 2, 1, 3).reshape(q.shape[0], q.shape[1], D)
        return out @ Wo + bo

    def _L0_ffn_ref(inputs, Wr, br, W1, b1, W2, b2):
        import jax, jax.numpy as jnp
        import numpy as np
        B, T, D = inputs.shape
        E = Wr.shape[1]
        x = inputs.reshape(B * T, D)
        N = x.shape[0]
        C = N // E
        logits = x @ Wr + br
        probs = jax.nn.softmax(logits, axis=-1)
        gate = jnp.max(probs, axis=-1, keepdims=True)
        idx = jnp.argmax(probs, axis=-1)
        mask = jax.nn.one_hot(idx, E, dtype=jnp.float32)
        pos = (jnp.cumsum(mask, axis=0) * mask).astype(jnp.int32)
        mask = mask * (pos < C).astype(jnp.float32)
        mask_flat = jnp.sum(mask, axis=-1, keepdims=True)
        gate = gate * mask_flat
        combine = (gate * mask_flat * jax.nn.one_hot(idx, E, dtype=jnp.float32))[..., None] * jax.nn.one_hot(pos, C, dtype=jnp.float32)
        dispatch = combine
        expert_in = jnp.einsum('nd,nec->ecd', x, dispatch)
        h = jax.nn.relu(jnp.einsum('ecd,edf->ecf', expert_in, W1) + b1[:, None, :])
        eo = jnp.einsum('ecf,efd->ecd', h, W2) + b2[:, None, :]
        out = jnp.einsum('ecd,nec->nd', eo, combine)
        return out.reshape(B, T, D)

    def _L1_xattn_ref(query, key, value, Wq, bq, Wk, bk, Wv, bv, Wo, bo):
        import jax, jax.numpy as jnp
        import numpy as np
        EMBED_DIM = 256
        NUM_HEADS = 16
        HEAD_DIM = EMBED_DIM // NUM_HEADS
        B, T, E = query.shape
        S = key.shape[1]
        H, D = (NUM_HEADS, HEAD_DIM)
        q = (query @ Wq.T + bq).reshape(B, T, H, D).transpose(0, 2, 1, 3)
        k = (key @ Wk.T + bk).reshape(B, S, H, D).transpose(0, 2, 1, 3)
        v = (value @ Wv.T + bv).reshape(B, S, H, D).transpose(0, 2, 1, 3)
        scores = jnp.einsum('bhtd,bhsd->bhts', q, k) / np.sqrt(D)
        causal = jnp.triu(jnp.full((T, S), -jnp.inf, jnp.float32), k=1)
        scores = scores + causal[None, None]
        attn = jax.nn.softmax(scores, axis=-1)
        out = jnp.einsum('bhts,bhsd->bhtd', attn, v)
        out = out.transpose(0, 2, 1, 3).reshape(B, T, E)
        out = out @ Wo.T + bo
        return out

    def _L1_ffn_ref(x, Wm, bm, expert_emb, W1, b1, W2, b2, Wo, bo):
        import jax, jax.numpy as jnp
        import numpy as np
        BS, L, D = (4, 512, 256)
        H, E, K = (8, 16, 2)
        HD = D // H
        I = 1024 // H
        bs, L_, d = x.shape
        h = x @ Wm + bm
        t = h.reshape(bs * L_ * H, HD)
        logits = t @ expert_emb
        w = jax.nn.softmax(logits, axis=-1)
        topw, topi = jax.lax.top_k(w, K)
        hmid = jax.nn.gelu(jnp.einsum('td,edi->tei', t, W1) + b1, approximate=False)
        eo = jnp.einsum('tei,eio->teo', hmid, W2) + b2
        sel = jnp.take_along_axis(eo, topi[:, :, None], axis=1)
        comb = (sel * topw[:, :, None]).sum(axis=1)
        out = comb.reshape(bs, L_, d)
        return out @ Wo + bo
    x = x + _L0_xattn_ref(_layernorm(x, axis=-1), ctx_1024, ctx_1024, mask_Bx1xSxS2_bk1, L0_xattn_Wq, L0_xattn_bq, L0_xattn_Wk, L0_xattn_bk, L0_xattn_Wv, L0_xattn_bv, L0_xattn_Wo, L0_xattn_bo)
    x = x + _L0_ffn_ref(_layernorm(x, axis=-1), L0_ffn_Wr, L0_ffn_br, L0_ffn_W1, L0_ffn_b1, L0_ffn_W2, L0_ffn_b2)
    x = x + _L1_xattn_ref(_layernorm(x, axis=-1), ctx_1024, ctx_1024, L1_xattn_Wq, L1_xattn_bq, L1_xattn_Wk, L1_xattn_bk, L1_xattn_Wv, L1_xattn_bv, L1_xattn_Wo, L1_xattn_bo)
    x = x + _L1_ffn_ref(_layernorm(x, axis=-1), L1_ffn_Wm, L1_ffn_bm, L1_ffn_expert_emb, L1_ffn_W1, L1_ffn_b1, L1_ffn_W2, L1_ffn_b2, L1_ffn_Wo, L1_ffn_bo)
    return x

_drawn_inputs = setup_inputs


def setup_inputs(seed=0):
    import zlib

    import numpy as np

    out = dict(_drawn_inputs(seed))
    spreads = {'L0_xattn_bq': (0.0, 0.1),
     'L0_xattn_bk': (0.0, 2.0),
     'L0_xattn_bv': (0.0, 0.1),
     'L0_xattn_bo': (0.0, 0.1),
     'L0_ffn_br': (0.0, 0.355),
     'L0_ffn_b1': (0.0, 0.8),
     'L0_ffn_b2': (0.0, 0.34),
     'L1_ffn_bm': (0.0, 0.1),
     'L1_ffn_b1': (0.0, 0.1),
     'L1_ffn_b2': (0.0, 0.1),
     'L1_ffn_bo': (0.0, 0.1)}
    factors = {'L0_ffn_W1': 8.0, 'L0_ffn_W2': 6.67, 'L1_xattn_bq': 31.954, 'L1_xattn_bk': 64.0}
    for name, (base, spread) in spreads.items():
        noise = np.random.default_rng([zlib.crc32(name.encode()), seed]).standard_normal(out[name].shape)
        drawn = base * np.exp(spread * noise) if base else spread * noise
        out[name] = jnp.asarray(drawn.astype(out[name].dtype))
    for name, factor in factors.items():
        out[name] = (out[name] * factor).astype(out[name].dtype)
    return out
```

```python
import concourse.bass as bass
from concourse import mybir
from contextlib import ExitStack

FP32 = mybir.dt.float32
BF16 = mybir.dt.bfloat16
U8 = mybir.dt.uint8
I32 = mybir.dt.int32
U32 = mybir.dt.uint32
ALU = mybir.AluOpType
ACT = mybir.ActivationFunctionType
AXIS = mybir.AxisListType

P = 128
T = 2048
D = 256
DC = D // P
S = 1601
H = 16
DH = D // H
TB = 512
NB = T // TB
TT = TB // P
NT = T // P
KT = -(-S // P)
KLAST = S - P * (KT - 1)
SFULL = S // TB
STACK = 6 * DH
ROWS = STACK + 2
GROUPS = ((0, 3), (3, 2), (5, 1))
BIG = 2.0 ** 100
EPS = 1e-5
E1 = 8
CAP = T // E1
HM, E2, HD, F2 = 8, 16, 32, 128
MX = 3
U = 4
LEAD = 4
FAST_FROM = 9


def keys_of(kt):
    return KLAST if kt == KT - 1 else P


def hold(eng, sem, value, passed):
    eng.wait_ge(sem, value)
    eng.sem_inc(passed, 1)


class Chain:

    def __init__(self, eng, sem):
        self.eng, self.sem, self.base, self.n = eng, sem, 0, 0

    def at(self, base):
        self.base, self.n = base, 0

    def __call__(self, ins):
        self.n += 1
        ins.then_inc(self.sem, 1)
        self.eng.wait_ge(self.sem, self.base + self.n)


class Shared:

    def __init__(self):
        self.semaphores = []

    def semaphore(self, nc, name):
        self.semaphores.append(nc.alloc_semaphore(name))
        return self.semaphores[-1]

    def clear_semaphores(self, nc):
        nc.clear_and_free_semaphores(self.semaphores)
        nc.all_engine_barrier()
        self.semaphores = []


def place_shared(nc, ctx):
    m = Shared()

    def sb(name, shape, dt):
        return ctx.enter_context(nc.sbuf_tensor(name, shape, dt))

    m.ident = sb("ident", [P, P], FP32)
    m.ident_bf = sb("ident_bf", [P, P], BF16)
    m.neg_big = sb("neg_big", [P, P], BF16)
    m.late_key = sb("late_key", [P, P], BF16)
    m.late_key_q = sb("late_key_q", [P, P], BF16)
    m.upto = sb("upto", [P, P], FP32)
    m.ones = sb("ones", [P, P], FP32)
    m.minus_half = sb("minus_half", [P, TT], FP32)
    m.v = [sb(f"v{l}", [P, KT, D], FP32) for l in range(2)]
    m.slots = sb("slots", [P, NT], U32)
    m.gates = sb("gates", [P, NT], FP32)
    m.wq1 = sb("wq1", [P, DC, D], FP32)
    m.wo1 = sb("wo1", [P, DC, D], FP32)
    m.passed = nc.alloc_semaphore("passed")
    m.flag = sb("flag", [P, 1], I32)
    return m


def make_constants(nc, pool, m, made):
    link = Chain(pool, made)
    link(nc.gpsimd.memset(m.ones[:], 1.0))
    link(nc.gpsimd.memset(m.minus_half[:], -0.5))
    for buf, op, base, step, up, fill in (
        (m.ident, ALU.not_equal, 0, -1, 1, 1.0),
        (m.ident_bf, ALU.not_equal, 0, -1, 1, 1.0),
        (m.neg_big, ALU.not_equal, 0, -1, 1, -BIG),
        (m.late_key, ALU.is_ge, 0, 1, -1, 1.0),
        (m.late_key_q, ALU.is_ge, 0, -1, 1, 1.0),
        (m.upto, ALU.is_gt, 0, -1, 1, 1.0),
    ):
        link(nc.gpsimd.memset(buf[:], 0.0))
        link(nc.gpsimd.affine_select(out=buf[:], in_=buf[:], compare_op=op, fill=fill, base=base,
                                     pattern=[[step, P]], channel_multiplier=up))
    return link.n


def normalize(nc, m, dve, link, xb, xn, stats, mv, rstd, stats_ready, rstd_ready, at):
    for j in range(TT):
        ins = nc.vector.bn_stats(stats[:, j, :], xb[:, j, :])
        if j == TT - 1:
            link(ins)
            dve.sem_inc(m.passed, 1)
    for j in range(TT):
        ins = nc.vector.bn_aggr(mv[:, j, :], stats[:, j, :])
    ins.then_inc(stats_ready, 1)
    dve.wait_ge(rstd_ready, at + 1)
    for j in range(TT):
        ins = nc.vector.tensor_scalar(xn[:, j, :], xb[:, j, :], mv[:, j, 0:1], rstd[:, j:j + 1],
                                      ALU.subtract, ALU.mult)
    return ins


def root(nc, pool, m, mv, ve, rstd, stats_ready, ve_ready, rstd_ready, at):
    hold(pool, stats_ready, at + 1, m.passed)
    nc.gpsimd.tensor_scalar(ve[:], mv[:, :, 1], EPS, None, ALU.add).then_inc(ve_ready, 1)
    pool.wait_ge(ve_ready, at + 1)
    nc.gpsimd.tensor_tensor(rstd[:], ve[:], m.minus_half[:], ALU.pow).then_inc(rstd_ready, 1)


def prepare(nc, m, d, mask):
    with ExitStack() as ctx:
        def sb(name, shape, dt):
            return ctx.enter_context(nc.sbuf_tensor("a_" + name, shape, dt))

        def sem(name):
            return m.semaphore(nc, "a_" + name)

        w = {n: sb(n, [P, DC, D], FP32) for n in ("wq0", "wk0", "wv0", "wk1", "wv1")}
        wraw = sb("wraw", [P, DC, 4, D], FP32)
        brow = sb("brow", [1, 2, D], FP32)
        bcol = sb("bcol", [P, 3, DC], FP32)
        xb = sb("xb", [P, TT, D], FP32)
        xn = sb("xn", [P, TT, D], FP32)
        xT = sb("xT", [P, DC, TB], FP32)
        kf = sb("kf", [P, DC, TB], FP32)
        rest = sb("rest", [P, DC, TB], FP32)
        parts = sb("parts", [P, 3, DC, TB], BF16)
        stats = sb("stats", [P, TT, 6], FP32)
        mv = sb("mv", [P, TT, 2], FP32)
        ve = sb("ve", [P, TT], FP32)
        rstd = sb("rstd", [P, TT], FP32)
        mraw = sb("mraw", [P, 2, S], U8)
        mlow = sb("mlow", [P, 2, NT], FP32)
        bad = sb("bad", [P, 4], FP32)
        pT = [ctx.enter_context(nc.psum_tensor(f"a_pT{k}", [P, TB], FP32)) for k in range(DC)]
        pK = [ctx.enter_context(nc.psum_tensor(f"a_pK{k}", [P, TB], FP32)) for k in range(DC)]
        pV = [ctx.enter_context(nc.psum_tensor(f"a_pV{k}", [P, D], FP32)) for k in range(2)]
        pF = ctx.enter_context(nc.psum_tensor("a_pF", [P, 1], FP32))

        made, w_in, wT, wT_sb = sem("made"), sem("w_in"), sem("wT"), sem("wT_sb")
        x_in, x_free = sem("x_in"), sem("x_free")
        stats_ready, ve_ready, rstd_ready, xn_ready = sem("stats"), sem("ve"), sem("rstd"), sem("xn_ready")
        turned, xT_ready = sem("turned"), sem("xT_ready")
        proj, kf_ready, kf_free = sem("proj"), sem("kf_ready"), sem("kf_free")
        split_done, parts_out, parts_free = sem("split_done"), sem("parts_out"), sem("parts_free")
        v_done, v_copied = sem("v_done"), sem("v_copied")
        m_in, m_cast, m_low = [sem(f"m_in{b}") for b in range(2)], sem("m_cast"), sem("m_low")
        bad_ready, bad_sum, dve_own = sem("bad_ready"), sem("bad_sum"), sem("dve_own")
        CONSTS = 14
        x_pass = NB
        c_blocks = SFULL + 1

        block = ctx.enter_context(nc.Block())

        @block.sync
        def _(sp):
            view = "(k p) n -> p k n"
            n = 0
            for name, src in (("wq0", d["L0_xattn_Wq"]), ("wk0", d["L0_xattn_Wk"]), ("wv0", d["L0_xattn_Wv"])):
                sp.dma_start(w[name][:], src.rearrange(view, p=P)).then_inc(w_in, 16)
            for i, name in enumerate(("Wq", "Wk", "Wv", "Wo")):
                sp.dma_start(wraw[:, :, i, :], d["L1_xattn_" + name].rearrange(view, p=P)).then_inc(w_in, 16)
            for l in range(2):
                sp.dma_start(brow[0:1, l, :], d[f"L{l}_xattn_bv"].rearrange("(a n) -> a n", a=1)).then_inc(w_in, 16)
            with nc.allow_non_contiguous_dma(reason="a bias as a column"):
                for i, name in enumerate(("L0_xattn_bq", "L0_xattn_bk", "L1_xattn_bk")):
                    sp.dma_start(bcol[:, i, :], d[name].rearrange("(k p) -> p k", p=P)).then_inc(w_in, 16)
            sp.sem_inc(x_free, 1)
            x_rows = d["x"].rearrange("a t d -> (a t) d")
            with sp.Fori(0, NB) as i:
                sp.wait_ge(x_free, i + 1)
                sp.dma_start(xb[:], x_rows[bass.ds(i * TB, TB), :].rearrange("(j p) d -> p j d", p=P)
                             ).then_inc(x_in, 16)
            c_rows = d["ctx_1024"].rearrange("a t d -> (a t) d")
            with sp.Fori(0, SFULL) as i:
                sp.wait_ge(x_free, i + NB + 1)
                sp.dma_start(xb[:], c_rows[bass.ds(i * TB, TB), :].rearrange("(j p) d -> p j d", p=P)
                             ).then_inc(x_in, 16)
            sp.wait_ge(x_free, SFULL + NB + 1)
            sp.dma_start(xb[0:KLAST, 0, :], c_rows[SFULL * TB:S, :]).then_inc(x_in, 16)
            m_rows = d["mask"].rearrange("a b t s -> (a b t) s")
            sp.sem_inc(m_cast, 2)
            sp.sem_inc(m_low, 2)
            with sp.Fori(0, NT // 2) as i:
                for b in range(2):
                    t = 2 * i + b
                    sp.wait_ge(m_cast, t + 1)
                    sp.wait_ge(m_low, t + 1)
                    sp.dma_start(mraw[:, b, :], m_rows[bass.ds(t * P, P), :]).then_inc(m_in[b], 16)

        @block.gpsimd
        def _(pool):
            n = make_constants(nc, pool, m, made)
            assert n == CONSTS
            pool.sem_inc(parts_free, 1)

            def store(at, to, col, cols):
                hold(pool, split_done, at + 1, m.passed)
                pool.dma_start(to[:, col].rearrange("(q p) c -> p q c", p=P),
                               parts[:, :, :, 0:cols].rearrange("p g k c -> p (g k) c")
                               ).then_inc(parts_out, 16)
                hold(pool, parts_out, 16 * (at + 1), parts_free)

            with pool.Fori(0, NB) as i:
                root(nc, pool, m, mv, ve, rstd, stats_ready, ve_ready, rstd_ready, i)
                store(i, d["q_parts"][0], bass.ds(i * TB, TB), TB)
            with pool.Fori(0, SFULL) as i:
                for l in range(2):
                    store(i * 2 + NB + l, d["k_parts"][l], bass.ds(i * TB, TB), TB)
            for l in range(2):
                store(SFULL * 2 + NB + l, d["k_parts"][l], slice(SFULL * TB, S), KLAST)
            with pool.Fori(0, NT // 2) as i:
                for b in range(2):
                    pool.wait_ge(m_in[b], 16 * (i + 1))
                    nc.gpsimd.tensor_copy(mask[:, bass.ds((2 * i + b) * S, S)], mraw[:, b, :]).then_inc(m_cast, 1)

        @block.scalar
        def _(act):
            act.wait_ge(w_in, 16 * 12)

            def evac(at, bias, cols):
                act.wait_ge(proj, at + 1)
                act.wait_ge(kf_free, at + 1)
                for k in range(DC):
                    ins = nc.scalar.activation(kf[:, k, 0:cols], pK[k][:, 0:cols], ACT.Identity,
                                               bias=bcol[:, bias, k:k + 1])
                ins.then_inc(kf_ready, 1)

            for i in range(4):
                act.wait_ge(wT, i + 1)
                dst = (m.wq1, w["wk1"], w["wv1"], m.wo1)[i]
                nc.scalar.copy(dst[:, 0, :], pT[0][:, 0:D])
                nc.scalar.copy(dst[:, 1, :], pT[1][:, 0:D]).then_inc(wT_sb, 1)
            with act.Fori(0, NB) as i:
                evac(i, 0, TB)
            with act.Fori(0, SFULL) as i:
                for l in range(2):
                    evac(i * 2 + NB + l, 1 + l, TB)
            for l in range(2):
                evac(SFULL * 2 + NB + l, 1 + l, KLAST)

        @block.vector
        def _(dve):
            link = Chain(dve, dve_own)
            dve.sem_inc(kf_free, 1)
            dve.sem_inc(v_copied, 2)
            LN = 1

            def cut(at, cols):
                dve.wait_ge(kf_ready, at + 1)
                dve.wait_ge(parts_free, at + 1)
                link(nc.vector.tensor_copy(parts[:, 0, :, 0:cols], kf[:, :, 0:cols]))
                link(nc.vector.tensor_tensor(rest[:, :, 0:cols], kf[:, :, 0:cols], parts[:, 0, :, 0:cols],
                                             ALU.subtract))
                dve.sem_inc(kf_free, 1)
                link(nc.vector.tensor_copy(parts[:, 1, :, 0:cols], rest[:, :, 0:cols]))
                nc.vector.tensor_tensor(parts[:, 2, :, 0:cols], rest[:, :, 0:cols], parts[:, 1, :, 0:cols],
                                        ALU.subtract).then_inc(split_done, 1)

            def take_turned(at, cols, rows=P):
                dve.wait_ge(turned, at + 1)
                for k in range(DC):
                    ins = nc.vector.tensor_copy(xT[:, k, 0:cols], pT[k][:, 0:cols])
                ins.then_inc(xT_ready, 1)

            with dve.Fori(0, NB) as i:
                link.at(i * (LN + 3))
                dve.wait_ge(x_in, 16 * (i + 1))
                normalize(nc, m, dve, link, xb, xn, stats, mv, rstd, stats_ready, rstd_ready, i
                          ).then_inc(xn_ready, 1)
                dve.wait_ge(xn_ready, i + 1)
                dve.sem_inc(x_free, 1)
                take_turned(i, TB)
                cut(i, TB)
            with dve.Fori(0, SFULL) as i:
                link.at(i * 6 + NB * (LN + 3))
                take_turned(i + NB, TB)
                for l in range(2):
                    cut(i * 2 + NB + l, TB)
                    for j in range(TT):
                        n = i * (2 * TT) + (l * TT + j)
                        dve.wait_ge(v_done, n + 1)
                        nc.vector.tensor_copy(m.v[l][:, bass.ds(i * TT + j, 1), :].rearrange("p a d -> p (a d)"),
                                              pV[j % 2][:]).then_inc(v_copied, 1)
            link.at(SFULL * 6 + NB * (LN + 3))
            take_turned(SFULL + NB, KLAST)
            for l in range(2):
                cut(SFULL * 2 + NB + l, KLAST)
                dve.wait_ge(v_done, SFULL * 2 * TT + l + 1)
                nc.vector.tensor_copy(m.v[l][0:KLAST, KT - 1, :], pV[l][0:KLAST, :]).then_inc(v_copied, 1)
            with dve.Fori(0, NT // 2) as i:
                for b in range(2):
                    t = 2 * i + b
                    dve.wait_ge(m_in[b], 16 * (i + 1))
                    nc.vector.tensor_reduce(mlow[:, 0, bass.ds(t, 1)], mraw[:, b, 0:FAST_FROM * P], AXIS.X, ALU.min)
                    nc.vector.tensor_reduce(mlow[:, 1, bass.ds(t, 1)], mraw[:, b, FAST_FROM * P:S], AXIS.X, ALU.min
                                            ).then_inc(m_low, 1)
            dve.wait_ge(m_low, NT + 2)
            link.at((SFULL + 1) * 6 + NB * (LN + 3))
            link(nc.vector.tensor_reduce(bad[:, 0:1], mlow[:, 0, :], AXIS.X, ALU.min))
            link(nc.vector.tensor_reduce(bad[:, 1:2], mlow[:, 1, :], AXIS.X, ALU.max))
            nc.vector.tensor_tensor(bad[:, 2:3], bad[:, 0:1], bad[:, 1:2], ALU.subtract).then_inc(bad_ready, 1)
            dve.wait_ge(bad_sum, 1)
            nc.vector.tensor_scalar(m.flag[:], pF[:], float(P), None, ALU.is_equal).then_inc(bad_ready, 1)

        @block.tensor
        def _(pe):
            pe.wait_ge(made, CONSTS)
            pe.wait_ge(w_in, 16 * 12)
            for i in range(4):
                if i:
                    pe.wait_ge(wT_sb, i)
                for k in range(DC):
                    for j in range(DC):
                        last = nc.tensor.transpose(pT[k][:, j * P:j * P + P], wraw[:, j, i, k * P:k * P + P],
                                                   m.ident[:])
                last.then_inc(wT, 1)
            pe.wait_ge(wT_sb, 4)

            def turn(src, tiles, rows):
                for k in range(DC):
                    for j in range(tiles):
                        last = nc.tensor.transpose(pT[k][:, j * P:j * P + rows], src[0:rows, j, k * P:k * P + P],
                                                   m.ident[0:rows, 0:rows])
                return last

            def project(at, weight, cols):
                pe.wait_ge(kf_free, at + 1)
                for k in range(DC):
                    for c in range(DC):
                        last = nc.tensor.matmul(pK[k][:, 0:cols], weight[:, c, k * P:k * P + P], xT[:, c, 0:cols],
                                                start=c == 0, stop=c == DC - 1)
                last.then_inc(proj, 1)

            def value(n, l, j, rows, buf):
                pe.wait_ge(v_copied, n + 1)
                for c in range(DC):
                    nc.tensor.matmul(pV[buf][0:rows, :], xT[:, c, j * P:j * P + rows], w[f"wv{l}"][:, c, :],
                                     start=c == 0, stop=False)
                nc.tensor.matmul(pV[buf][0:rows, :], m.ones[0:1, 0:rows], brow[0:1, l, :],
                                 start=False, stop=True).then_inc(v_done, 1)

            with pe.Fori(0, NB) as i:
                pe.wait_ge(xn_ready, i + 1)
                turn(xn, TT, P).then_inc(turned, 1)
                pe.wait_ge(xT_ready, i + 1)
                project(i, w["wq0"], TB)
            with pe.Fori(0, SFULL) as i:
                pe.wait_ge(x_in, 16 * (i + NB + 1))
                turn(xb, TT, P).then_inc(turned, 1)
                pe.wait_ge(turned, i + NB + 1)
                pe.sem_inc(x_free, 1)
                pe.wait_ge(xT_ready, i + NB + 1)
                for l in range(2):
                    project(i * 2 + NB + l, w[f"wk{l}"], TB)
                    for j in range(TT):
                        value(i * (2 * TT) + (l * TT + j), l, j, P, j % 2)
            pe.wait_ge(x_in, 16 * (SFULL + NB + 1))
            turn(xb, 1, KLAST).then_inc(turned, 1)
            pe.wait_ge(xT_ready, SFULL + NB + 1)
            for l in range(2):
                project(SFULL * 2 + NB + l, w[f"wk{l}"], KLAST)
                value(SFULL * 2 * TT + l, l, 0, KLAST, l)
            pe.wait_ge(bad_ready, 1)
            nc.tensor.matmul(pF[:], m.ones[:], bad[:, 2:3], start=True, stop=True).then_inc(bad_sum, 1)



class Tail:

    LOADS = 5
    LINKS = 3

    def __init__(t, nc, ctx, m, d, layer, x_from, x_to):
        def sb(name, shape, dt):
            return ctx.enter_context(nc.sbuf_tensor(f"e{layer}_" + name, shape, dt))

        def sem(name):
            return m.semaphore(nc, f"e{layer}_" + name)

        t.nc, t.m, t.d, t.layer, t.x_from, t.x_to = nc, m, d, layer, x_from, x_to
        t.num = sb("num", [P, DC, TB], FP32)
        t.den = sb("den", [P, DC, TB], FP32)
        t.x = sb("x", [P, TT, D], FP32)
        t.y = sb("y", [P, TT, D], FP32)
        t.xn = sb("xn", [P, TT, D], FP32)
        t.xT = sb("xT", [P, DC, TB], FP32)
        t.stats, t.mv = sb("stats", [P, TT, 6], FP32), sb("mv", [P, TT, 2], FP32)
        t.ve, t.rstd = sb("ve", [P, TT], FP32), sb("rstd", [P, TT], FP32)
        t.wo = m.wo1 if layer else sb("wo", [P, DC, D], FP32)
        t.bo = sb("bo", [1, D], FP32)
        t.w_in, t.x_in, t.x_free = sem("w_in"), sem("x_in"), sem("x_free")
        t.divided, t.projected, t.added = sem("divided"), sem("projected"), sem("added")
        t.stats_ready, t.ve_ready, t.rstd_ready = sem("stats_ready"), sem("ve_ready"), sem("rstd_ready")
        t.xn_ready, t.turned, t.xT_ready = sem("xn_ready"), sem("turned"), sem("xT_ready")
        t.stored = sem("stored")

    def weights(t, sp):
        name = f"L{t.layer}_xattn_"
        if not t.layer:
            sp.dma_start(t.wo[:], t.d[name + "Wo"].rearrange("(k p) n -> p k n", p=P)).then_inc(t.w_in, 16)
        sp.dma_start(t.bo[:], t.d[name + "bo"].rearrange("(a n) -> a n", a=1)).then_inc(t.w_in, 16)
        sp.sem_inc(t.x_free, 1)
        sp.sem_inc(t.stored, 16)
        return 1 if t.layer else 2

    def load(t, sp, i):
        sp.wait_ge(t.x_free, i + 1)
        for c in range(DC):
            for u, to in enumerate((t.num, t.den)):
                src = t.d["sums"].rearrange("(h j u r) c -> j u h r c", h=H, j=NB, u=2)
                src = src[bass.ds(i, 1), u, c * (H // DC):(c + 1) * (H // DC)]
                sp.dma_start(to[:, c, :], src).then_inc(t.x_in, 16)
        sp.dma_start(t.x[:], t.x_from[bass.ds(i * TB, TB), :].rearrange("(j p) d -> p j d", p=P)).then_inc(t.x_in, 16)

    def store(t, sp, i):
        sp.wait_ge(t.added, i + 1)
        sp.dma_start(t.x_to[bass.ds(i * TB, TB), :].rearrange("(j p) d -> p j d", p=P), t.y[:]).then_inc(t.stored, 16)

    def vector(t, dve, link, i, po):
        nc = t.nc
        dve.wait_ge(t.x_in, (i + 1) * (16 * t.LOADS))
        link(nc.vector.reciprocal(t.den[:], t.den[:]))
        nc.vector.tensor_tensor(t.num[:], t.num[:], t.den[:], ALU.mult).then_inc(t.divided, 1)
        dve.wait_ge(t.projected, i + 1)
        dve.wait_ge(t.stored, 16 * (i + 1))
        link(nc.vector.tensor_tensor(t.y[:].rearrange("p j d -> p (j d)"), t.x[:].rearrange("p j d -> p (j d)"),
                                     po[:], ALU.add))
        dve.sem_inc(t.added, 1)
        dve.sem_inc(t.x_free, 1)
        normalize(nc, t.m, dve, link, t.y, t.xn, t.stats, t.mv, t.rstd, t.stats_ready, t.rstd_ready, i
                  ).then_inc(t.xn_ready, 1)

    def gpsimd(t, pool, i):
        root(t.nc, pool, t.m, t.mv, t.ve, t.rstd, t.stats_ready, t.ve_ready, t.rstd_ready, i)

    def scalar(t, act, i, pT):
        act.wait_ge(t.turned, i + 1)
        for k in range(DC):
            ins = t.nc.scalar.copy(t.xT[:, k, :], pT[k][:])
        ins.then_inc(t.xT_ready, 1)

    def tensor(t, pe, i, po, pT):
        nc = t.nc
        pe.wait_ge(t.divided, i + 1)
        for j in range(TT):
            to = po[:, j * D:(j + 1) * D]
            for c in range(DC):
                nc.tensor.matmul(to, t.num[:, c, j * P:(j + 1) * P], t.wo[:, c, :], start=c == 0, stop=False)
            last = nc.tensor.matmul(to, t.m.ones[0:1, :], t.bo[:], start=False, stop=True)
        last.then_inc(t.projected, 1)
        pe.wait_ge(t.xn_ready, i + 1)
        for k in range(DC):
            for j in range(TT):
                last = nc.tensor.transpose(pT[k][:, j * P:(j + 1) * P], t.xn[:, j, k * P:(k + 1) * P], t.m.ident[:])
        last.then_inc(t.turned, 1)
        pe.wait_ge(t.xT_ready, i + 1)


def router(nc, m, d):
    with ExitStack() as ctx:
        t = Tail(nc, ctx, m, d, 0, d["x_rows"], d["x1"])

        def sb(name, shape, dt):
            return ctx.enter_context(nc.sbuf_tensor("r_" + name, shape, dt))

        def sem(name):
            return m.semaphore(nc, "r_" + name)

        wr = sb("wr", [P, DC, E1], FP32)
        br = sb("br", [1, E1], FP32)
        rank = sb("rank", [P, TT, E1], FP32)
        first_slot = sb("first_slot", [P, TT, E1], FP32)
        zero = sb("zero", [P, T // P * D], FP32)
        l = sb("l", [P, TT, E1], FP32)
        ex = sb("ex", [P, TT, E1], FP32)
        prob = sb("prob", [P, TT, E1], FP32)
        key = sb("key", [P, TT, E1], FP32)
        pick = sb("pick", [P, TT, E1], FP32)
        seen = sb("seen", [P, E1], FP32)
        seen_now = sb("seen_now", [P, E1], FP32)
        col = sb("col", [P, 10, TT], FP32)
        slot = sb("slot", [P, TT], U32)
        xg = sb("xg", [P, TT, D], FP32)
        po = ctx.enter_context(nc.psum_tensor("r_po", [P, TT * D], FP32))
        pT = [ctx.enter_context(nc.psum_tensor(f"r_pT{k}", [P, TB], FP32)) for k in range(DC)]
        pl = ctx.enter_context(nc.psum_tensor("r_pl", [P, TT * E1], FP32))
        pp = ctx.enter_context(nc.psum_tensor("r_pp", [P, TT * E1], FP32))
        consts, own, zeroed = sem("consts"), sem("own"), sem("zeroed")
        logits, lowered, expd = sem("logits"), sem("lowered"), sem("expd")
        picked, counted, slotted = sem("picked"), sem("counted"), sem("slotted")
        scattered, rows_free = sem("scattered"), sem("rows_free")
        top, den, gate, best, pos, off, drop, keep, fs = range(9)
        CONSTS = 3 + 2 * E1
        block = ctx.enter_context(nc.Block())

        @block.sync
        def _(sp):
            assert t.weights(sp) == 2
            sp.dma_start(wr[:], d["L0_ffn_Wr"].rearrange("(k p) n -> p k n", p=P)).then_inc(t.w_in, 16)
            sp.dma_start(br[:], d["L0_ffn_br"].rearrange("(a n) -> a n", a=1)).then_inc(t.w_in, 16)
            sp.wait_ge(consts, CONSTS)
            sp.dma_start(d["slots_in"].rearrange("(p n) d -> p (n d)", p=P), zero[:]).then_inc(zeroed, 16)
            with sp.Fori(0, NB) as i:
                t.load(sp, i)
                t.store(sp, i)
            sp.wait_ge(t.stored, 16 * (NB + 1))
            sp.wait_ge(zeroed, 16)

        @block.gpsimd
        def _(pool):
            nc.gpsimd.memset(zero[:], 0.0).then_inc(consts, 1)
            nc.gpsimd.memset(seen[:], 0.0).then_inc(consts, 1)
            nc.gpsimd.memset(seen_now[:], 0.0).then_inc(consts, 1)
            for e in range(E1):
                nc.gpsimd.memset(rank[:, :, e], float(E1 - e)).then_inc(consts, 1)
                nc.gpsimd.memset(first_slot[:, :, e], float(CAP * e)).then_inc(consts, 1)
            pool.sem_inc(rows_free, 1)
            pool.wait_ge(zeroed, 16)
            with pool.Fori(0, NB) as i:
                t.gpsimd(pool, i)
                hold(pool, slotted, i + 1, m.passed)
                for j in range(TT):
                    nc.gpsimd.indirect_dma_start(
                        out=d["slots_in"], out_offset=bass.IndirectOffsetOnAxis(ap=slot[:, j:j + 1], axis=0),
                        in_=xg[:, j, :], in_offset=None, bounds_check=T - 1, oob_is_err=False,
                    ).then_inc(scattered, 16)
                hold(pool, scattered, (i + 1) * (16 * TT), rows_free)

        @block.scalar
        def _(act):
            with act.Fori(0, NB) as i:
                t.scalar(act, i, pT)
                act.wait_ge(lowered, i + 1)
                nc.scalar.activation(ex[:], l[:], ACT.Exp).then_inc(expd, 1)

        @block.vector
        def _(dve):
            link = Chain(dve, own)
            V = nc.vector
            LINKS = t.LINKS + 18

            def wide(c):
                return col[:, c, :].unsqueeze(2).to_broadcast([P, TT, E1])

            plv = pl[:].rearrange("p (j e) -> p j e", e=E1)
            ppv = pp[:].rearrange("p (j e) -> p j e", e=E1)
            dve.wait_ge(consts, CONSTS)
            with dve.Fori(0, NB) as i:
                link.at(i * LINKS)
                t.vector(dve, link, i, po)
                dve.wait_ge(logits, i + 1)
                link(V.tensor_reduce(col[:, top, :], plv, AXIS.X, ALU.max))
                V.tensor_tensor(l[:], plv, wide(top), ALU.subtract).then_inc(lowered, 1)
                dve.wait_ge(expd, i + 1)
                link(V.tensor_reduce(col[:, den, :], ex[:], AXIS.X, ALU.add))
                link(V.reciprocal(col[:, den, :], col[:, den, :]))
                link(V.tensor_tensor(prob[:], ex[:], wide(den), ALU.mult))
                link(V.tensor_reduce(col[:, gate, :], prob[:], AXIS.X, ALU.max))
                link(V.tensor_tensor(key[:], prob[:], wide(gate), ALU.is_equal))
                link(V.tensor_tensor(key[:], key[:], rank[:], ALU.mult))
                link(V.tensor_reduce(col[:, best, :], key[:], AXIS.X, ALU.max))
                V.tensor_tensor(pick[:], key[:], wide(best), ALU.is_equal).then_inc(picked, 1)
                dve.wait_ge(counted, i + 1)
                link(V.tensor_tensor(key[:], ppv, pick[:], ALU.mult))
                link(V.tensor_reduce(col[:, pos, :], key[:], AXIS.X, ALU.add))
                link(V.tensor_tensor(key[:], first_slot[:], pick[:], ALU.mult))
                link(V.tensor_reduce(col[:, off, :], key[:], AXIS.X, ALU.add))
                link(V.tensor_reduce(seen_now[:], pick[:].rearrange("p j e -> p e j"), AXIS.X, ALU.add))
                link(V.tensor_tensor(seen[:], seen[:], seen_now[:], ALU.add))
                link(V.tensor_scalar(col[:, drop, :], col[:, pos, :], float(CAP), float(4 * T), ALU.is_ge, ALU.mult))
                link(V.tensor_scalar(col[:, keep, :], col[:, pos, :], float(CAP), None, ALU.is_lt))
                link(V.tensor_tensor(col[:, fs, :], col[:, pos, :], col[:, off, :], ALU.add))
                dve.wait_ge(rows_free, i + 1)
                link(V.tensor_tensor(slot[:], col[:, fs, :], col[:, drop, :], ALU.add))
                V.tensor_copy(m.slots[:, bass.ds(i * TT, TT)], slot[:])
                V.tensor_tensor(m.gates[:, bass.ds(i * TT, TT)], col[:, gate, :], col[:, keep, :], ALU.mult)
                for j in range(TT):
                    ins = V.tensor_scalar(xg[:, j, :], t.xn[:, j, :], col[:, gate, j:j + 1], None, ALU.mult)
                ins.then_inc(slotted, 1)
            assert link.n == LINKS, link.n

        @block.tensor
        def _(pe):
            pe.wait_ge(t.w_in, 16 * 4)
            pe.wait_ge(consts, CONSTS)
            with pe.Fori(0, NB) as i:
                t.tensor(pe, i, po, pT)
                for j in range(TT):
                    to = pl[:, j * E1:(j + 1) * E1]
                    for c in range(DC):
                        nc.tensor.matmul(to, t.xT[:, c, j * P:(j + 1) * P], wr[:, c, :], start=c == 0, stop=False)
                    last = nc.tensor.matmul(to, m.ones[0:1, :], br[:], start=False, stop=True)
                last.then_inc(logits, 1)
                pe.wait_ge(picked, i + 1)
                for j in range(TT):
                    to = pp[:, j * E1:(j + 1) * E1]
                    nc.tensor.matmul(to, m.ones[:], seen[:], start=True, stop=False)
                    for a in range(j):
                        nc.tensor.matmul(to, m.ones[:], pick[:, a, :], start=False, stop=False)
                    last = nc.tensor.matmul(to, m.upto[:], pick[:, j, :], start=False, stop=True)
                last.then_inc(counted, 1)


def experts(nc, m, d):
    with ExitStack() as ctx:
        def sb(name, shape, dt):
            return ctx.enter_context(nc.sbuf_tensor("f_" + name, shape, dt))

        def sem(name):
            return m.semaphore(nc, "f_" + name)

        SC = CAP // P
        LOADS = 5
        w1, w2, b1, b2, xs, xsT, hT, eo, pT, ph, pe_ = [], [], [], [], [], [], [], [], [], [], []
        for b in range(2):
            w1.append(sb(f"w1{b}", [P, DC, D], FP32))
            w2.append(sb(f"w2{b}", [P, DC, D], FP32))
            b1.append(sb(f"b1{b}", [P, DC], FP32))
            b2.append(sb(f"b2{b}", [1, D], FP32))
            xs.append(sb(f"xs{b}", [P, SC, D], FP32))
            xsT.append(sb(f"xsT{b}", [P, DC, CAP], FP32))
            hT.append(sb(f"hT{b}", [P, DC, CAP], FP32))
            eo.append(sb(f"eo{b}", [P, SC, D], FP32))
            pT.append(ctx.enter_context(nc.psum_tensor(f"f_pT{b}", [P, DC * CAP], FP32)))
            ph.append(ctx.enter_context(nc.psum_tensor(f"f_ph{b}", [P, DC * CAP], FP32)))
            pe_.append(ctx.enter_context(nc.psum_tensor(f"f_pe{b}", [P, SC * D], FP32)))
        loaded = [sem(f"loaded{b}") for b in range(2)]
        stored = [sem(f"stored{b}") for b in range(2)]
        turned, xsT_ready, hidden, hT_ready, made, copied = (
            sem("turned"), sem("xsT_ready"), sem("hidden"), sem("hT_ready"), sem("made"), sem("copied"))
        eo_free = sem("eo_free")
        block = ctx.enter_context(nc.Block())

        def both(eng, body):
            with eng.Fori(0, E1 // 2) as p:
                for b in range(2):
                    body(p, b, p * 2 + b)

        @block.sync
        def _(sp):
            sp.sem_inc(made, 2)

            def body(p, b, e):
                hold(sp, made, e + 1, m.passed)
                for to, name in ((w1[b], "L0_ffn_W1"), (w2[b], "L0_ffn_W2")):
                    sp.dma_start(to[:], d[name].rearrange("e k n -> (e k) n")[bass.ds(e * D, D), :]
                                 .rearrange("(k p) n -> p k n", p=P)).then_inc(loaded[b], 16)
                with nc.allow_non_contiguous_dma(reason="a bias as a column"):
                    sp.dma_start(b1[b][:], d["L0_ffn_b1"].rearrange("e n -> (e n)")[bass.ds(e * D, D)]
                                 .rearrange("(k p) -> p k", p=P)).then_inc(loaded[b], 16)
                sp.dma_start(b2[b][:], d["L0_ffn_b2"][bass.ds(e, 1), :]).then_inc(loaded[b], 16)
                sp.dma_start(xs[b][:], d["slots_in"][bass.ds(e * CAP, CAP), :].rearrange("(k p) n -> p k n", p=P)
                             ).then_inc(loaded[b], 16)
            both(sp, body)

        @block.gpsimd
        def _(pool):
            def body(p, b, e):
                hold(pool, copied, e + 1, m.passed)
                pool.dma_start(d["slots_out"][bass.ds(e * CAP, CAP), :].rearrange("(k p) n -> p k n", p=P), eo[b][:]
                               ).then_inc(stored[b], 16)
                hold(pool, stored[b], 16 * (p + 1), eo_free)
            pool.sem_inc(eo_free, 2)
            both(pool, body)

        @block.scalar
        def _(act):
            def body(p, b, e):
                act.wait_ge(hidden, e + 1)
                for k in range(DC):
                    ins = nc.scalar.activation(hT[b][:, k, :], ph[b][:, k * CAP:(k + 1) * CAP], ACT.Relu,
                                               bias=b1[b][:, k:k + 1])
                ins.then_inc(hT_ready, 1)
            both(act, body)

        @block.vector
        def _(dve):
            def body(p, b, e):
                dve.wait_ge(turned, e + 1)
                nc.vector.tensor_copy(xsT[b][:].rearrange("p k c -> p (k c)"), pT[b][:]).then_inc(xsT_ready, 1)
                dve.wait_ge(made, e + 3)
                dve.wait_ge(eo_free, e + 1)
                nc.vector.tensor_copy(eo[b][:].rearrange("p k c -> p (k c)"), pe_[b][:]).then_inc(copied, 1)
            both(dve, body)

        @block.tensor
        def _(pe):
            def body(p, b, e):
                pe.wait_ge(loaded[b], (p + 1) * (16 * LOADS))
                for k in range(DC):
                    for j in range(SC):
                        last = nc.tensor.transpose(pT[b][:, k * CAP + j * P:k * CAP + (j + 1) * P],
                                                   xs[b][:, j, k * P:(k + 1) * P], m.ident[:])
                last.then_inc(turned, 1)
                pe.wait_ge(xsT_ready, e + 1)
                for k in range(DC):
                    for c in range(DC):
                        last = nc.tensor.matmul(ph[b][:, k * CAP:(k + 1) * CAP], w1[b][:, c, k * P:(k + 1) * P],
                                                xsT[b][:, c, :], start=c == 0, stop=c == DC - 1)
                last.then_inc(hidden, 1)
                pe.wait_ge(hT_ready, e + 1)
                for j in range(SC):
                    to = pe_[b][:, j * D:(j + 1) * D]
                    for c in range(DC):
                        nc.tensor.matmul(to, hT[b][:, c, j * P:(j + 1) * P], w2[b][:, c, :], start=c == 0, stop=False)
                    last = nc.tensor.matmul(to, m.ones[0:1, :], b2[b][:], start=False, stop=True)
                last.then_inc(made, 1)
            both(pe, body)


def gather(nc, m, d):
    with ExitStack() as ctx:
        def sb(name, shape, dt):
            return ctx.enter_context(nc.sbuf_tensor("g_" + name, shape, dt))

        def sem(name):
            return m.semaphore(nc, "g_" + name)

        x = sb("x", [P, TT, D], FP32)
        eo = sb("eo", [P, TT, D], FP32)
        y = sb("y", [P, TT, D], FP32)
        xn = sb("xn", [P, TT, D], FP32)
        xT = sb("xT", [P, DC, TB], FP32)
        kf = sb("kf", [P, DC, TB], FP32)
        rest = sb("rest", [P, DC, TB], FP32)
        parts = sb("parts", [P, 3, DC, TB], BF16)
        bq = sb("bq", [P, DC], FP32)
        slot = sb("slot", [P, TT], U32)
        gate = sb("gate", [P, TT], FP32)
        stats, mv = sb("stats", [P, TT, 6], FP32), sb("mv", [P, TT, 2], FP32)
        ve, rstd = sb("ve", [P, TT], FP32), sb("rstd", [P, TT], FP32)
        pT = [ctx.enter_context(nc.psum_tensor(f"g_pT{k}", [P, TB], FP32)) for k in range(DC)]
        pq = [ctx.enter_context(nc.psum_tensor(f"g_pq{k}", [P, TB], FP32)) for k in range(DC)]
        w_in, x_in, x_free, eo_in, cleared, own = (
            sem("w_in"), sem("x_in"), sem("x_free"), sem("eo_in"), sem("cleared"), sem("own"))
        added, x_out, stats_ready, ve_ready, rstd_ready = (
            sem("added"), sem("x_out"), sem("stats_ready"), sem("ve_ready"), sem("rstd_ready"))
        xn_ready, turned, xT_ready, proj, kf_ready, split_done, parts_out, slot_ready = (
            sem("xn_ready"), sem("turned"), sem("xT_ready"), sem("proj"), sem("kf_ready"), sem("split_done"),
            sem("parts_out"), sem("slot_ready"))
        block = ctx.enter_context(nc.Block())

        @block.sync
        def _(sp):
            with nc.allow_non_contiguous_dma(reason="a bias as a column"):
                sp.dma_start(bq[:], d["L1_xattn_bq"].rearrange("(k p) -> p k", p=P)).then_inc(w_in, 16)
            sp.sem_inc(x_free, 1)
            sp.sem_inc(x_out, 16)
            sp.sem_inc(parts_out, 16)
            with sp.Fori(0, NB) as i:
                hold(sp, x_free, i + 1, m.passed)
                sp.dma_start(x[:], d["x1"][bass.ds(i * TB, TB), :].rearrange("(j p) d -> p j d", p=P)).then_inc(x_in, 16)
                hold(sp, added, i + 1, m.passed)
                sp.dma_start(d["x2"][bass.ds(i * TB, TB), :].rearrange("(j p) d -> p j d", p=P), y[:]).then_inc(x_out, 16)
                hold(sp, split_done, i + 1, m.passed)
                sp.dma_start(d["q_parts"][1][:, bass.ds(i * TB, TB)].rearrange("(q p) c -> p q c", p=P),
                             parts[:].rearrange("p g k c -> p (g k) c")).then_inc(parts_out, 16)
            sp.wait_ge(x_out, 16 * (NB + 1))
            sp.wait_ge(parts_out, 16 * (NB + 1))

        @block.gpsimd
        def _(pool):
            with pool.Fori(0, NB) as i:
                hold(pool, slot_ready, i + 1, m.passed)
                nc.gpsimd.memset(eo[:], 0.0).then_inc(cleared, 1)
                hold(pool, cleared, i + 1, m.passed)
                for j in range(TT):
                    nc.gpsimd.indirect_dma_start(
                        out=eo[:, j, :], out_offset=None, in_=d["slots_out"],
                        in_offset=bass.IndirectOffsetOnAxis(ap=slot[:, j:j + 1], axis=0),
                        bounds_check=T - 1, oob_is_err=False).then_inc(eo_in, 16)
                root(nc, pool, m, mv, ve, rstd, stats_ready, ve_ready, rstd_ready, i)

        @block.scalar
        def _(act):
            act.wait_ge(w_in, 16)
            with act.Fori(0, NB) as i:
                act.wait_ge(turned, i + 1)
                for k in range(DC):
                    ins = nc.scalar.copy(xT[:, k, :], pT[k][:])
                ins.then_inc(xT_ready, 1)
                act.wait_ge(proj, i + 1)
                for k in range(DC):
                    ins = nc.scalar.activation(kf[:, k, :], pq[k][:], ACT.Identity, bias=bq[:, k:k + 1])
                ins.then_inc(kf_ready, 1)

        @block.vector
        def _(dve):
            link = Chain(dve, own)
            V = nc.vector
            LINKS = 6
            with dve.Fori(0, NB) as i:
                link.at(i * LINKS)
                V.tensor_copy(slot[:], m.slots[:, bass.ds(i * TT, TT)])
                link(V.tensor_copy(gate[:], m.gates[:, bass.ds(i * TT, TT)]))
                dve.sem_inc(slot_ready, 1)
                dve.wait_ge(x_in, 16 * (i + 1))
                dve.wait_ge(eo_in, (i + 1) * (16 * TT))
                dve.wait_ge(x_out, 16 * (i + 1))
                for j in range(TT):
                    ins = V.scalar_tensor_tensor(out=y[:, j, :], in0=eo[:, j, :], scalar=gate[:, j:j + 1], in1=x[:, j, :],
                                                 op0=ALU.mult, op1=ALU.add)
                link(ins)
                dve.sem_inc(added, 1)
                dve.sem_inc(x_free, 1)
                normalize(nc, m, dve, link, y, xn, stats, mv, rstd, stats_ready, rstd_ready, i).then_inc(xn_ready, 1)
                dve.wait_ge(kf_ready, i + 1)
                dve.wait_ge(parts_out, 16 * (i + 1))
                link(V.tensor_copy(parts[:, 0], kf[:]))
                link(V.tensor_tensor(rest[:], kf[:], parts[:, 0], ALU.subtract))
                link(V.tensor_copy(parts[:, 1], rest[:]))
                V.tensor_tensor(parts[:, 2], rest[:], parts[:, 1], ALU.subtract).then_inc(split_done, 1)
            assert link.n == LINKS, link.n

        @block.tensor
        def _(pe):
            with pe.Fori(0, NB) as i:
                pe.wait_ge(xn_ready, i + 1)
                for k in range(DC):
                    for j in range(TT):
                        last = nc.tensor.transpose(pT[k][:, j * P:(j + 1) * P], xn[:, j, k * P:(k + 1) * P], m.ident[:])
                last.then_inc(turned, 1)
                pe.wait_ge(xT_ready, i + 1)
                for k in range(DC):
                    for c in range(DC):
                        last = nc.tensor.matmul(pq[k][:], m.wq1[:, c, k * P:(k + 1) * P], xT[:, c, :],
                                                start=c == 0, stop=c == DC - 1)
                last.then_inc(proj, 1)


class Path:

    def __init__(self, name, kts, causal, pbufs):
        self.name, self.kts, self.causal, self.pbufs = name, kts, causal, pbufs
        self.c0 = kts[0] * P
        self.steps = [(kt, half, max(half * 2 * TB, kt * P if causal else 0)) for kt in kts for half in range(2)
                      if not causal or kt * P < (half + 1) * 2 * TB]
        self.pieces = []
        for i in range(NT):
            end = min(S, P * (i + 1)) if causal else S
            self.pieces += [(i, n, c, min(c + TB, end)) for n, c in enumerate(range(self.c0, end, TB))]
        self.ne = len(self.steps)
        self.nm = len(self.pieces) + 1
        assert (U * self.ne) % pbufs == 0 
        self.plan()

    def plan(self):
        cost = [(half + 1) * 2 * TB - q0 + 220 for _, half, q0 in self.steps]
        work = [end - c + 80 for _, _, c, end in self.pieces]
        done, at, share = 0, 0, []
        for n in range(self.nm):
            share.append(done / sum(work))
            done += work[n] if n < len(work) else 0
        self.slots = [[] for _ in range(self.ne)]
        shift = 1 - sum(cost[-LEAD:]) / sum(cost)
        edges = [sum(cost[:e + 1]) / sum(cost) for e in range(self.ne)]
        for k in (1, 2):
            for n in range(self.nm):
                when = shift - 1 + share[n] + (k - 1)
                if n == self.nm - 1:
                    when = shift - 1e-6 + (k - 1)
                if 0 <= when < 1:
                    self.slots[next(e for e in range(self.ne) if when < edges[e])].append((k, n))
        self.early = [n for slot in self.slots for k, n in slot if k == 2]


def wait(eng, sem, value):
    if not (isinstance(value, int) and value <= 0):
        eng.wait_ge(sem, value)


def attend(nc, m, d, layer, paths, mask=None):
    with ExitStack() as ctx:
        def sb(name, shape, dt):
            return ctx.enter_context(nc.sbuf_tensor(f"t{layer}_" + name, shape, dt))

        q = [sb(f"q{b}", [ROWS, T], BF16) for b in range(U)]
        k = [sb(f"k{b}", [ROWS, KT * P], BF16) for b in range(U)]
        vo = [sb(f"vo{b}", [P, KT, 2 * DH], FP32) for b in range(2)]
        prob = [sb(f"prob{b}", [P, 2 * TB], FP32) for b in range(max(x.pbufs for x in paths))]
        osb = [sb(f"osb{b}", [P, TB], FP32) for b in range(2)]
        part_max = sb("part_max", [P, NT, 4], FP32)
        neg_max = sb("neg_max", [P, NT], FP32)
        neg_rest = sb("neg_rest", [P, NT], FP32)
        neg_cols = sb("neg_cols", [P, 2 * NT], BF16)
        neg_rows = sb("neg_rows", [2 * NT, P], BF16)
        mask_t = sb("mask_t", [P, len(paths[-1].kts), T], BF16) if mask is not None else None
        scores = [ctx.enter_context(nc.psum_tensor(f"t{layer}_s{b}", [P, 2 * TB], FP32)) for b in range(2)]
        mx = [ctx.enter_context(nc.psum_tensor(f"t{layer}_m{b}", [P, TB], FP32)) for b in range(MX)]
        out = ctx.enter_context(nc.psum_tensor(f"t{layer}_o", [P, TB], FP32))
        READY = 2 + 1 + U
        NLOAD = 6

        class Sems:
            def __init__(s, name):
                def sem(n):
                    return m.semaphore(nc, f"t{layer}{name}_{n}")
                s.qk_in = [sem(f"qk_in{b}") for b in range(U)]
                s.neg_in = [sem(f"neg_in{b}") for b in range(U)]
                s.v_in = [sem(f"v_in{b}") for b in range(2)]
                s.scored = sem("scored")
                s.expd = sem("expd")
                s.used = sem("used")
                s.piece = sem("piece")
                s.taken = sem("taken")
                s.neg_cols = sem("neg_cols")
                s.neg_rows = sem("neg_rows")
                s.copied = sem("copied")
                s.stored = [sem(f"stored{b}") for b in range(2)]
                s.own = sem("own")
                s.mturned = sem("mturned")
                s.mcopied = sem("mcopied")
                s.ready = sem("ready")

        sems = [Sems(x.name) for x in paths]
        block = ctx.enter_context(nc.Block())

        def choose(eng, run):
            if len(paths) == 1:
                run(paths[0], sems[0])
                return
            fast = eng.value_load(m.flag[0:1, 0:1], min_val=0, max_val=1)
            with eng.If(fast >= 1):
                run(paths[0], sems[0])
                eng.nop()
            with eng.Else():
                run(paths[1], sems[1])
                eng.nop()
            eng.nop()

        def heads(eng, body):
            for b in range(U):
                body(0, b)
            with eng.Fori(1, H // U - 1) as p:
                for b in range(U):
                    body(p, b)
            for b in range(U):
                body(H // U - 1, b)

        def after(p, b, n):
            p, b = p + (b + n) // U, (b + n) % U
            if isinstance(p, int) and not 0 <= p < H // U:
                return None
            return p, b

        def turn(p, b):
            return p * (U // 2) + b // 2

        @block.sync
        def _(sp):
            def run(path, s):
                def load(p, b):
                    rows = bass.ds(p * (U * DH) + b * DH, DH)
                    for g, (at, n) in enumerate(GROUPS):
                        to = slice(at * DH, (at + n) * DH)
                        sp.dma_start(q[b][to, :], d["q_parts"][layer].rearrange("(g r) c -> g r c", g=3)[0:n, rows, :]
                                     ).then_inc(s.qk_in[b], 16)
                        sp.dma_start(k[b][to, path.c0:S],
                                     d["k_parts"][layer].rearrange("(g r) c -> g r c", g=3)[g:g + 1, rows, path.c0:S]
                                     .to_broadcast([n, DH, S - path.c0])).then_inc(s.qk_in[b], 16)

                def neg(p, b):
                    sp.wait_ge(s.neg_rows, p * U + b + 1)
                    for r in range(2):
                        sp.dma_start(q[b][STACK + r:STACK + r + 1, :].rearrange("a (i c) -> a i c", c=P),
                                     neg_rows[r * NT:(r + 1) * NT, :]).then_inc(s.neg_in[b], 16)

                def store(p, b):
                    sp.wait_ge(s.copied, p * U + b + 1)
                    sp.dma_start(d["sums"][bass.ds(p * (U * P) + b * P, P), :], osb[b % 2][:]
                                 ).then_inc(s.stored[b % 2], 16)

                for b in range(2):
                    sp.sem_inc(s.stored[b], 16)
                for b in range(3):
                    load(0, b)
                neg(0, 0)

                def body(p, b):
                    if after(p, b, 3):
                        wait(sp, s.scored, (p * U + b) * path.ne)
                        load(*after(p, b, 3))
                    if after(p, b, -1):
                        store(*after(p, b, -1))
                    if after(p, b, 1):
                        neg(*after(p, b, 1))

                heads(sp, body)
                store(H // U - 1, U - 1)
                for b in range(2):
                    sp.wait_ge(s.stored[b], 16 * (H // 2 + 1))
            choose(sp, run)

        @block.gpsimd
        def _(pool):
            def run(path, s):
                for b in range(2):
                    nc.gpsimd.memset(vo[b][:, :, DH:2 * DH], 1.0).then_inc(s.ready, 1)
                pool.wait_ge(s.ready, READY)

                def body(p, b):
                    wait(pool, s.used, (p * U + b - 1) * path.ne)
                    at = bass.ds(p * (U * DH) + b * DH, DH)
                    full = [kt for kt in path.kts if kt < KT - 1]
                    nc.gpsimd.tensor_copy(vo[b % 2][:, full[0]:full[-1] + 1, 0:DH],
                                          m.v[layer][:, full[0]:full[-1] + 1, at]).then_inc(s.v_in[b % 2], 1)
                    nc.gpsimd.tensor_copy(vo[b % 2][0:KLAST, KT - 1, 0:DH],
                                          m.v[layer][0:KLAST, KT - 1, at]).then_inc(s.v_in[b % 2], 1)
                heads(pool, body)
            choose(pool, run)

        @block.scalar
        def _(act):
            def run(path, s):
                def body(p, b):
                    base = p * (U * path.ne) + b * path.ne
                    for e, (kt, half, q0) in enumerate(path.steps):
                        n = b * path.ne + e
                        act.wait_ge(s.scored, base + e + 1)
                        wait(act, s.used, base + e + 1 - path.pbufs)
                        c = q0 - half * 2 * TB
                        rows = keys_of(kt)
                        nc.scalar.activation(prob[n % path.pbufs][0:rows, c:], scores[n % 2][0:rows, c:],
                                             ACT.Exp, scale=DH ** -0.5).then_inc(s.expd, 1)
                heads(act, body)
            choose(act, run)

        @block.vector
        def _(dve):
            def run(path, s):
                link = Chain(dve, s.own)
                nc.vector.memset(part_max[:], -3.0e38).then_inc(s.ready, 1)
                for b in range(U):
                    nc.vector.memset(k[b][STACK:ROWS, :], 1.0).then_inc(s.ready, 1)
                dve.wait_ge(s.ready, READY)
                if mask is not None:
                    for i, kt in enumerate(path.kts):
                        dve.wait_ge(s.mturned, i + 1)
                        rows = keys_of(kt)
                        nc.vector.tensor_copy(mask_t[0:rows, i, :], scores[i % 2][:].bitcast(BF16)[0:rows, :]
                                              ).then_inc(s.mcopied, 1)
                LINKS = 3

                def piece(p, b, n):
                    base = p * (U * path.nm) + b * path.nm
                    ps = mx[n % MX]
                    if n < path.nm - 1:
                        i, part, c, end = path.pieces[n]
                        dve.wait_ge(s.piece, base + n + 1)
                        nc.vector.tensor_reduce(part_max[:, i, part:part + 1], ps[:, 0:end - c], AXIS.X, ALU.max
                                                ).then_inc(s.taken, 1)
                        return
                    link.at((p * U + b) * LINKS)
                    dve.wait_ge(s.taken, base + n)
                    link(nc.vector.tensor_reduce(neg_max[:], part_max[:], AXIS.X, ALU.max, negate=True))
                    link(nc.vector.tensor_copy(neg_cols[:, 0:NT], neg_max[:]))
                    link(nc.vector.tensor_tensor(neg_rest[:], neg_max[:], neg_cols[:, 0:NT], ALU.subtract))
                    nc.vector.tensor_copy(neg_cols[:, NT:2 * NT], neg_rest[:]).then_inc(s.neg_cols, 1)
                    dve.wait_ge(s.piece, base + path.nm)
                    before = after(p, b, -1)
                    if before:
                        dve.wait_ge(s.neg_in[before[1]], 32 * (before[0] + 1))
                    nc.vector.tensor_copy(neg_rows[:], ps[:].bitcast(BF16)[0:2 * NT, 0:P]).then_inc(s.taken, 1)
                    dve.wait_ge(s.taken, base + path.nm)
                    dve.sem_inc(s.neg_rows, 1)

                def copy_sums(p, b):
                    dve.wait_ge(s.used, (p * U + b + 1) * path.ne)
                    dve.wait_ge(s.stored[b % 2], 16 * (turn(p, b) + 1))
                    nc.vector.tensor_copy(osb[b % 2][:], out[:]).then_inc(s.copied, 1)

                for n in range(path.nm):
                    piece(0, 0, n)
                for n in path.early:
                    piece(0, 1, n)

                def body(p, b):
                    for e, slot in enumerate(path.slots):
                        for k_, n in slot:
                            if after(p, b, k_):
                                piece(*after(p, b, k_), n)
                        if e == 1 and after(p, b, -1):
                            copy_sums(*after(p, b, -1))
                heads(dve, body)
                copy_sums(H // U - 1, U - 1)
            choose(dve, run)

        @block.tensor
        def _(pe):
            def run(path, s):
                pe.wait_ge(s.ready, READY)
                if mask is not None:
                    for i, kt in enumerate(path.kts):
                        rows = keys_of(kt)
                        wait(pe, s.mcopied, i - 1)
                        for t in range(NT):
                            last = nc.tensor.transpose(scores[i % 2][:].bitcast(BF16)[0:rows, t * P:(t + 1) * P],
                                                       mask[:, t * S + kt * P:t * S + kt * P + rows], m.ident_bf[:])
                        last.then_inc(s.mturned, 1)
                    pe.wait_ge(s.mcopied, len(path.kts))

                def score(p, b, e):
                    kt, half, q0 = path.steps[e]
                    n = b * path.ne + e
                    base = p * (U * path.ne) + n
                    if e == 0:
                        pe.wait_ge(s.neg_in[b], 32 * (p + 1))
                    wait(pe, s.expd, base - 1)
                    rows = keys_of(kt)
                    c = q0
                    while c < (half + 1) * 2 * TB:
                        end = (c // TB + 1) * TB
                        at = c - half * 2 * TB
                        diag = path.causal and c == kt * P
                        ps = scores[n % 2]
                        last = nc.tensor.matmul(ps[0:rows, at:at + end - c], k[b][:, kt * P:kt * P + rows],
                                                q[b][:, c:end], start=True, stop=mask is None and not diag)
                        if mask is not None:
                            last = nc.tensor.matmul(ps[0:rows, at:at + end - c], m.neg_big[0:rows, 0:rows],
                                                    mask_t[0:rows, path.kts.index(kt), c:end], start=False, stop=True)
                        if diag:
                            last = nc.tensor.matmul(ps[0:rows, at:at + P], m.neg_big[0:rows, 0:rows],
                                                    m.late_key[0:rows, :], start=False, stop=True)
                        c = end
                    last.then_inc(s.scored, 1)

                def weigh(p, b, e):
                    kt, half, q0 = path.steps[e]
                    n = b * path.ne + e
                    pe.wait_ge(s.expd, p * (U * path.ne) + n + 1)
                    if e == 0:
                        pe.wait_ge(s.v_in[b % 2], 2 * (turn(p, b) + 1))
                        wait(pe, s.copied, p * U + b)
                    rows = keys_of(kt)
                    for j in (2 * half, 2 * half + 1):
                        c = max(q0, j * TB)
                        if c >= (j + 1) * TB:
                            continue
                        at = c - half * 2 * TB
                        final = kt == path.kts[-1] or (path.causal and kt == 4 * j + 3)
                        last = nc.tensor.matmul(out[32 * j:32 * j + 32, c - j * TB:TB], vo[b % 2][0:rows, kt, :],
                                                prob[n % path.pbufs][0:rows, at:at + (j + 1) * TB - c],
                                                start=kt == path.kts[0], stop=final)
                    last.then_inc(s.used, 1)

                def piece(p, b, n):
                    base = p * (U * path.nm) + b * path.nm
                    if n == 0:
                        pe.wait_ge(s.qk_in[b], (16 * NLOAD) * (p + 1))
                    prior = n - MX if n >= MX else (path.nm - 1 - n) // MX * MX + n - path.nm
                    wait(pe, s.taken, base + prior + 1)
                    ps = mx[n % MX]
                    if n == path.nm - 1:
                        pe.wait_ge(s.neg_cols, p * U + b + 1)
                        nc.tensor.transpose(ps[:].bitcast(BF16)[0:2 * NT, 0:P], neg_cols[:], m.ident_bf[:]
                                            ).then_inc(s.piece, 1)
                        return
                    i, _, c, end = path.pieces[n]
                    diag = path.causal and i < KT and end == min(S, P * (i + 1))
                    last = nc.tensor.matmul(ps[:, 0:end - c], q[b][0:STACK, i * P:(i + 1) * P], k[b][0:STACK, c:end],
                                            start=True, stop=mask is None and not diag)
                    if mask is not None:
                        last = nc.tensor.matmul(ps[:, 0:end - c], m.neg_big[:], mask[:, i * S + c:i * S + end],
                                                start=False, stop=True)
                    if diag:
                        last = nc.tensor.matmul(ps[:, i * P - c:end - c], m.neg_big[:], m.late_key_q[:, 0:end - i * P],
                                                start=False, stop=True)
                    last.then_inc(s.piece, 1)

                for n in range(path.nm):
                    piece(0, 0, n)
                for n in path.early:
                    piece(0, 1, n)

                def body(p, b):
                    for e in range(path.ne):
                        score(p, b, e)
                        if e >= 2:
                            weigh(p, b, e - 2)
                        elif after(p, b, -1):
                            weigh(*after(p, b, -1), path.ne - 2 + e)
                        for k_, n in path.slots[e]:
                            if after(p, b, k_):
                                piece(*after(p, b, k_), n)
                heads(pe, body)
                for e in (path.ne - 2, path.ne - 1):
                    weigh(H // U - 1, U - 1, e)
            choose(pe, run)


def weights_of_experts(nc, m, d):
    with ExitStack() as ctx:
        t = Tail(nc, ctx, m, d, 1, d["x2"], d["x3"])

        def sb(name, shape, dt):
            return ctx.enter_context(nc.sbuf_tensor("w_" + name, shape, dt))

        def sem(name):
            return m.semaphore(nc, "w_" + name)

        G = TT * HM
        HC = HM // DC
        wm = sb("wm", [P, DC, D], FP32)
        bm = sb("bm", [P, DC], FP32)
        emb = sb("emb", [P, HC * E2], FP32)
        rank = sb("rank", [P, G, E2], FP32)
        h = sb("h", [P, DC, TB], FP32)
        rest = sb("rest", [P, DC, TB], FP32)
        parts = sb("parts", [P, 3, DC, TB], BF16)
        l, ex, w, key, first, second_, low = (sb(n, [P, G, E2], FP32) for n in
                                              ("l", "ex", "w", "key", "first", "second", "low"))
        col = sb("col", [P, 6, G], FP32)
        wT = sb("wT", [P, TB], FP32)
        po = ctx.enter_context(nc.psum_tensor("w_po", [P, TT * D], FP32))
        pT = [ctx.enter_context(nc.psum_tensor(f"w_pT{k}", [P, TB], FP32)) for k in range(DC)]
        ph = [ctx.enter_context(nc.psum_tensor(f"w_ph{k}", [P, TB], FP32)) for k in range(DC)]
        pg = ctx.enter_context(nc.psum_tensor("w_pg", [P, G * E2], FP32))
        pw = ctx.enter_context(nc.psum_tensor("w_pw", [P, TB], FP32))
        consts, own, hid, h_ready, split_done, parts_out = (
            sem("consts"), sem("own"), sem("hid"), sem("h_ready"), sem("split_done"), sem("parts_out"))
        logits, lowered, expd, weighed, w_turned, wT_ready, wT_out = (
            sem("logits"), sem("lowered"), sem("expd"), sem("weighed"), sem("w_turned"), sem("wT_ready"), sem("wT_out"))
        top, den, best, best2, top2 = range(5)
        CONSTS = 1 + E2
        WEIGHTS = 1 + 2 + HC
        block = ctx.enter_context(nc.Block())

        @block.sync
        def _(sp):
            assert t.weights(sp) == 1
            sp.dma_start(wm[:], d["L1_ffn_Wm"].rearrange("(k p) n -> p k n", p=P)).then_inc(t.w_in, 16)
            with nc.allow_non_contiguous_dma(reason="a bias as a column"):
                sp.dma_start(bm[:], d["L1_ffn_bm"].rearrange("(k p) -> p k", p=P)).then_inc(t.w_in, 16)
            sp.wait_ge(consts, CONSTS)
            for a in range(HC):
                sp.dma_start(emb[a * HD:(a + 1) * HD, a * E2:(a + 1) * E2], d["L1_ffn_expert_emb"]).then_inc(t.w_in, 16)
            sp.sem_inc(parts_out, 16)
            sp.sem_inc(wT_out, 16)
            with sp.Fori(0, NB) as i:
                t.load(sp, i)
                t.store(sp, i)
                hold(sp, split_done, i + 1, m.passed)
                sp.dma_start(d["t_parts"][:, bass.ds(i * TB, TB)].rearrange("(q p) c -> p q c", p=P),
                             parts[:].rearrange("p g k c -> p (g k) c")).then_inc(parts_out, 16)
                hold(sp, wT_ready, i + 1, m.passed)
                sp.dma_start(d["w_t"][bass.ds(i * P, P), :], wT[:]).then_inc(wT_out, 16)
            sp.wait_ge(t.stored, 16 * (NB + 1))
            sp.wait_ge(parts_out, 16 * (NB + 1))
            sp.wait_ge(wT_out, 16 * (NB + 1))

        @block.gpsimd
        def _(pool):
            nc.gpsimd.memset(emb[:], 0.0).then_inc(consts, 1)
            for e in range(E2):
                nc.gpsimd.memset(rank[:, :, e], float(E2 - e)).then_inc(consts, 1)
            with pool.Fori(0, NB) as i:
                t.gpsimd(pool, i)

        @block.scalar
        def _(act):
            act.wait_ge(t.w_in, 16 * WEIGHTS)
            with act.Fori(0, NB) as i:
                t.scalar(act, i, pT)
                act.wait_ge(hid, i + 1)
                for k in range(DC):
                    ins = nc.scalar.activation(h[:, k, :], ph[k][:], ACT.Identity, bias=bm[:, k:k + 1])
                ins.then_inc(h_ready, 1)
                act.wait_ge(lowered, i + 1)
                nc.scalar.activation(ex[:], l[:], ACT.Exp).then_inc(expd, 1)
                act.wait_ge(w_turned, i + 1)
                act.wait_ge(wT_out, 16 * (i + 1))
                nc.scalar.copy(wT[:], pw[:]).then_inc(wT_ready, 1)

        @block.vector
        def _(dve):
            link = Chain(dve, own)
            V = nc.vector
            LINKS = t.LINKS + 19
            pgv = pg[:].rearrange("p (g e) -> p g e", e=E2)

            def wide(c):
                return col[:, c, :].unsqueeze(2).to_broadcast([P, G, E2])

            def greatest(values, at, top_at, pick):
                link(V.tensor_reduce(col[:, top_at, :], values[:], AXIS.X, ALU.max))
                link(V.tensor_tensor(key[:], values[:], wide(top_at), ALU.is_equal))
                link(V.tensor_tensor(key[:], key[:], rank[:], ALU.mult))
                link(V.tensor_reduce(col[:, at, :], key[:], AXIS.X, ALU.max))
                link(V.tensor_tensor(pick[:], key[:], wide(at), ALU.is_equal))

            dve.wait_ge(consts, CONSTS)
            with dve.Fori(0, NB) as i:
                link.at(i * LINKS)
                t.vector(dve, link, i, po)
                dve.wait_ge(h_ready, i + 1)
                dve.wait_ge(parts_out, 16 * (i + 1))
                link(V.tensor_copy(parts[:, 0], h[:]))
                link(V.tensor_tensor(rest[:], h[:], parts[:, 0], ALU.subtract))
                link(V.tensor_copy(parts[:, 1], rest[:]))
                V.tensor_tensor(parts[:, 2], rest[:], parts[:, 1], ALU.subtract).then_inc(split_done, 1)
                dve.wait_ge(logits, i + 1)
                link(V.tensor_reduce(col[:, top, :], pgv, AXIS.X, ALU.max))
                V.tensor_tensor(l[:], pgv, wide(top), ALU.subtract).then_inc(lowered, 1)
                dve.wait_ge(expd, i + 1)
                link(V.tensor_reduce(col[:, den, :], ex[:], AXIS.X, ALU.add))
                link(V.reciprocal(col[:, den, :], col[:, den, :]))
                link(V.tensor_tensor(w[:], ex[:], wide(den), ALU.mult))
                greatest(w, best, top, first)
                link(V.scalar_tensor_tensor(out=low[:], in0=first[:], scalar=-2.0, in1=w[:], op0=ALU.mult, op1=ALU.add))
                greatest(low, best2, top2, second_)
                link(V.tensor_tensor(first[:], first[:], second_[:], ALU.add))
                V.tensor_tensor(w[:], w[:], first[:], ALU.mult).then_inc(weighed, 1)
                dve.wait_ge(w_turned, i + 1)
            assert link.n == LINKS, link.n

        @block.tensor
        def _(pe):
            pe.wait_ge(t.w_in, 16 * WEIGHTS)
            with pe.Fori(0, NB) as i:
                t.tensor(pe, i, po, pT)
                for k in range(DC):
                    for c in range(DC):
                        last = nc.tensor.matmul(ph[k][:], wm[:, c, k * P:(k + 1) * P], t.xT[:, c, :],
                                                start=c == 0, stop=c == DC - 1)
                last.then_inc(hid, 1)
                pe.wait_ge(h_ready, i + 1)
                for j in range(TT):
                    for c in range(DC):
                        at = (j * HM + c * HC) * E2
                        last = nc.tensor.matmul(pg[:, at:at + HC * E2], h[:, c, j * P:(j + 1) * P], emb[:],
                                                start=True, stop=True)
                last.then_inc(logits, 1)
                pe.wait_ge(weighed, i + 1)
                for j in range(TT):
                    last = nc.tensor.transpose(pw[:, j * P:(j + 1) * P],
                                               w[:, j * HM:(j + 1) * HM, :].rearrange("p h e -> p (h e)"), m.ident[:])
                last.then_inc(w_turned, 1)


def head_experts(nc, m, d):
    with ExitStack() as ctx:
        def sb(name, shape, dt):
            return ctx.enter_context(nc.sbuf_tensor("x_" + name, shape, dt))

        def sem(name):
            return m.semaphore(nc, "x_" + name)

        HC = HM // DC
        K3 = 3 * HD
        HB = 4
        w1f = sb("w1f", [K3, E2, F2], FP32)
        w1r = sb("w1r", [K3, E2, F2], FP32)
        w1m = sb("w1m", [K3, E2, F2], BF16)
        w1 = [sb(f"w1{n}", [K3, E2, F2], BF16) for n in range(2)]
        b1 = sb("b1", [F2, E2], FP32)
        w2 = sb("w2", [F2, E2, HD], FP32)
        b2 = sb("b2", [P, E2], FP32)
        wo = sb("wo", [P, DC, D], FP32)
        bo = sb("bo", [1, D], FP32)
        xt = [[sb(f"xt{c}{n}", [K3, HC, TB], BF16) for n in range(2)] for c in range(DC)]
        wb = [sb(f"wb{c}", [P, E2, TB], FP32) for c in range(DC)]
        hm = [sb(f"hm{n}", [F2, 2 * TB], FP32) for n in range(HB)]
        weighed_ = [sb(f"we{n}", [P, TB], FP32) for n in range(2)]
        acc = [sb(f"acc{c}", [P, TB], FP32) for c in range(DC)]
        x = sb("x", [P, TT, D], FP32)
        y = sb("y", [P, TT, D], FP32)
        pu = [ctx.enter_context(nc.psum_tensor(f"x_pu{n}", [F2, 2 * TB], FP32)) for n in range(2)]
        pe_ = [ctx.enter_context(nc.psum_tensor(f"x_pe{n}", [P, TB], FP32)) for n in range(2)]
        po = ctx.enter_context(nc.psum_tensor("x_po", [P, TT * D], FP32))
        w_in, w1_ready, own = sem("w_in"), sem("w1_ready"), sem("own")
        t_in = [sem(f"t_in{c}") for c in range(DC)]
        up, active, down, taken, summed = sem("up"), sem("active"), sem("down"), sem("taken"), sem("summed")
        projected, x_in, x_free, added, out_done = (
            sem("projected"), sem("x_in"), sem("x_free"), sem("added"), sem("out_done"))
        LOADS = 6 + HC
        N = E2 * 2
        WEIGHTS = 3 + 1 + 1 + HC + 2
        block = ctx.enter_context(nc.Block())

        def blocks(eng, body):
            body(0, True)
            with eng.Fori(1, NB) as i:
                body(i, False)

        @block.sync
        def _(sp):
            for n in range(3):
                sp.dma_start(w1f[n * HD:(n + 1) * HD, :, :], d["L1_ffn_W1"].rearrange("e k f -> k e f")).then_inc(w_in, 16)
            with nc.allow_non_contiguous_dma(reason="biases as columns"):
                sp.dma_start(b1[:], d["L1_ffn_b1"].rearrange("e f -> f e")).then_inc(w_in, 16)
                for a in range(HC):
                    sp.dma_start(b2[a * HD:(a + 1) * HD, :], d["L1_ffn_b2"].rearrange("e f -> f e")).then_inc(w_in, 16)
            sp.dma_start(w2[:], d["L1_ffn_W2"].rearrange("e f o -> f e o")).then_inc(w_in, 16)
            sp.dma_start(wo[:], d["L1_ffn_Wo"].rearrange("(k p) n -> p k n", p=P)).then_inc(w_in, 16)
            sp.dma_start(bo[:], d["L1_ffn_bo"].rearrange("(a n) -> a n", a=1)).then_inc(w_in, 16)
            sp.sem_inc(x_free, 1)
            sp.sem_inc(out_done, 16)

            def body(i, first):
                for c in range(DC):
                    if not first:
                        hold(sp, summed, (i - 1) * DC + c + 1, m.passed)
                    for n, parts in enumerate(((0, 1, 2), (0, 1, 0))):
                        for r, g in enumerate(parts):
                            src = d["t_parts"][g * D + c * P:g * D + (c + 1) * P, bass.ds(i * TB, TB)]
                            sp.dma_start(xt[c][n][r * HD:(r + 1) * HD, :, :], src.rearrange("(a r) c -> r a c", a=HC)
                                         ).then_inc(t_in[c], 16)
                    for a in range(HC):
                        rows = bass.ds(i * P + (c * HC + a) * E2, E2)
                        src = d["w_t"][rows, :].rearrange("(o e) c -> o (e c)", o=1).to_broadcast([HD, E2 * TB])
                        sp.dma_start(wb[c][a * HD:(a + 1) * HD, :, :].rearrange("p e c -> p (e c)"), src
                                     ).then_inc(t_in[c], 16)
                hold(sp, x_free, i + 1, m.passed)
                sp.dma_start(x[:], d["x3"][bass.ds(i * TB, TB), :].rearrange("(j p) d -> p j d", p=P)).then_inc(x_in, 16)
                if not first:
                    store(i - 1)

            def store(i):
                hold(sp, added, i + 1, m.passed)
                sp.dma_start(d["out_rows"][bass.ds(i * TB, TB), :].rearrange("(j p) d -> p j d", p=P), y[:]
                             ).then_inc(out_done, 16)
            blocks(sp, body)
            store(NB - 1)
            sp.wait_ge(out_done, 16 * (NB + 1))

        @block.gpsimd
        def _(pool):
            pool.nop()

        @block.scalar
        def _(act):
            act.wait_ge(w_in, 16 * WEIGHTS)

            def body(i, first):
                for c in range(DC):
                    for n in range(N):
                        base = i * (DC * N) + (c * N + n)
                        act.wait_ge(up, base + 1)
                        if not (first and c * N + n < HB):
                            act.wait_ge(down, base + 1 - HB)
                        nc.scalar.activation(hm[n % HB][:], pu[n % 2][:], ACT.Gelu, bias=b1[:, n // 2:n // 2 + 1]
                                             ).then_inc(active, 1)
            blocks(act, body)

        @block.vector
        def _(dve):
            link = Chain(dve, own)
            V = nc.vector
            dve.wait_ge(w_in, 16 * WEIGHTS)
            link(V.tensor_copy(w1[0][:], w1f[:]))
            link(V.tensor_tensor(w1r[:], w1f[:], w1[0][:], ALU.subtract))
            link(V.tensor_copy(w1m[:], w1r[:]))
            V.tensor_copy(w1[1][0:2 * HD], w1m[0:2 * HD]).then_inc(w1_ready, 1)
            V.tensor_tensor(w1[1][2 * HD:K3], w1r[2 * HD:K3], w1m[2 * HD:K3], ALU.subtract).then_inc(w1_ready, 1)
            START = link.n
            CH = 2 * E2 - 1

            def result(i):
                dve.wait_ge(projected, i + 1)
                dve.wait_ge(x_in, 16 * (i + 1))
                dve.wait_ge(out_done, 16 * (i + 1))
                V.tensor_tensor(y[:].rearrange("p j d -> p (j d)"), x[:].rearrange("p j d -> p (j d)"), po[:], ALU.add
                                ).then_inc(added, 1)
                dve.wait_ge(added, i + 1)
                dve.sem_inc(x_free, 1)

            def body(i, first):
                for c in range(DC):
                    link.at(i * (DC * CH) + (START + c * CH))
                    if c == 1 and not first:
                        result(i - 1)
                    for e in range(E2):
                        dve.wait_ge(down, i * (DC * N) + (c * N + 2 * e + 2))
                        if e == 0:
                            dve.wait_ge(t_in[c], (i + 1) * (16 * LOADS))
                            if not first:
                                dve.wait_ge(projected, i)
                        to = weighed_[e % 2] if e else acc[c]
                        ins = V.scalar_tensor_tensor(out=to[:], in0=pe_[e % 2][:], scalar=b2[:, e:e + 1],
                                                     in1=wb[c][:, e, :], op0=ALU.add, op1=ALU.mult)
                        link(ins)
                        dve.sem_inc(taken, 1)
                        if e:
                            link(V.tensor_tensor(acc[c][:], acc[c][:], to[:], ALU.add))
                    dve.sem_inc(summed, 1)
            blocks(dve, body)
            result(NB - 1)

        @block.tensor
        def _(pe):
            pe.wait_ge(w1_ready, 2)

            def project(i):
                pe.wait_ge(summed, (i + 1) * DC)
                if not isinstance(i, int) or i > 0:
                    pe.wait_ge(added, i)
                for j in range(TT):
                    to = po[:, j * D:(j + 1) * D]
                    for c in range(DC):
                        nc.tensor.matmul(to, acc[c][:, j * P:(j + 1) * P], wo[:, c, :], start=c == 0, stop=False)
                    last = nc.tensor.matmul(to, m.ones[0:1, :], bo[:], start=False, stop=True)
                last.then_inc(projected, 1)

            def lower(i, c, n):
                base = i * (DC * N) + (c * N + n)
                pe.wait_ge(active, base + 1)
                e, pair = n // 2, n % 2
                if pair == 0 and not (isinstance(i, int) and i == 0 and c == 0 and e < 2):
                    pe.wait_ge(taken, i * (DC * E2) + (c * E2 + e - 1))
                for a in range(2):
                    g = 2 * pair + a
                    last = nc.tensor.matmul(pe_[e % 2][g * HD:(g + 1) * HD, :], w2[:, e, :],
                                            hm[n % HB][:, a * TB:(a + 1) * TB], start=True, stop=True)
                last.then_inc(down, 1)

            def body(i, first):
                for c in range(DC):
                    for n in range(N):
                        base = i * (DC * N) + (c * N + n)
                        if n == 0:
                            pe.wait_ge(t_in[c], (i + 1) * (16 * LOADS))
                        if not (first and c == 0 and n < 2):
                            pe.wait_ge(active, base - 1)
                        e, pair = n // 2, n % 2
                        for a in range(2):
                            for s in range(2):
                                last = nc.tensor.matmul(pu[n % 2][:, a * TB:(a + 1) * TB], w1[s][:, e, :],
                                                        xt[c][s][:, 2 * pair + a, :], start=s == 0, stop=s == 1)
                        last.then_inc(up, 1)
                        if n >= 2:
                            lower(i, c, n - 2)
                        elif c:
                            lower(i, c - 1, N - 2 + n)
                        elif not first:
                            lower(i - 1, DC - 1, N - 2 + n)
                        if n == 3 and c == 0 and not first:
                            project(i - 1)
            blocks(pe, body)
            for n in (N - 2, N - 1):
                lower(NB - 1, DC - 1, n)
            project(NB - 1)


def second(nc, m, d):
    weights_of_experts(nc, m, d)
    if UPTO == 3:
        return finish_debug(nc, d, "x3")
    head_experts(nc, m, d)


_SCRATCH = (("q_parts0", (3 * D, T), BF16), ("q_parts1", (3 * D, T), BF16), ("k_parts0", (3 * D, S), BF16),
            ("k_parts1", (3 * D, S), BF16), ("sums", (H * P, TB), FP32), ("x1", (T, D), FP32), ("x2", (T, D), FP32),
            ("x3", (T, D), FP32), ("t_parts", (3 * D, T), BF16), ("w_t", (NB * HM * E2, TB), FP32), ("slots_in", (T, D), FP32), ("slots_out", (T, D), FP32))
UPTO = None


def program(nc, d, out):
    d = dict(d)
    for name, shape, dt in _SCRATCH:
        d[name] = nc.dram_tensor(name, shape, dt, kind="Internal").ap()
    for n in ("q_parts", "k_parts"):
        d[n] = [d[n + "0"], d[n + "1"]]
    d["x_rows"] = d["x"].rearrange("a t d -> (a t) d")
    d["out_rows"] = out.rearrange("a t d -> (a t) d")
    fast = Path("f", list(range(FAST_FROM, KT)), False, 4)
    full = Path("a", list(range(KT)), False, 4)
    causal = Path("c", list(range(KT)), True, 4)
    with ExitStack() as ctx:
        m = place_shared(nc, ctx)
        with nc.sbuf_tensor("mask", [P, NT * S], BF16) as mask:
            prepare(nc, m, d, mask)
            attend(nc, m, d, 0, [fast, full], mask)
        m.clear_semaphores(nc)
        router(nc, m, d)
        if UPTO == 1:
            return finish_debug(nc, d, "x1")
        experts(nc, m, d)
        gather(nc, m, d)
        if UPTO == 2:
            return finish_debug(nc, d, "x2")
        m.clear_semaphores(nc)
        attend(nc, m, d, 1, [causal])
        second(nc, m, d)


def finish_debug(nc, d, name):
    with nc.semaphore("dbg") as sem, nc.Block() as block:
        @block.sync
        def _(sp):
            sp.dma_start(d["out_rows"], d[name]).then_inc(sem, 16)
            sp.wait_ge(sem, 16)


_INS = ['x', 'ctx_1024', 'mask_Bx1xSxS2_bk1'] + [
    f'L{l}_xattn_{n}' for l in range(2) for n in ('Wq', 'bq', 'Wk', 'bk', 'Wv', 'bv', 'Wo', 'bo')] + [
    f'L0_ffn_{n}' for n in ('Wr', 'br', 'W1', 'b1', 'W2', 'b2')] + [
    f'L1_ffn_{n}' for n in ('Wm', 'bm', 'expert_emb', 'W1', 'b1', 'W2', 'b2', 'Wo', 'bo')]


def kernel(**inputs):
    import numpy as np
    import concourse.bacc as bacc
    from concourse.bass_utils import run_bass_kernel_spmd

    nc = bacc.Bacc("TRN2", target_bir_lowering=False, num_devices=1)
    arrays, d = {}, {}
    for name in _INS:
        a = np.ascontiguousarray(inputs[name])
        arrays["in_" + name] = a
        d[name] = nc.dram_tensor("in_" + name, a.shape, mybir.dt.from_np(a.dtype), kind="ExternalInput").ap()
    d["mask"] = d["mask_Bx1xSxS2_bk1"]
    out = nc.dram_tensor("out_0", (1, T, D), FP32, kind="ExternalOutput").ap()
    program(nc, d, out)
    return run_bass_kernel_spmd(nc, [arrays], core_ids=[0]).results[0]["out_0"]
```

```python
import concourse.bass as bass
from concourse import mybir
from contextlib import ExitStack

FP32 = mybir.dt.float32
BF16 = mybir.dt.bfloat16
U8 = mybir.dt.uint8
I32 = mybir.dt.int32
U32 = mybir.dt.uint32
ALU = mybir.AluOpType
ACT = mybir.ActivationFunctionType
AXIS = mybir.AxisListType

P = 128
T = 2048
D = 256
DC = D // P
S = 1601
H = 16
DH = D // H
TB = 512
NB = T // TB
TT = TB // P
NT = T // P
KT = -(-S // P)
KLAST = S - P * (KT - 1)
SFULL = S // TB
STACK = 6 * DH
ROWS = STACK + 2
GROUPS = ((0, 3), (3, 2), (5, 1))
BIG = 2.0 ** 100
EPS = 1e-5
E1 = 8
CAP = T // E1
HM, E2, HD, F2 = 8, 16, 32, 128
MX = 3
U = 4
LEAD = 4
FAST_FROM = 9


def keys_of(kt):
    return KLAST if kt == KT - 1 else P


def hold(eng, sem, value, passed):
    eng.wait_ge(sem, value)
    eng.sem_inc(passed, 1)


class Chain:

    def __init__(self, eng, sem):
        self.eng, self.sem, self.base, self.n = eng, sem, 0, 0

    def at(self, base):
        self.base, self.n = base, 0

    def __call__(self, ins):
        self.n += 1
        ins.then_inc(self.sem, 1)
        self.eng.wait_ge(self.sem, self.base + self.n)


class Shared:

    def __init__(self):
        self.semaphores = []

    def semaphore(self, nc, name):
        self.semaphores.append(nc.alloc_semaphore(name))
        return self.semaphores[-1]

    def clear_semaphores(self, nc):
        nc.clear_and_free_semaphores(self.semaphores)
        nc.all_engine_barrier()
        self.semaphores = []


def place_shared(nc, ctx):
    m = Shared()

    def sb(name, shape, dt):
        return ctx.enter_context(nc.sbuf_tensor(name, shape, dt))

    m.ident = sb("ident", [P, P], FP32)
    m.ident_bf = sb("ident_bf", [P, P], BF16)
    m.neg_big = sb("neg_big", [P, P], BF16)
    m.late_key = sb("late_key", [P, P], BF16)
    m.late_key_q = sb("late_key_q", [P, P], BF16)
    m.upto = sb("upto", [P, P], FP32)
    m.ones = sb("ones", [P, P], FP32)
    m.minus_half = sb("minus_half", [P, TT], FP32)
    m.v = [sb(f"v{l}", [P, KT, D], FP32) for l in range(2)]
    m.slots = sb("slots", [P, NT], U32)
    m.gates = sb("gates", [P, NT], FP32)
    m.wq1 = sb("wq1", [P, DC, D], FP32)
    m.wo1 = sb("wo1", [P, DC, D], FP32)
    m.passed = nc.alloc_semaphore("passed")
    m.flag = sb("flag", [P, 1], I32)
    return m


def make_constants(nc, pool, m, made):
    link = Chain(pool, made)
    link(nc.gpsimd.memset(m.ones[:], 1.0))
    link(nc.gpsimd.memset(m.minus_half[:], -0.5))
    for buf, op, base, step, up, fill in (
        (m.ident, ALU.not_equal, 0, -1, 1, 1.0),
        (m.ident_bf, ALU.not_equal, 0, -1, 1, 1.0),
        (m.neg_big, ALU.not_equal, 0, -1, 1, -BIG),
        (m.late_key, ALU.is_ge, 0, 1, -1, 1.0),
        (m.late_key_q, ALU.is_ge, 0, -1, 1, 1.0),
        (m.upto, ALU.is_gt, 0, -1, 1, 1.0),
    ):
        link(nc.gpsimd.memset(buf[:], 0.0))
        link(nc.gpsimd.affine_select(out=buf[:], in_=buf[:], compare_op=op, fill=fill, base=base,
                                     pattern=[[step, P]], channel_multiplier=up))
    return link.n


def normalize(nc, m, dve, link, xb, xn, stats, mv, rstd, stats_ready, rstd_ready, at):
    for j in range(TT):
        ins = nc.vector.bn_stats(stats[:, j, :], xb[:, j, :])
        if j == TT - 1:
            link(ins)
            dve.sem_inc(m.passed, 1)
    for j in range(TT):
        ins = nc.vector.bn_aggr(mv[:, j, :], stats[:, j, :])
    ins.then_inc(stats_ready, 1)
    dve.wait_ge(rstd_ready, at + 1)
    for j in range(TT):
        ins = nc.vector.tensor_scalar(xn[:, j, :], xb[:, j, :], mv[:, j, 0:1], rstd[:, j:j + 1],
                                      ALU.subtract, ALU.mult)
    return ins


def root(nc, pool, m, mv, ve, rstd, stats_ready, ve_ready, rstd_ready, at):
    hold(pool, stats_ready, at + 1, m.passed)
    nc.gpsimd.tensor_scalar(ve[:], mv[:, :, 1], EPS, None, ALU.add).then_inc(ve_ready, 1)
    pool.wait_ge(ve_ready, at + 1)
    nc.gpsimd.tensor_tensor(rstd[:], ve[:], m.minus_half[:], ALU.pow).then_inc(rstd_ready, 1)


def prepare(nc, m, d, mask):
    with ExitStack() as ctx:
        def sb(name, shape, dt):
            return ctx.enter_context(nc.sbuf_tensor("a_" + name, shape, dt))

        def sem(name):
            return m.semaphore(nc, "a_" + name)

        Q, K0, K1 = range(3)
        w = {n: sb(n, [P, DC, D], FP32) for n in ("wq0", "wk0", "wv0", "wk1", "wv1")}
        weight = [w["wq0"], w["wk0"], w["wk1"]]
        wraw = sb("wraw", [P, DC, 4, D], FP32)
        brow = sb("brow", [1, 2, D], FP32)
        bcol = sb("bcol", [P, 3, DC], FP32)
        xb = sb("xb", [P, TT, D], FP32)
        cb = sb("cb", [P, TT, D], FP32)
        xn = sb("xn", [P, TT, D], FP32)
        xT = sb("xT", [P, DC, TB], FP32)
        cT = sb("cT", [P, DC, TB], FP32)
        kf = [sb(f"kf{s}", [P, DC, TB], FP32) for s in range(3)]
        rest = sb("rest", [P, DC, TB], FP32)
        parts = [sb(f"parts{s}", [P, 3, DC, TB], BF16) for s in range(3)]
        stats = sb("stats", [P, TT, 6], FP32)
        mv = sb("mv", [P, TT, 2], FP32)
        ve = sb("ve", [P, TT], FP32)
        rstd = sb("rstd", [P, TT], FP32)
        mraw = sb("mraw", [P, NT, S], U8)
        mlow = sb("mlow", [P, 2, NT], FP32)
        bad = sb("bad", [P, 4], FP32)
        pX = ctx.enter_context(nc.psum_tensor("a_pX", [P, DC, TB], FP32))
        pC = ctx.enter_context(nc.psum_tensor("a_pC", [P, DC, TB], FP32))
        pK = [ctx.enter_context(nc.psum_tensor(f"a_pK{l}", [P, DC, TB], FP32)) for l in range(2)]
        pP = [pX, pK[0], pK[1]]
        pF = pX[:, 0, 0:1]

        made, raw_in, w_in, wT, wT_sb = sem("made"), sem("raw_in"), sem("w_in"), sem("wT"), sem("wT_sb")
        x_in, x_free, c_in, c_free = sem("x_in"), sem("x_free"), sem("c_in"), sem("c_free")
        stats_ready, ve_ready, rstd_ready, xn_ready = sem("stats"), sem("ve"), sem("rstd"), sem("xn_ready")
        x_turned, xT_ready, c_turned, cT_ready = sem("x_turned"), sem("xT_ready"), sem("c_turned"), sem("cT_ready")
        proj, kf_ready, kf_free, split_done, parts_out = (
            [sem(f"{n}{s}") for s in range(3)] for n in ("proj", "kf_ready", "kf_free", "split_done", "parts_out"))
        v_done, v_copied, q_read = sem("v_done"), sem("v_copied"), sem("q_read")
        m_in, m_cast = sem("m_in"), sem("m_cast")
        bad_ready, bad_sum, dve_own = sem("bad_ready"), sem("bad_sum"), sem("dve_own")
        CONSTS = 14

        block = ctx.enter_context(nc.Block())

        def turns(eng, body):
            assert NB == SFULL + 1 and KT == SFULL * TT + 1
            with eng.Fori(0, SFULL) as i:
                body(i, TT, P)
            body(SFULL, 1, KLAST)

        @block.sync
        def _(sp):
            view = "(k p) n -> p k n"
            x_rows = d["x"].rearrange("a t d -> (a t) d")
            c_rows = d["ctx_1024"].rearrange("a t d -> (a t) d")

            def load(i, last):
                sp.wait_ge(x_free, i + 1)
                sp.dma_start(xb[:], x_rows[bass.ds(i * TB, TB), :].rearrange("(j p) d -> p j d", p=P)
                             ).then_inc(x_in, 16)
                sp.wait_ge(c_free, i + 1)
                if last:
                    sp.dma_start(cb[0:KLAST, 0, :], c_rows[SFULL * TB:S, :]).then_inc(c_in, 16)
                else:
                    sp.dma_start(cb[:], c_rows[bass.ds(i * TB, TB), :].rearrange("(j p) d -> p j d", p=P)
                                 ).then_inc(c_in, 16)

            def store(i, cols):
                for s, to in ((K0, d["k_parts"][0]), (K1, d["k_parts"][1]), (Q, d["q_parts"][0])):
                    n = TB if s == Q else cols
                    hold(sp, split_done[s], i + 1, m.passed)
                    sp.dma_start(to[:, bass.ds(i * TB, n)].rearrange("(q p) c -> p q c", p=P),
                                 parts[s][:, :, :, 0:n].rearrange("p g k c -> p (g k) c")).then_inc(parts_out[s], 16)

            sp.sem_inc(x_free, 1)
            sp.sem_inc(c_free, 1)
            for s in range(3):
                sp.sem_inc(parts_out[s], 16)
            load(0, False)
            for i, name in enumerate(("Wq", "Wk", "Wv", "Wo")):
                sp.dma_start(wraw[:, :, i, :], d["L1_xattn_" + name].rearrange(view, p=P)).then_inc(raw_in, 16)
            for name, src in (("wq0", d["L0_xattn_Wq"]), ("wk0", d["L0_xattn_Wk"]), ("wv0", d["L0_xattn_Wv"])):
                sp.dma_start(w[name][:], src.rearrange(view, p=P)).then_inc(w_in, 16)
            for l in range(2):
                sp.dma_start(brow[0:1, l, :], d[f"L{l}_xattn_bv"].rearrange("(a n) -> a n", a=1)).then_inc(w_in, 16)
            with nc.allow_non_contiguous_dma(reason="a bias as a column"):
                for i, name in enumerate(("L0_xattn_bq", "L0_xattn_bk", "L1_xattn_bk")):
                    sp.dma_start(bcol[:, i, :], d[name].rearrange("(k p) -> p k", p=P)).then_inc(w_in, 16)
            with sp.Fori(0, SFULL - 1) as i:
                load(i + 1, False)
                store(i, TB)
            load(SFULL, True)
            store(SFULL - 1, TB)
            store(SFULL, KLAST)
            for s in range(3):
                sp.wait_ge(parts_out[s], 16 * (NB + 1))

        @block.gpsimd
        def _(pool):
            n = make_constants(nc, pool, m, made)
            assert n == CONSTS
            m_rows = d["mask"].rearrange("a b t s -> (a b t) s")

            def body(i, tiles, rows):
                pool.dma_start(mraw[:, bass.ds(i * TT, TT), :],
                               m_rows[bass.ds(i * TB, TB), :].rearrange("(j p) s -> p j s", p=P)).then_inc(m_in, 16)
                root(nc, pool, m, mv, ve, rstd, stats_ready, ve_ready, rstd_ready, i)
                hold(pool, m_in, 16 * (i + 1), m.passed)
            turns(pool, body)

        @block.scalar
        def _(act):
            def evac(i, s, cols):
                act.wait_ge(proj[s], i + 1)
                act.wait_ge(kf_free[s], i + 1)
                for k in range(DC):
                    ins = nc.scalar.activation(kf[s][:, k, 0:cols], pP[s][:, k, 0:cols], ACT.Identity,
                                               bias=bcol[:, s, k:k + 1])
                ins.then_inc(kf_ready[s], 1)
                if s == Q:
                    act.wait_ge(kf_ready[s], i + 1)
                    act.sem_inc(q_read, 1)

            def copy_v(i, l, tiles, rows):
                act.wait_ge(v_done, i * 2 + (l + 1))
                v = pC[:].rearrange("p k (j d) -> p (k j) d", d=D)
                half = -(-tiles // 2)
                for j in range(0, tiles, half):
                    ins = nc.scalar.copy(m.v[l][0:rows, bass.ds(i * TT + j, half), :], v[0:rows, j:j + half, :])
                ins.then_inc(v_copied, 1)

            def cast(i, first):
                act.wait_ge(m_in, 16 * (i + 1))
                for j in (first, first + 1):
                    nc.scalar.copy(mask[:, bass.ds(i * (TT * S) + j * S, S)],
                                   mraw[:, bass.ds(i * TT + j, 1), :].rearrange("p j s -> p (j s)")).then_inc(m_cast, 1)

            for i in range(4):
                act.wait_ge(wT, i + 1)
                dst = (m.wq1, w["wk1"], w["wv1"], m.wo1)[i]
                nc.scalar.copy(dst[:], pK[i % 2][:, :, 0:D]).then_inc(wT_sb, 1)
            act.wait_ge(w_in, 16 * 8)

            def body(i, tiles, rows):
                cols = tiles * P if tiles > 1 else rows
                act.wait_ge(c_turned, i + 1)
                nc.scalar.copy(cT[:, :, 0:cols], pC[:, :, 0:cols]).then_inc(cT_ready, 1)
                act.wait_ge(x_turned, i + 1)
                nc.scalar.copy(xT[:], pX[:]).then_inc(xT_ready, 1)
                evac(i, K0, cols)
                cast(i, 0)
                copy_v(i, 0, tiles, rows)
                evac(i, K1, cols)
                evac(i, Q, TB)
                copy_v(i, 1, tiles, rows)
                cast(i, 2)
            turns(act, body)
            act.wait_ge(m_cast, NT)

        @block.vector
        def _(dve):
            link = Chain(dve, dve_own)
            for s in range(3):
                dve.sem_inc(kf_free[s], 1)
            LINKS = 1 + 3 * 3

            def cut(i, s, cols):
                dve.wait_ge(kf_ready[s], i + 1)
                dve.wait_ge(parts_out[s], 16 * (i + 1))
                link(nc.vector.tensor_copy(parts[s][:, 0, :, 0:cols], kf[s][:, :, 0:cols]))
                link(nc.vector.tensor_tensor(rest[:, :, 0:cols], kf[s][:, :, 0:cols], parts[s][:, 0, :, 0:cols],
                                             ALU.subtract))
                dve.sem_inc(kf_free[s], 1)
                link(nc.vector.tensor_copy(parts[s][:, 1, :, 0:cols], rest[:, :, 0:cols]))
                nc.vector.tensor_tensor(parts[s][:, 2, :, 0:cols], rest[:, :, 0:cols], parts[s][:, 1, :, 0:cols],
                                        ALU.subtract).then_inc(split_done[s], 1)

            def body(i, tiles, rows):
                cols = tiles * P if tiles > 1 else rows
                link.at(i * LINKS)
                dve.wait_ge(x_in, 16 * (i + 1))
                normalize(nc, m, dve, link, xb, xn, stats, mv, rstd, stats_ready, rstd_ready, i
                          ).then_inc(xn_ready, 1)
                dve.wait_ge(xn_ready, i + 1)
                dve.sem_inc(x_free, 1)
                dve.wait_ge(m_in, 16 * (i + 1))
                at = bass.ds(i * TT, TT)
                nc.vector.tensor_reduce(mlow[:, 0, at], mraw[:, at, 0:FAST_FROM * P], AXIS.X, ALU.min)
                cut(i, K0, cols)
                nc.vector.tensor_reduce(mlow[:, 1, at], mraw[:, at, FAST_FROM * P:S], AXIS.X, ALU.min)
                cut(i, K1, cols)
                cut(i, Q, TB)
            turns(dve, body)
            dve.wait_ge(split_done[Q], NB)
            link.at(NB * LINKS)
            link(nc.vector.tensor_reduce(bad[:, 0:1], mlow[:, 0, :], AXIS.X, ALU.min))
            link(nc.vector.tensor_reduce(bad[:, 1:2], mlow[:, 1, :], AXIS.X, ALU.max))
            nc.vector.tensor_tensor(bad[:, 2:3], bad[:, 0:1], bad[:, 1:2], ALU.subtract).then_inc(bad_ready, 1)
            dve.wait_ge(bad_sum, 1)
            nc.vector.tensor_scalar(m.flag[:], pF, float(P), None, ALU.is_equal).then_inc(bad_ready, 1)

        @block.tensor
        def _(pe):
            pe.wait_ge(made, CONSTS)
            pe.wait_ge(raw_in, 16 * 4)
            for i in range(4):
                if i >= 2:
                    pe.wait_ge(wT_sb, i - 1)
                for k in range(DC):
                    for j in range(DC):
                        last = nc.tensor.transpose(pK[i % 2][:, k, j * P:j * P + P], wraw[:, j, i, k * P:k * P + P],
                                                   m.ident[:])
                last.then_inc(wT, 1)
            pe.wait_ge(wT_sb, 4)
            pe.wait_ge(w_in, 16 * 8)
            pe.sem_inc(v_copied, 1)
            pe.sem_inc(q_read, 1)

            def turn(to, src, tiles, rows):
                for k in range(DC):
                    for j in range(tiles):
                        last = nc.tensor.transpose(to[:, k, j * P:j * P + rows], src[0:rows, j, k * P:k * P + P],
                                                   m.ident[0:rows, 0:rows])
                return last

            def project(s, src, cols):
                for k in range(DC):
                    for c in range(DC):
                        last = nc.tensor.matmul(pP[s][:, k, 0:cols], weight[s][:, c, k * P:k * P + P],
                                                src[:, c, 0:cols], start=c == 0, stop=c == DC - 1)
                last.then_inc(proj[s], 1)

            def values(l, tiles, rows):
                for j in range(tiles):
                    to = pC[0:rows, j // 2, (j % 2) * D:(j % 2 + 1) * D]
                    for c in range(DC):
                        nc.tensor.matmul(to, cT[:, c, j * P:j * P + rows], w[f"wv{l}"][:, c, :],
                                         start=c == 0, stop=False)
                    last = nc.tensor.matmul(to, m.ones[0:1, 0:rows], brow[0:1, l, :], start=False, stop=True)
                last.then_inc(v_done, 1)

            def body(i, tiles, rows):
                cols = tiles * P if tiles > 1 else rows
                pe.wait_ge(c_in, 16 * (i + 1))
                pe.wait_ge(v_copied, i * 2 + 1)
                turn(pC, cb, tiles, rows).then_inc(c_turned, 1)
                pe.wait_ge(xn_ready, i + 1)
                pe.wait_ge(q_read, i + 1)
                turn(pX, xn, TT, P).then_inc(x_turned, 1)
                pe.wait_ge(c_turned, i + 1)
                pe.sem_inc(c_free, 1)
                pe.wait_ge(cT_ready, i + 1)
                project(K0, cT, cols)
                values(0, tiles, rows)
                pe.wait_ge(xT_ready, i + 1)
                project(K1, cT, cols)
                project(Q, xT, TB)
                pe.wait_ge(v_copied, i * 2 + 2)
                values(1, tiles, rows)
            turns(pe, body)
            pe.wait_ge(bad_ready, 1)
            nc.tensor.matmul(pF, m.ones[:], bad[:, 2:3], start=True, stop=True).then_inc(bad_sum, 1)


class Tail:

    LOADS = 5
    LINKS = 3

    def __init__(t, nc, ctx, m, d, layer, x_from, x_to):
        def sb(name, shape, dt):
            return ctx.enter_context(nc.sbuf_tensor(f"e{layer}_" + name, shape, dt))

        def sem(name):
            return m.semaphore(nc, f"e{layer}_" + name)

        t.nc, t.m, t.d, t.layer, t.x_from, t.x_to = nc, m, d, layer, x_from, x_to
        t.num = sb("num", [P, DC, TB], FP32)
        t.den = sb("den", [P, DC, TB], FP32)
        t.x = sb("x", [P, TT, D], FP32)
        t.y = sb("y", [P, TT, D], FP32)
        t.xn = sb("xn", [P, TT, D], FP32)
        t.xT = sb("xT", [P, DC, TB], FP32)
        t.stats, t.mv = sb("stats", [P, TT, 6], FP32), sb("mv", [P, TT, 2], FP32)
        t.ve, t.rstd = sb("ve", [P, TT], FP32), sb("rstd", [P, TT], FP32)
        t.wo = m.wo1 if layer else sb("wo", [P, DC, D], FP32)
        t.bo = sb("bo", [1, D], FP32)
        t.w_in, t.x_in, t.x_free = sem("w_in"), sem("x_in"), sem("x_free")
        t.divided, t.projected, t.added = sem("divided"), sem("projected"), sem("added")
        t.stats_ready, t.ve_ready, t.rstd_ready = sem("stats_ready"), sem("ve_ready"), sem("rstd_ready")
        t.xn_ready, t.turned, t.xT_ready = sem("xn_ready"), sem("turned"), sem("xT_ready")
        t.stored = sem("stored")

    def weights(t, sp):
        name = f"L{t.layer}_xattn_"
        if not t.layer:
            sp.dma_start(t.wo[:], t.d[name + "Wo"].rearrange("(k p) n -> p k n", p=P)).then_inc(t.w_in, 16)
        sp.dma_start(t.bo[:], t.d[name + "bo"].rearrange("(a n) -> a n", a=1)).then_inc(t.w_in, 16)
        sp.sem_inc(t.x_free, 1)
        sp.sem_inc(t.stored, 16)
        return 1 if t.layer else 2

    def load(t, sp, i):
        sp.wait_ge(t.x_free, i + 1)
        for c in range(DC):
            for u, to in enumerate((t.num, t.den)):
                src = t.d["sums"].rearrange("(h j u r) c -> j u h r c", h=H, j=NB, u=2)
                src = src[bass.ds(i, 1), u, c * (H // DC):(c + 1) * (H // DC)]
                sp.dma_start(to[:, c, :], src).then_inc(t.x_in, 16)
        sp.dma_start(t.x[:], t.x_from[bass.ds(i * TB, TB), :].rearrange("(j p) d -> p j d", p=P)).then_inc(t.x_in, 16)

    def store(t, sp, i):
        sp.wait_ge(t.added, i + 1)
        sp.dma_start(t.x_to[bass.ds(i * TB, TB), :].rearrange("(j p) d -> p j d", p=P), t.y[:]).then_inc(t.stored, 16)

    def vector(t, dve, link, i, po):
        nc = t.nc
        dve.wait_ge(t.x_in, (i + 1) * (16 * t.LOADS))
        link(nc.vector.reciprocal(t.den[:], t.den[:]))
        nc.vector.tensor_tensor(t.num[:], t.num[:], t.den[:], ALU.mult).then_inc(t.divided, 1)
        dve.wait_ge(t.projected, i + 1)
        dve.wait_ge(t.stored, 16 * (i + 1))
        link(nc.vector.tensor_tensor(t.y[:].rearrange("p j d -> p (j d)"), t.x[:].rearrange("p j d -> p (j d)"),
                                     po[:], ALU.add))
        dve.sem_inc(t.added, 1)
        dve.sem_inc(t.x_free, 1)
        normalize(nc, t.m, dve, link, t.y, t.xn, t.stats, t.mv, t.rstd, t.stats_ready, t.rstd_ready, i
                  ).then_inc(t.xn_ready, 1)

    def gpsimd(t, pool, i):
        root(t.nc, pool, t.m, t.mv, t.ve, t.rstd, t.stats_ready, t.ve_ready, t.rstd_ready, i)

    def scalar(t, act, i, pT):
        act.wait_ge(t.turned, i + 1)
        for k in range(DC):
            ins = t.nc.scalar.copy(t.xT[:, k, :], pT[k][:])
        ins.then_inc(t.xT_ready, 1)

    def tensor(t, pe, i, po, pT):
        nc = t.nc
        pe.wait_ge(t.divided, i + 1)
        for j in range(TT):
            to = po[:, j * D:(j + 1) * D]
            for c in range(DC):
                nc.tensor.matmul(to, t.num[:, c, j * P:(j + 1) * P], t.wo[:, c, :], start=c == 0, stop=False)
            last = nc.tensor.matmul(to, t.m.ones[0:1, :], t.bo[:], start=False, stop=True)
        last.then_inc(t.projected, 1)
        pe.wait_ge(t.xn_ready, i + 1)
        for k in range(DC):
            for j in range(TT):
                last = nc.tensor.transpose(pT[k][:, j * P:(j + 1) * P], t.xn[:, j, k * P:(k + 1) * P], t.m.ident[:])
        last.then_inc(t.turned, 1)
        pe.wait_ge(t.xT_ready, i + 1)


def router(nc, m, d):
    with ExitStack() as ctx:
        t = Tail(nc, ctx, m, d, 0, d["x_rows"], d["x1"])

        def sb(name, shape, dt):
            return ctx.enter_context(nc.sbuf_tensor("r_" + name, shape, dt))

        def sem(name):
            return m.semaphore(nc, "r_" + name)

        wr = sb("wr", [P, DC, E1], FP32)
        br = sb("br", [1, E1], FP32)
        rank = sb("rank", [P, TT, E1], FP32)
        first_slot = sb("first_slot", [P, TT, E1], FP32)
        zero = sb("zero", [P, T // P * D], FP32)
        l = sb("l", [P, TT, E1], FP32)
        ex = sb("ex", [P, TT, E1], FP32)
        prob = sb("prob", [P, TT, E1], FP32)
        key = sb("key", [P, TT, E1], FP32)
        pick = sb("pick", [P, TT, E1], FP32)
        seen = sb("seen", [P, E1], FP32)
        seen_now = sb("seen_now", [P, E1], FP32)
        col = sb("col", [P, 10, TT], FP32)
        slot = sb("slot", [P, TT], U32)
        xg = sb("xg", [P, TT, D], FP32)
        po = ctx.enter_context(nc.psum_tensor("r_po", [P, TT * D], FP32))
        pT = [ctx.enter_context(nc.psum_tensor(f"r_pT{k}", [P, TB], FP32)) for k in range(DC)]
        pl = ctx.enter_context(nc.psum_tensor("r_pl", [P, TT * E1], FP32))
        pp = ctx.enter_context(nc.psum_tensor("r_pp", [P, TT * E1], FP32))
        consts, own, zeroed = sem("consts"), sem("own"), sem("zeroed")
        logits, lowered, expd = sem("logits"), sem("lowered"), sem("expd")
        picked, counted, slotted = sem("picked"), sem("counted"), sem("slotted")
        scattered, rows_free = sem("scattered"), sem("rows_free")
        top, den, gate, best, pos, off, drop, keep, fs = range(9)
        CONSTS = 3 + 2 * E1
        block = ctx.enter_context(nc.Block())

        @block.sync
        def _(sp):
            assert t.weights(sp) == 2
            sp.dma_start(wr[:], d["L0_ffn_Wr"].rearrange("(k p) n -> p k n", p=P)).then_inc(t.w_in, 16)
            sp.dma_start(br[:], d["L0_ffn_br"].rearrange("(a n) -> a n", a=1)).then_inc(t.w_in, 16)
            sp.wait_ge(consts, CONSTS)
            sp.dma_start(d["slots_in"].rearrange("(p n) d -> p (n d)", p=P), zero[:]).then_inc(zeroed, 16)
            with sp.Fori(0, NB) as i:
                t.load(sp, i)
                t.store(sp, i)
            sp.wait_ge(t.stored, 16 * (NB + 1))
            sp.wait_ge(zeroed, 16)

        @block.gpsimd
        def _(pool):
            nc.gpsimd.memset(zero[:], 0.0).then_inc(consts, 1)
            nc.gpsimd.memset(seen[:], 0.0).then_inc(consts, 1)
            nc.gpsimd.memset(seen_now[:], 0.0).then_inc(consts, 1)
            for e in range(E1):
                nc.gpsimd.memset(rank[:, :, e], float(E1 - e)).then_inc(consts, 1)
                nc.gpsimd.memset(first_slot[:, :, e], float(CAP * e)).then_inc(consts, 1)
            pool.sem_inc(rows_free, 1)
            pool.wait_ge(zeroed, 16)
            with pool.Fori(0, NB) as i:
                t.gpsimd(pool, i)
                hold(pool, slotted, i + 1, m.passed)
                for j in range(TT):
                    nc.gpsimd.indirect_dma_start(
                        out=d["slots_in"], out_offset=bass.IndirectOffsetOnAxis(ap=slot[:, j:j + 1], axis=0),
                        in_=xg[:, j, :], in_offset=None, bounds_check=T - 1, oob_is_err=False,
                    ).then_inc(scattered, 16)
                hold(pool, scattered, (i + 1) * (16 * TT), rows_free)

        @block.scalar
        def _(act):
            with act.Fori(0, NB) as i:
                t.scalar(act, i, pT)
                act.wait_ge(lowered, i + 1)
                nc.scalar.activation(ex[:], l[:], ACT.Exp).then_inc(expd, 1)

        @block.vector
        def _(dve):
            link = Chain(dve, own)
            V = nc.vector
            LINKS = t.LINKS + 18

            def wide(c):
                return col[:, c, :].unsqueeze(2).to_broadcast([P, TT, E1])

            plv = pl[:].rearrange("p (j e) -> p j e", e=E1)
            ppv = pp[:].rearrange("p (j e) -> p j e", e=E1)
            dve.wait_ge(consts, CONSTS)
            with dve.Fori(0, NB) as i:
                link.at(i * LINKS)
                t.vector(dve, link, i, po)
                dve.wait_ge(logits, i + 1)
                link(V.tensor_reduce(col[:, top, :], plv, AXIS.X, ALU.max))
                V.tensor_tensor(l[:], plv, wide(top), ALU.subtract).then_inc(lowered, 1)
                dve.wait_ge(expd, i + 1)
                link(V.tensor_reduce(col[:, den, :], ex[:], AXIS.X, ALU.add))
                link(V.reciprocal(col[:, den, :], col[:, den, :]))
                link(V.tensor_tensor(prob[:], ex[:], wide(den), ALU.mult))
                link(V.tensor_reduce(col[:, gate, :], prob[:], AXIS.X, ALU.max))
                link(V.tensor_tensor(key[:], prob[:], wide(gate), ALU.is_equal))
                link(V.tensor_tensor(key[:], key[:], rank[:], ALU.mult))
                link(V.tensor_reduce(col[:, best, :], key[:], AXIS.X, ALU.max))
                V.tensor_tensor(pick[:], key[:], wide(best), ALU.is_equal).then_inc(picked, 1)
                dve.wait_ge(counted, i + 1)
                link(V.tensor_tensor(key[:], ppv, pick[:], ALU.mult))
                link(V.tensor_reduce(col[:, pos, :], key[:], AXIS.X, ALU.add))
                link(V.tensor_tensor(key[:], first_slot[:], pick[:], ALU.mult))
                link(V.tensor_reduce(col[:, off, :], key[:], AXIS.X, ALU.add))
                link(V.tensor_reduce(seen_now[:], pick[:].rearrange("p j e -> p e j"), AXIS.X, ALU.add))
                link(V.tensor_tensor(seen[:], seen[:], seen_now[:], ALU.add))
                link(V.tensor_scalar(col[:, drop, :], col[:, pos, :], float(CAP), float(4 * T), ALU.is_ge, ALU.mult))
                link(V.tensor_scalar(col[:, keep, :], col[:, pos, :], float(CAP), None, ALU.is_lt))
                link(V.tensor_tensor(col[:, fs, :], col[:, pos, :], col[:, off, :], ALU.add))
                dve.wait_ge(rows_free, i + 1)
                link(V.tensor_tensor(slot[:], col[:, fs, :], col[:, drop, :], ALU.add))
                V.tensor_copy(m.slots[:, bass.ds(i * TT, TT)], slot[:])
                V.tensor_tensor(m.gates[:, bass.ds(i * TT, TT)], col[:, gate, :], col[:, keep, :], ALU.mult)
                for j in range(TT):
                    ins = V.tensor_scalar(xg[:, j, :], t.xn[:, j, :], col[:, gate, j:j + 1], None, ALU.mult)
                ins.then_inc(slotted, 1)
            assert link.n == LINKS, link.n

        @block.tensor
        def _(pe):
            pe.wait_ge(t.w_in, 16 * 4)
            pe.wait_ge(consts, CONSTS)
            with pe.Fori(0, NB) as i:
                t.tensor(pe, i, po, pT)
                for j in range(TT):
                    to = pl[:, j * E1:(j + 1) * E1]
                    for c in range(DC):
                        nc.tensor.matmul(to, t.xT[:, c, j * P:(j + 1) * P], wr[:, c, :], start=c == 0, stop=False)
                    last = nc.tensor.matmul(to, m.ones[0:1, :], br[:], start=False, stop=True)
                last.then_inc(logits, 1)
                pe.wait_ge(picked, i + 1)
                for j in range(TT):
                    to = pp[:, j * E1:(j + 1) * E1]
                    nc.tensor.matmul(to, m.ones[:], seen[:], start=True, stop=False)
                    for a in range(j):
                        nc.tensor.matmul(to, m.ones[:], pick[:, a, :], start=False, stop=False)
                    last = nc.tensor.matmul(to, m.upto[:], pick[:, j, :], start=False, stop=True)
                last.then_inc(counted, 1)


def experts(nc, m, d):
    with ExitStack() as ctx:
        def sb(name, shape, dt):
            return ctx.enter_context(nc.sbuf_tensor("f_" + name, shape, dt))

        def sem(name):
            return m.semaphore(nc, "f_" + name)

        SC = CAP // P
        LOADS = 5
        w1, w2, b1, b2, xs, xsT, hT, eo, pT, ph, pe_ = [], [], [], [], [], [], [], [], [], [], []
        for b in range(2):
            w1.append(sb(f"w1{b}", [P, DC, D], FP32))
            w2.append(sb(f"w2{b}", [P, DC, D], FP32))
            b1.append(sb(f"b1{b}", [P, DC], FP32))
            b2.append(sb(f"b2{b}", [1, D], FP32))
            xs.append(sb(f"xs{b}", [P, SC, D], FP32))
            xsT.append(sb(f"xsT{b}", [P, DC, CAP], FP32))
            hT.append(sb(f"hT{b}", [P, DC, CAP], FP32))
            eo.append(sb(f"eo{b}", [P, SC, D], FP32))
            pT.append(ctx.enter_context(nc.psum_tensor(f"f_pT{b}", [P, DC * CAP], FP32)))
            ph.append(ctx.enter_context(nc.psum_tensor(f"f_ph{b}", [P, DC * CAP], FP32)))
            pe_.append(ctx.enter_context(nc.psum_tensor(f"f_pe{b}", [P, SC * D], FP32)))
        loaded = [sem(f"loaded{b}") for b in range(2)]
        stored = [sem(f"stored{b}") for b in range(2)]
        turned, xsT_ready, hidden, hT_ready, made, copied = (
            sem("turned"), sem("xsT_ready"), sem("hidden"), sem("hT_ready"), sem("made"), sem("copied"))
        eo_free = sem("eo_free")
        block = ctx.enter_context(nc.Block())

        def both(eng, body):
            with eng.Fori(0, E1 // 2) as p:
                for b in range(2):
                    body(p, b, p * 2 + b)

        @block.sync
        def _(sp):
            sp.sem_inc(made, 2)

            def body(p, b, e):
                hold(sp, made, e + 1, m.passed)
                for to, name in ((w1[b], "L0_ffn_W1"), (w2[b], "L0_ffn_W2")):
                    sp.dma_start(to[:], d[name].rearrange("e k n -> (e k) n")[bass.ds(e * D, D), :]
                                 .rearrange("(k p) n -> p k n", p=P)).then_inc(loaded[b], 16)
                with nc.allow_non_contiguous_dma(reason="a bias as a column"):
                    sp.dma_start(b1[b][:], d["L0_ffn_b1"].rearrange("e n -> (e n)")[bass.ds(e * D, D)]
                                 .rearrange("(k p) -> p k", p=P)).then_inc(loaded[b], 16)
                sp.dma_start(b2[b][:], d["L0_ffn_b2"][bass.ds(e, 1), :]).then_inc(loaded[b], 16)
                sp.dma_start(xs[b][:], d["slots_in"][bass.ds(e * CAP, CAP), :].rearrange("(k p) n -> p k n", p=P)
                             ).then_inc(loaded[b], 16)
            both(sp, body)

        @block.gpsimd
        def _(pool):
            def body(p, b, e):
                hold(pool, copied, e + 1, m.passed)
                pool.dma_start(d["slots_out"][bass.ds(e * CAP, CAP), :].rearrange("(k p) n -> p k n", p=P), eo[b][:]
                               ).then_inc(stored[b], 16)
                hold(pool, stored[b], 16 * (p + 1), eo_free)
            pool.sem_inc(eo_free, 2)
            both(pool, body)

        @block.scalar
        def _(act):
            def body(p, b, e):
                act.wait_ge(hidden, e + 1)
                for k in range(DC):
                    ins = nc.scalar.activation(hT[b][:, k, :], ph[b][:, k * CAP:(k + 1) * CAP], ACT.Relu,
                                               bias=b1[b][:, k:k + 1])
                ins.then_inc(hT_ready, 1)
            both(act, body)

        @block.vector
        def _(dve):
            def body(p, b, e):
                dve.wait_ge(turned, e + 1)
                nc.vector.tensor_copy(xsT[b][:].rearrange("p k c -> p (k c)"), pT[b][:]).then_inc(xsT_ready, 1)
                dve.wait_ge(made, e + 3)
                dve.wait_ge(eo_free, e + 1)
                nc.vector.tensor_copy(eo[b][:].rearrange("p k c -> p (k c)"), pe_[b][:]).then_inc(copied, 1)
            both(dve, body)

        @block.tensor
        def _(pe):
            def body(p, b, e):
                pe.wait_ge(loaded[b], (p + 1) * (16 * LOADS))
                for k in range(DC):
                    for j in range(SC):
                        last = nc.tensor.transpose(pT[b][:, k * CAP + j * P:k * CAP + (j + 1) * P],
                                                   xs[b][:, j, k * P:(k + 1) * P], m.ident[:])
                last.then_inc(turned, 1)
                pe.wait_ge(xsT_ready, e + 1)
                for k in range(DC):
                    for c in range(DC):
                        last = nc.tensor.matmul(ph[b][:, k * CAP:(k + 1) * CAP], w1[b][:, c, k * P:(k + 1) * P],
                                                xsT[b][:, c, :], start=c == 0, stop=c == DC - 1)
                last.then_inc(hidden, 1)
                pe.wait_ge(hT_ready, e + 1)
                for j in range(SC):
                    to = pe_[b][:, j * D:(j + 1) * D]
                    for c in range(DC):
                        nc.tensor.matmul(to, hT[b][:, c, j * P:(j + 1) * P], w2[b][:, c, :], start=c == 0, stop=False)
                    last = nc.tensor.matmul(to, m.ones[0:1, :], b2[b][:], start=False, stop=True)
                last.then_inc(made, 1)
            both(pe, body)


def gather(nc, m, d):
    with ExitStack() as ctx:
        def sb(name, shape, dt):
            return ctx.enter_context(nc.sbuf_tensor("g_" + name, shape, dt))

        def sem(name):
            return m.semaphore(nc, "g_" + name)

        x = sb("x", [P, TT, D], FP32)
        eo = sb("eo", [P, TT, D], FP32)
        y = sb("y", [P, TT, D], FP32)
        xn = sb("xn", [P, TT, D], FP32)
        xT = sb("xT", [P, DC, TB], FP32)
        kf = sb("kf", [P, DC, TB], FP32)
        rest = sb("rest", [P, DC, TB], FP32)
        parts = sb("parts", [P, 3, DC, TB], BF16)
        bq = sb("bq", [P, DC], FP32)
        slot = sb("slot", [P, TT], U32)
        gate = sb("gate", [P, TT], FP32)
        stats, mv = sb("stats", [P, TT, 6], FP32), sb("mv", [P, TT, 2], FP32)
        ve, rstd = sb("ve", [P, TT], FP32), sb("rstd", [P, TT], FP32)
        pT = [ctx.enter_context(nc.psum_tensor(f"g_pT{k}", [P, TB], FP32)) for k in range(DC)]
        pq = [ctx.enter_context(nc.psum_tensor(f"g_pq{k}", [P, TB], FP32)) for k in range(DC)]
        w_in, x_in, x_free, eo_in, cleared, own = (
            sem("w_in"), sem("x_in"), sem("x_free"), sem("eo_in"), sem("cleared"), sem("own"))
        added, x_out, stats_ready, ve_ready, rstd_ready = (
            sem("added"), sem("x_out"), sem("stats_ready"), sem("ve_ready"), sem("rstd_ready"))
        xn_ready, turned, xT_ready, proj, kf_ready, split_done, parts_out, slot_ready = (
            sem("xn_ready"), sem("turned"), sem("xT_ready"), sem("proj"), sem("kf_ready"), sem("split_done"),
            sem("parts_out"), sem("slot_ready"))
        block = ctx.enter_context(nc.Block())

        @block.sync
        def _(sp):
            with nc.allow_non_contiguous_dma(reason="a bias as a column"):
                sp.dma_start(bq[:], d["L1_xattn_bq"].rearrange("(k p) -> p k", p=P)).then_inc(w_in, 16)
            sp.sem_inc(x_free, 1)
            sp.sem_inc(x_out, 16)
            sp.sem_inc(parts_out, 16)
            with sp.Fori(0, NB) as i:
                hold(sp, x_free, i + 1, m.passed)
                sp.dma_start(x[:], d["x1"][bass.ds(i * TB, TB), :].rearrange("(j p) d -> p j d", p=P)).then_inc(x_in, 16)
                hold(sp, added, i + 1, m.passed)
                sp.dma_start(d["x2"][bass.ds(i * TB, TB), :].rearrange("(j p) d -> p j d", p=P), y[:]).then_inc(x_out, 16)
                hold(sp, split_done, i + 1, m.passed)
                sp.dma_start(d["q_parts"][1][:, bass.ds(i * TB, TB)].rearrange("(q p) c -> p q c", p=P),
                             parts[:].rearrange("p g k c -> p (g k) c")).then_inc(parts_out, 16)
            sp.wait_ge(x_out, 16 * (NB + 1))
            sp.wait_ge(parts_out, 16 * (NB + 1))

        @block.gpsimd
        def _(pool):
            with pool.Fori(0, NB) as i:
                hold(pool, slot_ready, i + 1, m.passed)
                nc.gpsimd.memset(eo[:], 0.0).then_inc(cleared, 1)
                hold(pool, cleared, i + 1, m.passed)
                for j in range(TT):
                    nc.gpsimd.indirect_dma_start(
                        out=eo[:, j, :], out_offset=None, in_=d["slots_out"],
                        in_offset=bass.IndirectOffsetOnAxis(ap=slot[:, j:j + 1], axis=0),
                        bounds_check=T - 1, oob_is_err=False).then_inc(eo_in, 16)
                root(nc, pool, m, mv, ve, rstd, stats_ready, ve_ready, rstd_ready, i)

        @block.scalar
        def _(act):
            act.wait_ge(w_in, 16)
            with act.Fori(0, NB) as i:
                act.wait_ge(turned, i + 1)
                for k in range(DC):
                    ins = nc.scalar.copy(xT[:, k, :], pT[k][:])
                ins.then_inc(xT_ready, 1)
                act.wait_ge(proj, i + 1)
                for k in range(DC):
                    ins = nc.scalar.activation(kf[:, k, :], pq[k][:], ACT.Identity, bias=bq[:, k:k + 1])
                ins.then_inc(kf_ready, 1)

        @block.vector
        def _(dve):
            link = Chain(dve, own)
            V = nc.vector
            LINKS = 6
            with dve.Fori(0, NB) as i:
                link.at(i * LINKS)
                V.tensor_copy(slot[:], m.slots[:, bass.ds(i * TT, TT)])
                link(V.tensor_copy(gate[:], m.gates[:, bass.ds(i * TT, TT)]))
                dve.sem_inc(slot_ready, 1)
                dve.wait_ge(x_in, 16 * (i + 1))
                dve.wait_ge(eo_in, (i + 1) * (16 * TT))
                dve.wait_ge(x_out, 16 * (i + 1))
                for j in range(TT):
                    ins = V.scalar_tensor_tensor(out=y[:, j, :], in0=eo[:, j, :], scalar=gate[:, j:j + 1], in1=x[:, j, :],
                                                 op0=ALU.mult, op1=ALU.add)
                link(ins)
                dve.sem_inc(added, 1)
                dve.sem_inc(x_free, 1)
                normalize(nc, m, dve, link, y, xn, stats, mv, rstd, stats_ready, rstd_ready, i).then_inc(xn_ready, 1)
                dve.wait_ge(kf_ready, i + 1)
                dve.wait_ge(parts_out, 16 * (i + 1))
                link(V.tensor_copy(parts[:, 0], kf[:]))
                link(V.tensor_tensor(rest[:], kf[:], parts[:, 0], ALU.subtract))
                link(V.tensor_copy(parts[:, 1], rest[:]))
                V.tensor_tensor(parts[:, 2], rest[:], parts[:, 1], ALU.subtract).then_inc(split_done, 1)
            assert link.n == LINKS, link.n

        @block.tensor
        def _(pe):
            with pe.Fori(0, NB) as i:
                pe.wait_ge(xn_ready, i + 1)
                for k in range(DC):
                    for j in range(TT):
                        last = nc.tensor.transpose(pT[k][:, j * P:(j + 1) * P], xn[:, j, k * P:(k + 1) * P], m.ident[:])
                last.then_inc(turned, 1)
                pe.wait_ge(xT_ready, i + 1)
                for k in range(DC):
                    for c in range(DC):
                        last = nc.tensor.matmul(pq[k][:], m.wq1[:, c, k * P:(k + 1) * P], xT[:, c, :],
                                                start=c == 0, stop=c == DC - 1)
                last.then_inc(proj, 1)


class Path:

    def __init__(self, name, kts, causal, pbufs):
        self.name, self.kts, self.causal, self.pbufs = name, kts, causal, pbufs
        self.c0 = kts[0] * P
        self.steps = [(kt, half, max(half * 2 * TB, kt * P if causal else 0)) for kt in kts for half in range(2)
                      if not causal or kt * P < (half + 1) * 2 * TB]
        self.pieces = []
        for i in range(NT):
            end = min(S, P * (i + 1)) if causal else S
            self.pieces += [(i, n, c, min(c + TB, end)) for n, c in enumerate(range(self.c0, end, TB))]
        self.ne = len(self.steps)
        self.nm = len(self.pieces) + 1
        assert (U * self.ne) % pbufs == 0 
        self.plan()

    def plan(self):
        cost = [(half + 1) * 2 * TB - q0 + 220 for _, half, q0 in self.steps]
        work = [end - c + 80 for _, _, c, end in self.pieces]
        done, at, share = 0, 0, []
        for n in range(self.nm):
            share.append(done / sum(work))
            done += work[n] if n < len(work) else 0
        self.slots = [[] for _ in range(self.ne)]
        shift = 1 - sum(cost[-LEAD:]) / sum(cost)
        edges = [sum(cost[:e + 1]) / sum(cost) for e in range(self.ne)]
        for k in (1, 2):
            for n in range(self.nm):
                when = shift - 1 + share[n] + (k - 1)
                if n == self.nm - 1:
                    when = shift - 1e-6 + (k - 1)
                if 0 <= when < 1:
                    self.slots[next(e for e in range(self.ne) if when < edges[e])].append((k, n))
        self.early = [n for slot in self.slots for k, n in slot if k == 2]


def wait(eng, sem, value):
    if not (isinstance(value, int) and value <= 0):
        eng.wait_ge(sem, value)


def attend(nc, m, d, layer, paths, mask=None):
    with ExitStack() as ctx:
        def sb(name, shape, dt):
            return ctx.enter_context(nc.sbuf_tensor(f"t{layer}_" + name, shape, dt))

        q = [sb(f"q{b}", [ROWS, T], BF16) for b in range(U)]
        k = [sb(f"k{b}", [ROWS, KT * P], BF16) for b in range(U)]
        vo = [sb(f"vo{b}", [P, KT, 2 * DH], FP32) for b in range(2)]
        prob = [sb(f"prob{b}", [P, 2 * TB], FP32) for b in range(max(x.pbufs for x in paths))]
        osb = [sb(f"osb{b}", [P, TB], FP32) for b in range(2)]
        part_max = sb("part_max", [P, NT, 4], FP32)
        neg_max = sb("neg_max", [P, NT], FP32)
        neg_rest = sb("neg_rest", [P, NT], FP32)
        neg_cols = sb("neg_cols", [P, 2 * NT], BF16)
        neg_rows = sb("neg_rows", [2 * NT, P], BF16)
        mask_t = sb("mask_t", [P, len(paths[-1].kts), T], BF16) if mask is not None else None
        scores = [ctx.enter_context(nc.psum_tensor(f"t{layer}_s{b}", [P, 2 * TB], FP32)) for b in range(2)]
        mx = [ctx.enter_context(nc.psum_tensor(f"t{layer}_m{b}", [P, TB], FP32)) for b in range(MX)]
        out = ctx.enter_context(nc.psum_tensor(f"t{layer}_o", [P, TB], FP32))
        READY = 2 + 1 + U
        NLOAD = 6

        class Sems:
            def __init__(s, name):
                def sem(n):
                    return m.semaphore(nc, f"t{layer}{name}_{n}")
                s.qk_in = [sem(f"qk_in{b}") for b in range(U)]
                s.neg_in = [sem(f"neg_in{b}") for b in range(U)]
                s.v_in = [sem(f"v_in{b}") for b in range(2)]
                s.scored = sem("scored")
                s.expd = sem("expd")
                s.used = sem("used")
                s.piece = sem("piece")
                s.taken = sem("taken")
                s.neg_cols = sem("neg_cols")
                s.neg_rows = sem("neg_rows")
                s.copied = sem("copied")
                s.stored = [sem(f"stored{b}") for b in range(2)]
                s.own = sem("own")
                s.mturned = sem("mturned")
                s.mcopied = sem("mcopied")
                s.ready = sem("ready")

        sems = [Sems(x.name) for x in paths]
        block = ctx.enter_context(nc.Block())

        def choose(eng, run):
            if len(paths) == 1:
                run(paths[0], sems[0])
                return
            fast = eng.value_load(m.flag[0:1, 0:1], min_val=0, max_val=1)
            with eng.If(fast >= 1):
                run(paths[0], sems[0])
                eng.nop()
            with eng.Else():
                run(paths[1], sems[1])
                eng.nop()
            eng.nop()

        def heads(eng, body):
            for b in range(U):
                body(0, b)
            with eng.Fori(1, H // U - 1) as p:
                for b in range(U):
                    body(p, b)
            for b in range(U):
                body(H // U - 1, b)

        def after(p, b, n):
            p, b = p + (b + n) // U, (b + n) % U
            if isinstance(p, int) and not 0 <= p < H // U:
                return None
            return p, b

        def turn(p, b):
            return p * (U // 2) + b // 2

        @block.sync
        def _(sp):
            def run(path, s):
                def load(p, b):
                    rows = bass.ds(p * (U * DH) + b * DH, DH)
                    for g, (at, n) in enumerate(GROUPS):
                        to = slice(at * DH, (at + n) * DH)
                        sp.dma_start(q[b][to, :], d["q_parts"][layer].rearrange("(g r) c -> g r c", g=3)[0:n, rows, :]
                                     ).then_inc(s.qk_in[b], 16)
                        sp.dma_start(k[b][to, path.c0:S],
                                     d["k_parts"][layer].rearrange("(g r) c -> g r c", g=3)[g:g + 1, rows, path.c0:S]
                                     .to_broadcast([n, DH, S - path.c0])).then_inc(s.qk_in[b], 16)

                def neg(p, b):
                    sp.wait_ge(s.neg_rows, p * U + b + 1)
                    for r in range(2):
                        sp.dma_start(q[b][STACK + r:STACK + r + 1, :].rearrange("a (i c) -> a i c", c=P),
                                     neg_rows[r * NT:(r + 1) * NT, :]).then_inc(s.neg_in[b], 16)

                def store(p, b):
                    sp.wait_ge(s.copied, p * U + b + 1)
                    sp.dma_start(d["sums"][bass.ds(p * (U * P) + b * P, P), :], osb[b % 2][:]
                                 ).then_inc(s.stored[b % 2], 16)

                for b in range(2):
                    sp.sem_inc(s.stored[b], 16)
                for b in range(3):
                    load(0, b)
                neg(0, 0)

                def body(p, b):
                    if after(p, b, 3):
                        wait(sp, s.scored, (p * U + b) * path.ne)
                        load(*after(p, b, 3))
                    if after(p, b, -1):
                        store(*after(p, b, -1))
                    if after(p, b, 1):
                        neg(*after(p, b, 1))

                heads(sp, body)
                store(H // U - 1, U - 1)
                for b in range(2):
                    sp.wait_ge(s.stored[b], 16 * (H // 2 + 1))
            choose(sp, run)

        @block.gpsimd
        def _(pool):
            def run(path, s):
                for b in range(2):
                    nc.gpsimd.memset(vo[b][:, :, DH:2 * DH], 1.0).then_inc(s.ready, 1)
                pool.wait_ge(s.ready, READY)

                def body(p, b):
                    wait(pool, s.used, (p * U + b - 1) * path.ne)
                    at = bass.ds(p * (U * DH) + b * DH, DH)
                    full = [kt for kt in path.kts if kt < KT - 1]
                    nc.gpsimd.tensor_copy(vo[b % 2][:, full[0]:full[-1] + 1, 0:DH],
                                          m.v[layer][:, full[0]:full[-1] + 1, at]).then_inc(s.v_in[b % 2], 1)
                    nc.gpsimd.tensor_copy(vo[b % 2][0:KLAST, KT - 1, 0:DH],
                                          m.v[layer][0:KLAST, KT - 1, at]).then_inc(s.v_in[b % 2], 1)
                heads(pool, body)
            choose(pool, run)

        @block.scalar
        def _(act):
            def run(path, s):
                def body(p, b):
                    base = p * (U * path.ne) + b * path.ne
                    for e, (kt, half, q0) in enumerate(path.steps):
                        n = b * path.ne + e
                        act.wait_ge(s.scored, base + e + 1)
                        wait(act, s.used, base + e + 1 - path.pbufs)
                        c = q0 - half * 2 * TB
                        rows = keys_of(kt)
                        nc.scalar.activation(prob[n % path.pbufs][0:rows, c:], scores[n % 2][0:rows, c:],
                                             ACT.Exp, scale=DH ** -0.5).then_inc(s.expd, 1)
                heads(act, body)
            choose(act, run)

        @block.vector
        def _(dve):
            def run(path, s):
                link = Chain(dve, s.own)
                nc.vector.memset(part_max[:], -3.0e38).then_inc(s.ready, 1)
                for b in range(U):
                    nc.vector.memset(k[b][STACK:ROWS, :], 1.0).then_inc(s.ready, 1)
                dve.wait_ge(s.ready, READY)
                if mask is not None:
                    for i, kt in enumerate(path.kts):
                        dve.wait_ge(s.mturned, i + 1)
                        rows = keys_of(kt)
                        nc.vector.tensor_copy(mask_t[0:rows, i, :], scores[i % 2][:].bitcast(BF16)[0:rows, :]
                                              ).then_inc(s.mcopied, 1)
                LINKS = 3

                def piece(p, b, n):
                    base = p * (U * path.nm) + b * path.nm
                    ps = mx[n % MX]
                    if n < path.nm - 1:
                        i, part, c, end = path.pieces[n]
                        dve.wait_ge(s.piece, base + n + 1)
                        nc.vector.tensor_reduce(part_max[:, i, part:part + 1], ps[:, 0:end - c], AXIS.X, ALU.max
                                                ).then_inc(s.taken, 1)
                        return
                    link.at((p * U + b) * LINKS)
                    dve.wait_ge(s.taken, base + n)
                    link(nc.vector.tensor_reduce(neg_max[:], part_max[:], AXIS.X, ALU.max, negate=True))
                    link(nc.vector.tensor_copy(neg_cols[:, 0:NT], neg_max[:]))
                    link(nc.vector.tensor_tensor(neg_rest[:], neg_max[:], neg_cols[:, 0:NT], ALU.subtract))
                    nc.vector.tensor_copy(neg_cols[:, NT:2 * NT], neg_rest[:]).then_inc(s.neg_cols, 1)
                    dve.wait_ge(s.piece, base + path.nm)
                    before = after(p, b, -1)
                    if before:
                        dve.wait_ge(s.neg_in[before[1]], 32 * (before[0] + 1))
                    nc.vector.tensor_copy(neg_rows[:], ps[:].bitcast(BF16)[0:2 * NT, 0:P]).then_inc(s.taken, 1)
                    dve.wait_ge(s.taken, base + path.nm)
                    dve.sem_inc(s.neg_rows, 1)

                def copy_sums(p, b):
                    dve.wait_ge(s.used, (p * U + b + 1) * path.ne)
                    dve.wait_ge(s.stored[b % 2], 16 * (turn(p, b) + 1))
                    nc.vector.tensor_copy(osb[b % 2][:], out[:]).then_inc(s.copied, 1)

                for n in range(path.nm):
                    piece(0, 0, n)
                for n in path.early:
                    piece(0, 1, n)

                def body(p, b):
                    for e, slot in enumerate(path.slots):
                        for k_, n in slot:
                            if after(p, b, k_):
                                piece(*after(p, b, k_), n)
                        if e == 1 and after(p, b, -1):
                            copy_sums(*after(p, b, -1))
                heads(dve, body)
                copy_sums(H // U - 1, U - 1)
            choose(dve, run)

        @block.tensor
        def _(pe):
            def run(path, s):
                pe.wait_ge(s.ready, READY)
                if mask is not None:
                    for i, kt in enumerate(path.kts):
                        rows = keys_of(kt)
                        wait(pe, s.mcopied, i - 1)
                        for t in range(NT):
                            last = nc.tensor.transpose(scores[i % 2][:].bitcast(BF16)[0:rows, t * P:(t + 1) * P],
                                                       mask[:, t * S + kt * P:t * S + kt * P + rows], m.ident_bf[:])
                        last.then_inc(s.mturned, 1)
                    pe.wait_ge(s.mcopied, len(path.kts))

                def score(p, b, e):
                    kt, half, q0 = path.steps[e]
                    n = b * path.ne + e
                    base = p * (U * path.ne) + n
                    if e == 0:
                        pe.wait_ge(s.neg_in[b], 32 * (p + 1))
                    wait(pe, s.expd, base - 1)
                    rows = keys_of(kt)
                    c = q0
                    while c < (half + 1) * 2 * TB:
                        end = (c // TB + 1) * TB
                        at = c - half * 2 * TB
                        diag = path.causal and c == kt * P
                        ps = scores[n % 2]
                        last = nc.tensor.matmul(ps[0:rows, at:at + end - c], k[b][:, kt * P:kt * P + rows],
                                                q[b][:, c:end], start=True, stop=mask is None and not diag)
                        if mask is not None:
                            last = nc.tensor.matmul(ps[0:rows, at:at + end - c], m.neg_big[0:rows, 0:rows],
                                                    mask_t[0:rows, path.kts.index(kt), c:end], start=False, stop=True)
                        if diag:
                            last = nc.tensor.matmul(ps[0:rows, at:at + P], m.neg_big[0:rows, 0:rows],
                                                    m.late_key[0:rows, :], start=False, stop=True)
                        c = end
                    last.then_inc(s.scored, 1)

                def weigh(p, b, e):
                    kt, half, q0 = path.steps[e]
                    n = b * path.ne + e
                    pe.wait_ge(s.expd, p * (U * path.ne) + n + 1)
                    if e == 0:
                        pe.wait_ge(s.v_in[b % 2], 2 * (turn(p, b) + 1))
                        wait(pe, s.copied, p * U + b)
                    rows = keys_of(kt)
                    for j in (2 * half, 2 * half + 1):
                        c = max(q0, j * TB)
                        if c >= (j + 1) * TB:
                            continue
                        at = c - half * 2 * TB
                        final = kt == path.kts[-1] or (path.causal and kt == 4 * j + 3)
                        last = nc.tensor.matmul(out[32 * j:32 * j + 32, c - j * TB:TB], vo[b % 2][0:rows, kt, :],
                                                prob[n % path.pbufs][0:rows, at:at + (j + 1) * TB - c],
                                                start=kt == path.kts[0], stop=final)
                    last.then_inc(s.used, 1)

                def piece(p, b, n):
                    base = p * (U * path.nm) + b * path.nm
                    if n == 0:
                        pe.wait_ge(s.qk_in[b], (16 * NLOAD) * (p + 1))
                    prior = n - MX if n >= MX else (path.nm - 1 - n) // MX * MX + n - path.nm
                    wait(pe, s.taken, base + prior + 1)
                    ps = mx[n % MX]
                    if n == path.nm - 1:
                        pe.wait_ge(s.neg_cols, p * U + b + 1)
                        nc.tensor.transpose(ps[:].bitcast(BF16)[0:2 * NT, 0:P], neg_cols[:], m.ident_bf[:]
                                            ).then_inc(s.piece, 1)
                        return
                    i, _, c, end = path.pieces[n]
                    diag = path.causal and i < KT and end == min(S, P * (i + 1))
                    last = nc.tensor.matmul(ps[:, 0:end - c], q[b][0:STACK, i * P:(i + 1) * P], k[b][0:STACK, c:end],
                                            start=True, stop=mask is None and not diag)
                    if mask is not None:
                        last = nc.tensor.matmul(ps[:, 0:end - c], m.neg_big[:], mask[:, i * S + c:i * S + end],
                                                start=False, stop=True)
                    if diag:
                        last = nc.tensor.matmul(ps[:, i * P - c:end - c], m.neg_big[:], m.late_key_q[:, 0:end - i * P],
                                                start=False, stop=True)
                    last.then_inc(s.piece, 1)

                for n in range(path.nm):
                    piece(0, 0, n)
                for n in path.early:
                    piece(0, 1, n)

                def body(p, b):
                    for e in range(path.ne):
                        score(p, b, e)
                        if e >= 2:
                            weigh(p, b, e - 2)
                        elif after(p, b, -1):
                            weigh(*after(p, b, -1), path.ne - 2 + e)
                        for k_, n in path.slots[e]:
                            if after(p, b, k_):
                                piece(*after(p, b, k_), n)
                heads(pe, body)
                for e in (path.ne - 2, path.ne - 1):
                    weigh(H // U - 1, U - 1, e)
            choose(pe, run)


def weights_of_experts(nc, m, d):
    with ExitStack() as ctx:
        t = Tail(nc, ctx, m, d, 1, d["x2"], d["x3"])

        def sb(name, shape, dt):
            return ctx.enter_context(nc.sbuf_tensor("w_" + name, shape, dt))

        def sem(name):
            return m.semaphore(nc, "w_" + name)

        G = TT * HM
        HC = HM // DC
        wm = sb("wm", [P, DC, D], FP32)
        bm = sb("bm", [P, DC], FP32)
        emb = sb("emb", [P, HC * E2], FP32)
        rank = sb("rank", [P, G, E2], FP32)
        h = sb("h", [P, DC, TB], FP32)
        rest = sb("rest", [P, DC, TB], FP32)
        parts = sb("parts", [P, 3, DC, TB], BF16)
        l, ex, w, key, first, second_, low = (sb(n, [P, G, E2], FP32) for n in
                                              ("l", "ex", "w", "key", "first", "second", "low"))
        col = sb("col", [P, 6, G], FP32)
        wT = sb("wT", [P, TB], FP32)
        po = ctx.enter_context(nc.psum_tensor("w_po", [P, TT * D], FP32))
        pT = [ctx.enter_context(nc.psum_tensor(f"w_pT{k}", [P, TB], FP32)) for k in range(DC)]
        ph = [ctx.enter_context(nc.psum_tensor(f"w_ph{k}", [P, TB], FP32)) for k in range(DC)]
        pg = ctx.enter_context(nc.psum_tensor("w_pg", [P, G * E2], FP32))
        pw = ctx.enter_context(nc.psum_tensor("w_pw", [P, TB], FP32))
        consts, own, hid, h_ready, split_done, parts_out = (
            sem("consts"), sem("own"), sem("hid"), sem("h_ready"), sem("split_done"), sem("parts_out"))
        logits, lowered, expd, weighed, w_turned, wT_ready, wT_out = (
            sem("logits"), sem("lowered"), sem("expd"), sem("weighed"), sem("w_turned"), sem("wT_ready"), sem("wT_out"))
        top, den, best, best2, top2 = range(5)
        CONSTS = 1 + E2
        WEIGHTS = 1 + 2 + HC
        block = ctx.enter_context(nc.Block())

        @block.sync
        def _(sp):
            assert t.weights(sp) == 1
            sp.dma_start(wm[:], d["L1_ffn_Wm"].rearrange("(k p) n -> p k n", p=P)).then_inc(t.w_in, 16)
            with nc.allow_non_contiguous_dma(reason="a bias as a column"):
                sp.dma_start(bm[:], d["L1_ffn_bm"].rearrange("(k p) -> p k", p=P)).then_inc(t.w_in, 16)
            sp.wait_ge(consts, CONSTS)
            for a in range(HC):
                sp.dma_start(emb[a * HD:(a + 1) * HD, a * E2:(a + 1) * E2], d["L1_ffn_expert_emb"]).then_inc(t.w_in, 16)
            sp.sem_inc(parts_out, 16)
            sp.sem_inc(wT_out, 16)
            with sp.Fori(0, NB) as i:
                t.load(sp, i)
                t.store(sp, i)
                hold(sp, split_done, i + 1, m.passed)
                sp.dma_start(d["t_parts"][:, bass.ds(i * TB, TB)].rearrange("(q p) c -> p q c", p=P),
                             parts[:].rearrange("p g k c -> p (g k) c")).then_inc(parts_out, 16)
                hold(sp, wT_ready, i + 1, m.passed)
                sp.dma_start(d["w_t"][bass.ds(i * P, P), :], wT[:]).then_inc(wT_out, 16)
            sp.wait_ge(t.stored, 16 * (NB + 1))
            sp.wait_ge(parts_out, 16 * (NB + 1))
            sp.wait_ge(wT_out, 16 * (NB + 1))

        @block.gpsimd
        def _(pool):
            nc.gpsimd.memset(emb[:], 0.0).then_inc(consts, 1)
            for e in range(E2):
                nc.gpsimd.memset(rank[:, :, e], float(E2 - e)).then_inc(consts, 1)
            with pool.Fori(0, NB) as i:
                t.gpsimd(pool, i)

        @block.scalar
        def _(act):
            act.wait_ge(t.w_in, 16 * WEIGHTS)
            with act.Fori(0, NB) as i:
                t.scalar(act, i, pT)
                act.wait_ge(hid, i + 1)
                for k in range(DC):
                    ins = nc.scalar.activation(h[:, k, :], ph[k][:], ACT.Identity, bias=bm[:, k:k + 1])
                ins.then_inc(h_ready, 1)
                act.wait_ge(lowered, i + 1)
                nc.scalar.activation(ex[:], l[:], ACT.Exp).then_inc(expd, 1)
                act.wait_ge(w_turned, i + 1)
                act.wait_ge(wT_out, 16 * (i + 1))
                nc.scalar.copy(wT[:], pw[:]).then_inc(wT_ready, 1)

        @block.vector
        def _(dve):
            link = Chain(dve, own)
            V = nc.vector
            LINKS = t.LINKS + 19
            pgv = pg[:].rearrange("p (g e) -> p g e", e=E2)

            def wide(c):
                return col[:, c, :].unsqueeze(2).to_broadcast([P, G, E2])

            def greatest(values, at, top_at, pick):
                link(V.tensor_reduce(col[:, top_at, :], values[:], AXIS.X, ALU.max))
                link(V.tensor_tensor(key[:], values[:], wide(top_at), ALU.is_equal))
                link(V.tensor_tensor(key[:], key[:], rank[:], ALU.mult))
                link(V.tensor_reduce(col[:, at, :], key[:], AXIS.X, ALU.max))
                link(V.tensor_tensor(pick[:], key[:], wide(at), ALU.is_equal))

            dve.wait_ge(consts, CONSTS)
            with dve.Fori(0, NB) as i:
                link.at(i * LINKS)
                t.vector(dve, link, i, po)
                dve.wait_ge(h_ready, i + 1)
                dve.wait_ge(parts_out, 16 * (i + 1))
                link(V.tensor_copy(parts[:, 0], h[:]))
                link(V.tensor_tensor(rest[:], h[:], parts[:, 0], ALU.subtract))
                link(V.tensor_copy(parts[:, 1], rest[:]))
                V.tensor_tensor(parts[:, 2], rest[:], parts[:, 1], ALU.subtract).then_inc(split_done, 1)
                dve.wait_ge(logits, i + 1)
                link(V.tensor_reduce(col[:, top, :], pgv, AXIS.X, ALU.max))
                V.tensor_tensor(l[:], pgv, wide(top), ALU.subtract).then_inc(lowered, 1)
                dve.wait_ge(expd, i + 1)
                link(V.tensor_reduce(col[:, den, :], ex[:], AXIS.X, ALU.add))
                link(V.reciprocal(col[:, den, :], col[:, den, :]))
                link(V.tensor_tensor(w[:], ex[:], wide(den), ALU.mult))
                greatest(w, best, top, first)
                link(V.scalar_tensor_tensor(out=low[:], in0=first[:], scalar=-2.0, in1=w[:], op0=ALU.mult, op1=ALU.add))
                greatest(low, best2, top2, second_)
                link(V.tensor_tensor(first[:], first[:], second_[:], ALU.add))
                V.tensor_tensor(w[:], w[:], first[:], ALU.mult).then_inc(weighed, 1)
                dve.wait_ge(w_turned, i + 1)
            assert link.n == LINKS, link.n

        @block.tensor
        def _(pe):
            pe.wait_ge(t.w_in, 16 * WEIGHTS)
            with pe.Fori(0, NB) as i:
                t.tensor(pe, i, po, pT)
                for k in range(DC):
                    for c in range(DC):
                        last = nc.tensor.matmul(ph[k][:], wm[:, c, k * P:(k + 1) * P], t.xT[:, c, :],
                                                start=c == 0, stop=c == DC - 1)
                last.then_inc(hid, 1)
                pe.wait_ge(h_ready, i + 1)
                for j in range(TT):
                    for c in range(DC):
                        at = (j * HM + c * HC) * E2
                        last = nc.tensor.matmul(pg[:, at:at + HC * E2], h[:, c, j * P:(j + 1) * P], emb[:],
                                                start=True, stop=True)
                last.then_inc(logits, 1)
                pe.wait_ge(weighed, i + 1)
                for j in range(TT):
                    last = nc.tensor.transpose(pw[:, j * P:(j + 1) * P],
                                               w[:, j * HM:(j + 1) * HM, :].rearrange("p h e -> p (h e)"), m.ident[:])
                last.then_inc(w_turned, 1)


def head_experts(nc, m, d):
    with ExitStack() as ctx:
        def sb(name, shape, dt):
            return ctx.enter_context(nc.sbuf_tensor("x_" + name, shape, dt))

        def sem(name):
            return m.semaphore(nc, "x_" + name)

        HC = HM // DC
        K3 = 3 * HD
        HB = 4
        w1f = sb("w1f", [K3, E2, F2], FP32)
        w1r = sb("w1r", [K3, E2, F2], FP32)
        w1m = sb("w1m", [K3, E2, F2], BF16)
        w1 = [sb(f"w1{n}", [K3, E2, F2], BF16) for n in range(2)]
        b1 = sb("b1", [F2, E2], FP32)
        w2 = sb("w2", [F2, E2, HD], FP32)
        b2 = sb("b2", [P, E2], FP32)
        wo = sb("wo", [P, DC, D], FP32)
        bo = sb("bo", [1, D], FP32)
        xt = [[sb(f"xt{c}{n}", [K3, HC, TB], BF16) for n in range(2)] for c in range(DC)]
        wb = [sb(f"wb{c}", [P, E2, TB], FP32) for c in range(DC)]
        hm = [sb(f"hm{n}", [F2, 2 * TB], FP32) for n in range(HB)]
        weighed_ = [sb(f"we{n}", [P, TB], FP32) for n in range(2)]
        acc = [sb(f"acc{c}", [P, TB], FP32) for c in range(DC)]
        x = sb("x", [P, TT, D], FP32)
        y = sb("y", [P, TT, D], FP32)
        pu = [ctx.enter_context(nc.psum_tensor(f"x_pu{n}", [F2, 2 * TB], FP32)) for n in range(2)]
        pe_ = [ctx.enter_context(nc.psum_tensor(f"x_pe{n}", [P, TB], FP32)) for n in range(2)]
        po = ctx.enter_context(nc.psum_tensor("x_po", [P, TT * D], FP32))
        w_in, w1_ready, own = sem("w_in"), sem("w1_ready"), sem("own")
        t_in = [sem(f"t_in{c}") for c in range(DC)]
        up, active, down, taken, summed = sem("up"), sem("active"), sem("down"), sem("taken"), sem("summed")
        projected, x_in, x_free, added, out_done = (
            sem("projected"), sem("x_in"), sem("x_free"), sem("added"), sem("out_done"))
        LOADS = 6 + HC
        N = E2 * 2
        WEIGHTS = 3 + 1 + 1 + HC + 2
        block = ctx.enter_context(nc.Block())

        def blocks(eng, body):
            body(0, True)
            with eng.Fori(1, NB) as i:
                body(i, False)

        @block.sync
        def _(sp):
            for n in range(3):
                sp.dma_start(w1f[n * HD:(n + 1) * HD, :, :], d["L1_ffn_W1"].rearrange("e k f -> k e f")).then_inc(w_in, 16)
            with nc.allow_non_contiguous_dma(reason="biases as columns"):
                sp.dma_start(b1[:], d["L1_ffn_b1"].rearrange("e f -> f e")).then_inc(w_in, 16)
                for a in range(HC):
                    sp.dma_start(b2[a * HD:(a + 1) * HD, :], d["L1_ffn_b2"].rearrange("e f -> f e")).then_inc(w_in, 16)
            sp.dma_start(w2[:], d["L1_ffn_W2"].rearrange("e f o -> f e o")).then_inc(w_in, 16)
            sp.dma_start(wo[:], d["L1_ffn_Wo"].rearrange("(k p) n -> p k n", p=P)).then_inc(w_in, 16)
            sp.dma_start(bo[:], d["L1_ffn_bo"].rearrange("(a n) -> a n", a=1)).then_inc(w_in, 16)
            sp.sem_inc(x_free, 1)
            sp.sem_inc(out_done, 16)

            def body(i, first):
                for c in range(DC):
                    if not first:
                        hold(sp, summed, (i - 1) * DC + c + 1, m.passed)
                    for n, parts in enumerate(((0, 1, 2), (0, 1, 0))):
                        for r, g in enumerate(parts):
                            src = d["t_parts"][g * D + c * P:g * D + (c + 1) * P, bass.ds(i * TB, TB)]
                            sp.dma_start(xt[c][n][r * HD:(r + 1) * HD, :, :], src.rearrange("(a r) c -> r a c", a=HC)
                                         ).then_inc(t_in[c], 16)
                    for a in range(HC):
                        rows = bass.ds(i * P + (c * HC + a) * E2, E2)
                        src = d["w_t"][rows, :].rearrange("(o e) c -> o (e c)", o=1).to_broadcast([HD, E2 * TB])
                        sp.dma_start(wb[c][a * HD:(a + 1) * HD, :, :].rearrange("p e c -> p (e c)"), src
                                     ).then_inc(t_in[c], 16)
                hold(sp, x_free, i + 1, m.passed)
                sp.dma_start(x[:], d["x3"][bass.ds(i * TB, TB), :].rearrange("(j p) d -> p j d", p=P)).then_inc(x_in, 16)
                if not first:
                    store(i - 1)

            def store(i):
                hold(sp, added, i + 1, m.passed)
                sp.dma_start(d["out_rows"][bass.ds(i * TB, TB), :].rearrange("(j p) d -> p j d", p=P), y[:]
                             ).then_inc(out_done, 16)
            blocks(sp, body)
            store(NB - 1)
            sp.wait_ge(out_done, 16 * (NB + 1))

        @block.gpsimd
        def _(pool):
            pool.nop()

        @block.scalar
        def _(act):
            act.wait_ge(w_in, 16 * WEIGHTS)

            def body(i, first):
                for c in range(DC):
                    for n in range(N):
                        base = i * (DC * N) + (c * N + n)
                        act.wait_ge(up, base + 1)
                        if not (first and c * N + n < HB):
                            act.wait_ge(down, base + 1 - HB)
                        nc.scalar.activation(hm[n % HB][:], pu[n % 2][:], ACT.Gelu, bias=b1[:, n // 2:n // 2 + 1]
                                             ).then_inc(active, 1)
            blocks(act, body)

        @block.vector
        def _(dve):
            link = Chain(dve, own)
            V = nc.vector
            dve.wait_ge(w_in, 16 * WEIGHTS)
            link(V.tensor_copy(w1[0][:], w1f[:]))
            link(V.tensor_tensor(w1r[:], w1f[:], w1[0][:], ALU.subtract))
            link(V.tensor_copy(w1m[:], w1r[:]))
            V.tensor_copy(w1[1][0:2 * HD], w1m[0:2 * HD]).then_inc(w1_ready, 1)
            V.tensor_tensor(w1[1][2 * HD:K3], w1r[2 * HD:K3], w1m[2 * HD:K3], ALU.subtract).then_inc(w1_ready, 1)
            START = link.n
            CH = 2 * E2 - 1

            def result(i):
                dve.wait_ge(projected, i + 1)
                dve.wait_ge(x_in, 16 * (i + 1))
                dve.wait_ge(out_done, 16 * (i + 1))
                V.tensor_tensor(y[:].rearrange("p j d -> p (j d)"), x[:].rearrange("p j d -> p (j d)"), po[:], ALU.add
                                ).then_inc(added, 1)
                dve.wait_ge(added, i + 1)
                dve.sem_inc(x_free, 1)

            def body(i, first):
                for c in range(DC):
                    link.at(i * (DC * CH) + (START + c * CH))
                    if c == 1 and not first:
                        result(i - 1)
                    for e in range(E2):
                        dve.wait_ge(down, i * (DC * N) + (c * N + 2 * e + 2))
                        if e == 0:
                            dve.wait_ge(t_in[c], (i + 1) * (16 * LOADS))
                            if not first:
                                dve.wait_ge(projected, i)
                        to = weighed_[e % 2] if e else acc[c]
                        ins = V.scalar_tensor_tensor(out=to[:], in0=pe_[e % 2][:], scalar=b2[:, e:e + 1],
                                                     in1=wb[c][:, e, :], op0=ALU.add, op1=ALU.mult)
                        link(ins)
                        dve.sem_inc(taken, 1)
                        if e:
                            link(V.tensor_tensor(acc[c][:], acc[c][:], to[:], ALU.add))
                    dve.sem_inc(summed, 1)
            blocks(dve, body)
            result(NB - 1)

        @block.tensor
        def _(pe):
            pe.wait_ge(w1_ready, 2)

            def project(i):
                pe.wait_ge(summed, (i + 1) * DC)
                if not isinstance(i, int) or i > 0:
                    pe.wait_ge(added, i)
                for j in range(TT):
                    to = po[:, j * D:(j + 1) * D]
                    for c in range(DC):
                        nc.tensor.matmul(to, acc[c][:, j * P:(j + 1) * P], wo[:, c, :], start=c == 0, stop=False)
                    last = nc.tensor.matmul(to, m.ones[0:1, :], bo[:], start=False, stop=True)
                last.then_inc(projected, 1)

            def lower(i, c, n):
                base = i * (DC * N) + (c * N + n)
                pe.wait_ge(active, base + 1)
                e, pair = n // 2, n % 2
                if pair == 0 and not (isinstance(i, int) and i == 0 and c == 0 and e < 2):
                    pe.wait_ge(taken, i * (DC * E2) + (c * E2 + e - 1))
                for a in range(2):
                    g = 2 * pair + a
                    last = nc.tensor.matmul(pe_[e % 2][g * HD:(g + 1) * HD, :], w2[:, e, :],
                                            hm[n % HB][:, a * TB:(a + 1) * TB], start=True, stop=True)
                last.then_inc(down, 1)

            def body(i, first):
                for c in range(DC):
                    for n in range(N):
                        base = i * (DC * N) + (c * N + n)
                        if n == 0:
                            pe.wait_ge(t_in[c], (i + 1) * (16 * LOADS))
                        if not (first and c == 0 and n < 2):
                            pe.wait_ge(active, base - 1)
                        e, pair = n // 2, n % 2
                        for a in range(2):
                            for s in range(2):
                                last = nc.tensor.matmul(pu[n % 2][:, a * TB:(a + 1) * TB], w1[s][:, e, :],
                                                        xt[c][s][:, 2 * pair + a, :], start=s == 0, stop=s == 1)
                        last.then_inc(up, 1)
                        if n >= 2:
                            lower(i, c, n - 2)
                        elif c:
                            lower(i, c - 1, N - 2 + n)
                        elif not first:
                            lower(i - 1, DC - 1, N - 2 + n)
                        if n == 3 and c == 0 and not first:
                            project(i - 1)
            blocks(pe, body)
            for n in (N - 2, N - 1):
                lower(NB - 1, DC - 1, n)
            project(NB - 1)


def second(nc, m, d):
    weights_of_experts(nc, m, d)
    if UPTO == 3:
        return finish_debug(nc, d, "x3")
    head_experts(nc, m, d)


_SCRATCH = (("q_parts0", (3 * D, T), BF16), ("q_parts1", (3 * D, T), BF16), ("k_parts0", (3 * D, S), BF16),
            ("k_parts1", (3 * D, S), BF16), ("sums", (H * P, TB), FP32), ("x1", (T, D), FP32), ("x2", (T, D), FP32),
            ("x3", (T, D), FP32), ("t_parts", (3 * D, T), BF16), ("w_t", (NB * HM * E2, TB), FP32), ("slots_in", (T, D), FP32), ("slots_out", (T, D), FP32))
UPTO = None


def program(nc, d, out):
    d = dict(d)
    for name, shape, dt in _SCRATCH:
        d[name] = nc.dram_tensor(name, shape, dt, kind="Internal").ap()
    for n in ("q_parts", "k_parts"):
        d[n] = [d[n + "0"], d[n + "1"]]
    d["x_rows"] = d["x"].rearrange("a t d -> (a t) d")
    d["out_rows"] = out.rearrange("a t d -> (a t) d")
    fast = Path("f", list(range(FAST_FROM, KT)), False, 4)
    full = Path("a", list(range(KT)), False, 4)
    causal = Path("c", list(range(KT)), True, 4)
    with ExitStack() as ctx:
        m = place_shared(nc, ctx)
        with nc.sbuf_tensor("mask", [P, NT * S], BF16) as mask:
            prepare(nc, m, d, mask)
            attend(nc, m, d, 0, [fast, full], mask)
        m.clear_semaphores(nc)
        router(nc, m, d)
        if UPTO == 1:
            return finish_debug(nc, d, "x1")
        experts(nc, m, d)
        gather(nc, m, d)
        if UPTO == 2:
            return finish_debug(nc, d, "x2")
        m.clear_semaphores(nc)
        attend(nc, m, d, 1, [causal])
        second(nc, m, d)


def finish_debug(nc, d, name):
    with nc.semaphore("dbg") as sem, nc.Block() as block:
        @block.sync
        def _(sp):
            sp.dma_start(d["out_rows"], d[name]).then_inc(sem, 16)
            sp.wait_ge(sem, 16)


_INS = ['x', 'ctx_1024', 'mask_Bx1xSxS2_bk1'] + [
    f'L{l}_xattn_{n}' for l in range(2) for n in ('Wq', 'bq', 'Wk', 'bk', 'Wv', 'bv', 'Wo', 'bo')] + [
    f'L0_ffn_{n}' for n in ('Wr', 'br', 'W1', 'b1', 'W2', 'b2')] + [
    f'L1_ffn_{n}' for n in ('Wm', 'bm', 'expert_emb', 'W1', 'b1', 'W2', 'b2', 'Wo', 'bo')]


def kernel(**inputs):
    import numpy as np
    import concourse.bacc as bacc
    from concourse.bass_utils import run_bass_kernel_spmd

    nc = bacc.Bacc("TRN2", target_bir_lowering=False, num_devices=1)
    arrays, d = {}, {}
    for name in _INS:
        a = np.ascontiguousarray(inputs[name])
        arrays["in_" + name] = a
        d[name] = nc.dram_tensor("in_" + name, a.shape, mybir.dt.from_np(a.dtype), kind="ExternalInput").ap()
    d["mask"] = d["mask_Bx1xSxS2_bk1"]
    out = nc.dram_tensor("out_0", (1, T, D), FP32, kind="ExternalOutput").ap()
    program(nc, d, out)
    return run_bass_kernel_spmd(nc, [arrays], core_ids=[0]).results[0]["out_0"]
```

```python
import concourse.bass as bass
from concourse import mybir
from contextlib import ExitStack

FP32 = mybir.dt.float32
BF16 = mybir.dt.bfloat16
U8 = mybir.dt.uint8
I32 = mybir.dt.int32
U32 = mybir.dt.uint32
ALU = mybir.AluOpType
ACT = mybir.ActivationFunctionType
AXIS = mybir.AxisListType

P = 128
T = 2048
D = 256
DC = D // P
S = 1601
H = 16
DH = D // H
TB = 512
NB = T // TB
TT = TB // P
NT = T // P
KT = -(-S // P)
KLAST = S - P * (KT - 1)
SFULL = S // TB
STACK = 6 * DH
ROWS = STACK + 3
GROUPS = ((0, 3), (3, 2), (5, 1))
BIG = 2.0 ** 100
EPS = 1e-5
E1 = 8
CAP = T // E1
HM, E2, HD, F2 = 8, 16, 32, 128
MX = 3
U = 4
FAST_FROM = 9
CF = FAST_FROM * P


def keys_of(kt):
    return KLAST if kt == KT - 1 else P


def hold(eng, sem, value, passed):
    eng.wait_ge(sem, value)
    eng.sem_inc(passed, 1)


class Chain:

    def __init__(self, eng, sem):
        self.eng, self.sem, self.base, self.n = eng, sem, 0, 0

    def at(self, base):
        self.base, self.n = base, 0

    def __call__(self, ins):
        self.n += 1
        ins.then_inc(self.sem, 1)
        self.eng.wait_ge(self.sem, self.base + self.n)

    def mark(self, ins):
        self.n += 1
        ins.then_inc(self.sem, 1)
        return self.n

    def wait(self, n):
        self.eng.wait_ge(self.sem, self.base + n)


class Shared:

    def __init__(self):
        self.semaphores = []

    def semaphore(self, nc, name):
        self.semaphores.append(nc.alloc_semaphore(name))
        return self.semaphores[-1]

    def clear_semaphores(self, nc):
        nc.clear_and_free_semaphores(self.semaphores)
        nc.all_engine_barrier()
        self.semaphores = []


def place_shared(nc, ctx):
    m = Shared()

    def sb(name, shape, dt):
        return ctx.enter_context(nc.sbuf_tensor(name, shape, dt))

    m.ident = sb("ident", [P, P], FP32)
    m.ident_bf = sb("ident_bf", [P, P], BF16)
    m.neg_big = sb("neg_big", [P, P], BF16)
    m.late_key = sb("late_key", [P, P], BF16)
    m.late_key_q = sb("late_key_q", [P, P], BF16)
    m.upto = sb("upto", [P, P], FP32)
    m.ones = sb("ones", [P, P], FP32)
    m.minus_half = sb("minus_half", [P, 2 * TT], FP32)
    m.v = [sb(f"v{l}", [P, KT, D], FP32) for l in range(2)]
    m.slots = sb("slots", [P, NT], U32)
    m.gates = sb("gates", [P, NT], FP32)
    m.wq1 = sb("wq1", [P, DC, D], FP32)
    m.wo1 = sb("wo1", [P, DC, D], FP32)
    m.passed = nc.alloc_semaphore("passed")
    m.flag = sb("flag", [P, 1], I32)
    m.mask_row = sb("mask_row", [P, S - CF], BF16)
    return m


def make_constants(nc, pool, m, made):
    link = Chain(pool, made)
    link(nc.gpsimd.memset(m.ones[:], 1.0))
    link(nc.gpsimd.memset(m.minus_half[:], -0.5))
    for buf, op, base, step, up, fill in (
        (m.ident, ALU.not_equal, 0, -1, 1, 1.0),
        (m.ident_bf, ALU.not_equal, 0, -1, 1, 1.0),
        (m.neg_big, ALU.not_equal, 0, -1, 1, -BIG),
        (m.late_key, ALU.is_ge, 0, 1, -1, 1.0),
        (m.late_key_q, ALU.is_ge, 0, -1, 1, 1.0),
        (m.upto, ALU.is_gt, 0, -1, 1, 1.0),
    ):
        link(nc.gpsimd.memset(buf[:], 0.0))
        link(nc.gpsimd.affine_select(out=buf[:], in_=buf[:], compare_op=op, fill=fill, base=base,
                                     pattern=[[step, P]], channel_multiplier=up))
    return link.n


def normalize(nc, m, dve, link, xb, xn, stats, mv, rstd, stats_ready, rstd_ready, at):
    for j in range(TT):
        ins = nc.vector.bn_stats(stats[:, j, :], xb[:, j, :])
        if j == TT - 1:
            link(ins)
            dve.sem_inc(m.passed, 1)
    for j in range(TT):
        ins = nc.vector.bn_aggr(mv[:, j, :], stats[:, j, :])
    ins.then_inc(stats_ready, 1)
    dve.wait_ge(rstd_ready, at + 1)
    for j in range(TT):
        ins = nc.vector.tensor_scalar(xn[:, j, :], xb[:, j, :], mv[:, j, 0:1], rstd[:, j:j + 1],
                                      ALU.subtract, ALU.mult)
    return ins


def root(nc, pool, m, mv, ve, rstd, stats_ready, ve_ready, rstd_ready, at):
    hold(pool, stats_ready, at + 1, m.passed)
    nc.gpsimd.tensor_scalar(ve[:], mv[:, :, 1], EPS, None, ALU.add).then_inc(ve_ready, 1)
    pool.wait_ge(ve_ready, at + 1)
    nc.gpsimd.tensor_tensor(rstd[:], ve[:], m.minus_half[:, 0:mv.shape[1]], ALU.pow).then_inc(rstd_ready, 1)


def prepare(nc, m, d, mask):
    with ExitStack() as ctx:
        def sb(name, shape, dt):
            return ctx.enter_context(nc.sbuf_tensor("a_" + name, shape, dt))

        def sem(name):
            return m.semaphore(nc, "a_" + name)

        Q, K0, K1 = range(3)
        w = {n: sb(n, [P, DC, D], FP32) for n in ("wq0", "wk0", "wv0", "wk1", "wv1")}
        weight = [w["wq0"], w["wk0"], w["wk1"]]
        wraw = sb("wraw", [P, DC, 4, D], FP32)
        brow = sb("brow", [1, 2, D], FP32)
        bcol = sb("bcol", [P, 3, DC], FP32)
        xb = sb("xb", [P, TT, D], FP32)
        cb = sb("cb", [P, TT, D], FP32)
        xn = sb("xn", [P, TT, D], FP32)
        xT = sb("xT", [P, DC, TB], FP32)
        cT = sb("cT", [P, DC, TB], FP32)
        kf = [sb(f"kf{s}", [P, DC, TB], FP32) for s in range(3)]
        rest = sb("rest", [P, DC, TB], FP32)
        parts = [sb(f"parts{s}", [P, 3, DC, TB], BF16) for s in range(3)]
        stats = sb("stats", [P, TT, 6], FP32)
        mv = sb("mv", [P, TT, 2], FP32)
        ve = sb("ve", [P, TT], FP32)
        rstd = sb("rstd", [P, TT], FP32)
        mraw = sb("mraw", [P, NT, S], U8)
        ones_bf = sb("ones_bf", [P, P], BF16)
        some = sb("some", [P, S - CF], FP32)
        all_ = sb("all", [P, S - CF], FP32)
        sign = sb("sign", [P, 5], FP32)
        pX = ctx.enter_context(nc.psum_tensor("a_pX", [P, DC, TB], FP32))
        pC = ctx.enter_context(nc.psum_tensor("a_pC", [P, DC, TB], FP32))
        pKK = ctx.enter_context(nc.psum_tensor("a_pK", [P, 2, DC, TB], FP32))
        pK = [pKK[:, l] for l in range(2)]
        pP = [pX, pK[0], pK[1]]
        counts = pKK[:].rearrange("p l k c -> p (l k c)")

        made, raw_in, w_in, wT, wT_sb = sem("made"), sem("raw_in"), sem("w_in"), sem("wT"), sem("wT_sb")
        x_in, x_free, c_in, c_free = sem("x_in"), sem("x_free"), sem("c_in"), sem("c_free")
        stats_ready, ve_ready, rstd_ready, xn_ready = sem("stats"), sem("ve"), sem("rstd"), sem("xn_ready")
        x_turned, xT_ready, c_turned, cT_ready = sem("x_turned"), sem("xT_ready"), sem("c_turned"), sem("cT_ready")
        proj, kf_ready, kf_free, split_done, parts_out = (
            [sem(f"{n}{s}") for s in range(3)] for n in ("proj", "kf_ready", "kf_free", "split_done", "parts_out"))
        v_done, v_copied, q_read = sem("v_done"), sem("v_copied"), sem("q_read")
        m_in, m_cast = sem("m_in"), sem("m_cast")
        counted, dve_own = sem("counted"), sem("dve_own")
        CONSTS = 15

        block = ctx.enter_context(nc.Block())

        def turns(eng, body):
            assert NB == SFULL + 1 and KT == SFULL * TT + 1
            with eng.Fori(0, SFULL) as i:
                body(i, TT, P)
            body(SFULL, 1, KLAST)

        @block.sync
        def _(sp):
            view = "(k p) n -> p k n"
            x_rows = d["x"].rearrange("a t d -> (a t) d")
            c_rows = d["ctx_1024"].rearrange("a t d -> (a t) d")

            def load(i, last):
                sp.wait_ge(x_free, i + 1)
                sp.dma_start(xb[:], x_rows[bass.ds(i * TB, TB), :].rearrange("(j p) d -> p j d", p=P)
                             ).then_inc(x_in, 16)
                sp.wait_ge(c_free, i + 1)
                if last:
                    sp.dma_start(cb[0:KLAST, 0, :], c_rows[SFULL * TB:S, :]).then_inc(c_in, 16)
                else:
                    sp.dma_start(cb[:], c_rows[bass.ds(i * TB, TB), :].rearrange("(j p) d -> p j d", p=P)
                                 ).then_inc(c_in, 16)

            def store(i, cols):
                for s, to in ((K0, d["k_parts"][0]), (K1, d["k_parts"][1]), (Q, d["q_parts"][0])):
                    n = TB if s == Q else cols
                    hold(sp, split_done[s], i + 1, m.passed)
                    sp.dma_start(to[:, bass.ds(i * TB, n)].rearrange("(q p) c -> p q c", p=P),
                                 parts[s][:, :, :, 0:n].rearrange("p g k c -> p (g k) c")).then_inc(parts_out[s], 16)

            sp.sem_inc(x_free, 1)
            sp.sem_inc(c_free, 1)
            for s in range(3):
                sp.sem_inc(parts_out[s], 16)
            load(0, False)
            for i, name in enumerate(("Wq", "Wk", "Wv", "Wo")):
                sp.dma_start(wraw[:, :, i, :], d["L1_xattn_" + name].rearrange(view, p=P)).then_inc(raw_in, 16)
            for name, src in (("wq0", d["L0_xattn_Wq"]), ("wk0", d["L0_xattn_Wk"]), ("wv0", d["L0_xattn_Wv"])):
                sp.dma_start(w[name][:], src.rearrange(view, p=P)).then_inc(w_in, 16)
            for l in range(2):
                sp.dma_start(brow[0:1, l, :], d[f"L{l}_xattn_bv"].rearrange("(a n) -> a n", a=1)).then_inc(w_in, 16)
            with nc.allow_non_contiguous_dma(reason="a bias as a column"):
                for i, name in enumerate(("L0_xattn_bq", "L0_xattn_bk", "L1_xattn_bk")):
                    sp.dma_start(bcol[:, i, :], d[name].rearrange("(k p) -> p k", p=P)).then_inc(w_in, 16)
            with sp.Fori(0, SFULL - 1) as i:
                load(i + 1, False)
                store(i, TB)
            load(SFULL, True)
            store(SFULL - 1, TB)
            store(SFULL, KLAST)
            for s in range(3):
                sp.wait_ge(parts_out[s], 16 * (NB + 1))

        @block.gpsimd
        def _(pool):
            n = make_constants(nc, pool, m, made)
            assert n + 1 == CONSTS
            nc.gpsimd.memset(ones_bf[:], 1.0).then_inc(made, 1)
            m_rows = d["mask"].rearrange("a b t s -> (a b t) s")

            def body(i, tiles, rows):
                pool.dma_start(mraw[:, bass.ds(i * TT, TT), :],
                               m_rows[bass.ds(i * TB, TB), :].rearrange("(j p) s -> p j s", p=P)).then_inc(m_in, 16)
                root(nc, pool, m, mv, ve, rstd, stats_ready, ve_ready, rstd_ready, i)
                hold(pool, m_in, 16 * (i + 1), m.passed)
            turns(pool, body)

        @block.scalar
        def _(act):
            def evac(i, s, cols):
                act.wait_ge(proj[s], i + 1)
                act.wait_ge(kf_free[s], i + 1)
                for k in range(DC):
                    ins = nc.scalar.activation(kf[s][:, k, 0:cols], pP[s][:, k, 0:cols], ACT.Identity,
                                               bias=bcol[:, s, k:k + 1])
                ins.then_inc(kf_ready[s], 1)
                if s == Q:
                    act.wait_ge(kf_ready[s], i + 1)
                    act.sem_inc(q_read, 1)

            def copy_v(i, l, tiles, rows):
                act.wait_ge(v_done, i * 2 + (l + 1))
                v = pC[:].rearrange("p k (j d) -> p (k j) d", d=D)
                half = -(-tiles // 2)
                for j in range(0, tiles, half):
                    ins = nc.scalar.copy(m.v[l][0:rows, bass.ds(i * TT + j, half), :], v[0:rows, j:j + half, :])
                ins.then_inc(v_copied, 1)

            def cast(i, first):
                act.wait_ge(m_in, 16 * (i + 1))
                for j in (first, first + 1):
                    nc.scalar.copy(mask[:, bass.ds(i * (TT * S) + j * S, S)],
                                   mraw[:, bass.ds(i * TT + j, 1), :].rearrange("p j s -> p (j s)")).then_inc(m_cast, 1)

            for i in range(4):
                act.wait_ge(wT, i + 1)
                dst = (m.wq1, w["wk1"], w["wv1"], m.wo1)[i]
                nc.scalar.copy(dst[:], pK[i % 2][:, :, 0:D]).then_inc(wT_sb, 1)
            act.wait_ge(w_in, 16 * 8)

            def body(i, tiles, rows):
                cols = tiles * P if tiles > 1 else rows
                act.wait_ge(c_turned, i + 1)
                nc.scalar.copy(cT[:, :, 0:cols], pC[:, :, 0:cols]).then_inc(cT_ready, 1)
                act.wait_ge(x_turned, i + 1)
                nc.scalar.copy(xT[:], pX[:]).then_inc(xT_ready, 1)
                evac(i, K0, cols)
                cast(i, 0)
                copy_v(i, 0, tiles, rows)
                evac(i, K1, cols)
                evac(i, Q, TB)
                copy_v(i, 1, tiles, rows)
                cast(i, 2)
            turns(act, body)
            act.wait_ge(m_cast, NT)

        @block.vector
        def _(dve):
            link = Chain(dve, dve_own)
            for s in range(3):
                dve.sem_inc(kf_free[s], 1)
            LINKS = 1 + 3 * 3

            def cut(i, s, cols):
                dve.wait_ge(kf_ready[s], i + 1)
                dve.wait_ge(parts_out[s], 16 * (i + 1))
                link(nc.vector.tensor_copy(parts[s][:, 0, :, 0:cols], kf[s][:, :, 0:cols]))
                link(nc.vector.tensor_tensor(rest[:, :, 0:cols], kf[s][:, :, 0:cols], parts[s][:, 0, :, 0:cols],
                                             ALU.subtract))
                dve.sem_inc(kf_free[s], 1)
                link(nc.vector.tensor_copy(parts[s][:, 1, :, 0:cols], rest[:, :, 0:cols]))
                nc.vector.tensor_tensor(parts[s][:, 2, :, 0:cols], rest[:, :, 0:cols], parts[s][:, 1, :, 0:cols],
                                        ALU.subtract).then_inc(split_done[s], 1)

            def body(i, tiles, rows):
                cols = tiles * P if tiles > 1 else rows
                link.at(i * LINKS)
                dve.wait_ge(x_in, 16 * (i + 1))
                normalize(nc, m, dve, link, xb, xn, stats, mv, rstd, stats_ready, rstd_ready, i
                          ).then_inc(xn_ready, 1)
                dve.wait_ge(xn_ready, i + 1)
                dve.sem_inc(x_free, 1)
                cut(i, K0, cols)
                cut(i, K1, cols)
                cut(i, Q, TB)
            turns(dve, body)
            dve.wait_ge(split_done[Q], NB)
            dve.wait_ge(counted, 1)
            link.at(NB * LINKS)
            V = nc.vector
            V.tensor_reduce(sign[:, 0:1], counts[:, 0:CF], AXIS.X, ALU.min)
            V.tensor_reduce(sign[:, 1:2], counts[:, CF:S], AXIS.X, ALU.min)
            V.tensor_scalar(some[:], counts[:, CF:S], 0.5, None, ALU.is_gt)
            link(V.tensor_scalar(all_[:], counts[:, CF:S], float(T), None, ALU.is_ge))
            V.tensor_scalar(m.mask_row[:], some[:], -BIG, None, ALU.mult)
            link(V.tensor_tensor(all_[:], some[:], all_[:], ALU.subtract))
            link(V.tensor_reduce(sign[:, 2:3], all_[:], AXIS.X, ALU.max))
            link(V.tensor_tensor(sign[:, 3:4], sign[:, 0:1], sign[:, 1:2], ALU.subtract))
            link(V.tensor_tensor(sign[:, 4:5], sign[:, 3:4], sign[:, 2:3], ALU.subtract))
            link(V.tensor_scalar(m.flag[:], sign[:, 4:5], float(T), None, ALU.is_equal))

        @block.tensor
        def _(pe):
            pe.wait_ge(made, CONSTS)
            pe.wait_ge(raw_in, 16 * 4)
            for i in range(4):
                if i >= 2:
                    pe.wait_ge(wT_sb, i - 1)
                for k in range(DC):
                    for j in range(DC):
                        last = nc.tensor.transpose(pK[i % 2][:, k, j * P:j * P + P], wraw[:, j, i, k * P:k * P + P],
                                                   m.ident[:])
                last.then_inc(wT, 1)
            pe.wait_ge(wT_sb, 4)
            pe.wait_ge(w_in, 16 * 8)
            pe.sem_inc(v_copied, 1)
            pe.sem_inc(q_read, 1)

            def turn(to, src, tiles, rows):
                for k in range(DC):
                    for j in range(tiles):
                        last = nc.tensor.transpose(to[:, k, j * P:j * P + rows], src[0:rows, j, k * P:k * P + P],
                                                   m.ident[0:rows, 0:rows])
                return last

            def project(s, src, cols):
                for k in range(DC):
                    for c in range(DC):
                        last = nc.tensor.matmul(pP[s][:, k, 0:cols], weight[s][:, c, k * P:k * P + P],
                                                src[:, c, 0:cols], start=c == 0, stop=c == DC - 1)
                last.then_inc(proj[s], 1)

            def values(l, tiles, rows):
                for j in range(tiles):
                    to = pC[0:rows, j // 2, (j % 2) * D:(j % 2 + 1) * D]
                    for c in range(DC):
                        nc.tensor.matmul(to, cT[:, c, j * P:j * P + rows], w[f"wv{l}"][:, c, :],
                                         start=c == 0, stop=False)
                    last = nc.tensor.matmul(to, m.ones[0:1, 0:rows], brow[0:1, l, :], start=False, stop=True)
                last.then_inc(v_done, 1)

            def body(i, tiles, rows):
                cols = tiles * P if tiles > 1 else rows
                pe.wait_ge(c_in, 16 * (i + 1))
                pe.wait_ge(v_copied, i * 2 + 1)
                turn(pC, cb, tiles, rows).then_inc(c_turned, 1)
                pe.wait_ge(xn_ready, i + 1)
                pe.wait_ge(q_read, i + 1)
                turn(pX, xn, TT, P).then_inc(x_turned, 1)
                pe.wait_ge(c_turned, i + 1)
                pe.sem_inc(c_free, 1)
                pe.wait_ge(cT_ready, i + 1)
                project(K0, cT, cols)
                values(0, tiles, rows)
                pe.wait_ge(xT_ready, i + 1)
                project(K1, cT, cols)
                project(Q, xT, TB)
                pe.wait_ge(v_copied, i * 2 + 2)
                values(1, tiles, rows)
            turns(pe, body)
            for s in (K0, K1):
                pe.wait_ge(kf_ready[s], NB)
            for t in range(NT):
                pe.wait_ge(m_cast, t + 1)
                for c in range(0, S, TB):
                    end = min(c + TB, S)
                    last = nc.tensor.matmul(counts[:, c:end], ones_bf[:], mask[:, t * S + c:t * S + end],
                                            start=t == 0, stop=t == NT - 1)
            last.then_inc(counted, 1)


class PairNorm:

    LINKS = 2

    def __init__(t, nc, ctx, m, name):
        t.nc, t.m = nc, m
        sb = lambda n, shape: ctx.enter_context(nc.sbuf_tensor(name + n, shape, FP32))
        t.stats, t.mv = sb("stats", [P, 2 * TT, 6]), sb("mv", [P, 2 * TT, 2])
        t.ve, t.rstd = sb("ve", [P, 2 * TT]), sb("rstd", [P, 2 * TT])
        t.stats_ready, t.ve_ready, t.rstd_ready, t.xn_ready = (
            m.semaphore(nc, name + n) for n in ("stats_ready", "ve_ready", "rstd_ready", "xn_ready"))

    def vector(t, dve, link, p, ready, xn):
        seen = []
        for b in range(2):
            link.wait(ready[b])
            dve.sem_inc(t.m.passed, 1)
            for j in range(TT):
                ins = t.nc.vector.bn_stats(t.stats[:, b * TT + j, :], x_tile(t.m, p * 2 + b, j))
            seen.append(link.mark(ins))
        link.wait(seen[1])
        dve.sem_inc(t.m.passed, 1)
        for j in range(2 * TT):
            ins = t.nc.vector.bn_aggr(t.mv[:, j, :], t.stats[:, j, :])
        ins.then_inc(t.stats_ready, 1)
        dve.wait_ge(t.rstd_ready, p + 1)
        for b in range(2):
            for j in range(TT):
                n = b * TT + j
                ins = t.nc.vector.tensor_scalar(xn[b][:, j, :], x_tile(t.m, p * 2 + b, j), t.mv[:, n, 0:1],
                                                t.rstd[:, n:n + 1], ALU.subtract, ALU.mult)
            ins.then_inc(t.xn_ready, 1)

    def gpsimd(t, pool, p):
        root(t.nc, pool, t.m, t.mv, t.ve, t.rstd, t.stats_ready, t.ve_ready, t.rstd_ready, p)


def x_tile(m, i, j):
    return m.x[:, bass.ds(i * TT + j, 1), :].rearrange("p a d -> p (a d)")


def x_block(m, i):
    return m.x[:, bass.ds(i * TT, TT), :].rearrange("p j d -> p (j d)")


class Tail:

    LINKS = 2 + PairNorm.LINKS

    def __init__(t, nc, ctx, m, d, layer):
        def sb(name, shape, dt=FP32):
            return ctx.enter_context(nc.sbuf_tensor(f"e{layer}_" + name, shape, dt))

        def sem(name):
            return m.semaphore(nc, f"e{layer}_" + name)

        t.nc, t.m, t.d, t.layer = nc, m, d, layer
        t.loads = 2 * DC + (0 if layer else 1)
        t.sums = sb("sums", [P, H * T // P])
        t.num = [sb(f"num{b}", [P, DC, TB]) for b in range(2)]
        t.inv = [sb(f"inv{b}", [P, DC, TB]) for b in range(2)]
        t.xT = [sb(f"xT{b}", [P, DC, TB]) for b in range(2)]
        t.norm = PairNorm(nc, ctx, m, f"e{layer}_")
        t.wo = m.wo1 if layer else sb("wo", [P, DC, D])
        t.bo = sb("bo", [P, D])
        t.pa = [ctx.enter_context(nc.psum_tensor(f"e{layer}_pa{b}", [P, DC, TB], FP32)) for b in range(2)]
        t.w_in, t.b_in, t.x_free = sem("w_in"), sem("b_in"), sem("x_free")
        t.x_in = [sem(f"x_in{b}") for b in range(2)]
        t.sums_in, t.inverted, t.inv_out = sem("sums_in"), sem("inverted"), sem("inv_out")
        t.biased, t.divided, t.projected = sem("biased"), sem("divided"), sem("projected")
        t.turned, t.xT_ready = sem("turned"), sem("xT_ready")

    def weights(t, sp):
        name = f"L{t.layer}_xattn_"
        sums = t.d["sums"].rearrange("(n u r) (a c) -> u r n a c", u=2, r=DH, a=2)[1:2, 0:1]
        sp.dma_start(t.sums[:], sums).then_inc(t.sums_in, 16)
        sp.dma_start(t.bo[:], t.d[name + "bo"].rearrange("(a n) -> a n", a=1).to_broadcast([P, D])).then_inc(t.b_in, 16)
        if not t.layer:
            sp.dma_start(t.wo[:], t.d[name + "Wo"].rearrange("(k p) n -> p k n", p=P)).then_inc(t.w_in, 16)
        sp.sem_inc(t.x_free, 2)
        sp.wait_ge(t.inverted, 1)
        sp.dma_start(t.d["inverses"].rearrange("n (a c) -> (n a) c", a=2), t.sums[:]).then_inc(t.inv_out, 16)
        sp.wait_ge(t.inv_out, 16)

    def load(t, sp, p):
        for b in range(2):
            i = p * 2 + b
            sp.wait_ge(t.x_free, i + 1)
            if not t.layer:
                sp.dma_start(t.m.x[:, bass.ds(i * TT, TT), :],
                             t.d["x_rows"][bass.ds(i * TB, TB), :].rearrange("(j p) d -> p j d", p=P)
                             ).then_inc(t.x_in[b], 16)
            for c in range(DC):
                heads = slice(c * (H // DC), (c + 1) * (H // DC))
                src = t.d["sums"].rearrange("(h j u r) c -> j u h r c", h=H, j=NB, u=2)
                sp.dma_start(t.num[b][:, c, :], src[bass.ds(i, 1), 0, heads]).then_inc(t.x_in[b], 16)
                src = t.d["inverses"].rearrange("(h j r) c -> j h r c", h=H, r=1)[bass.ds(i, 1), heads]
                sp.dma_start(t.inv[b][:, c, :], src.to_broadcast([1, H // DC, DH, TB])).then_inc(t.x_in[b], 16)

    def invert(t, dve):
        dve.wait_ge(t.sums_in, 16)
        t.nc.vector.reciprocal(t.sums[:], t.sums[:]).then_inc(t.inverted, 1)

    def vector(t, dve, link, p, xn):
        nc = t.nc
        for b in range(2):
            dve.wait_ge(t.x_in[b], (p + 1) * (16 * t.loads))
            nc.vector.tensor_tensor(t.num[b][:], t.num[b][:], t.inv[b][:], ALU.mult).then_inc(t.divided, 1)
        ready = []
        for b in range(2):
            i = p * 2 + b
            dve.wait_ge(t.projected, i + 1)
            dve.sem_inc(t.x_free, 1)
            dve.wait_ge(t.biased, i + 1)
            ready.append(link.mark(nc.vector.tensor_tensor(
                x_block(t.m, i), x_block(t.m, i), t.pa[b][:].rearrange("p k c -> p (k c)"), ALU.add)))
        t.norm.vector(dve, link, p, ready, xn)

    def gpsimd(t, pool, p):
        for b in range(2):
            i = p * 2 + b
            if not t.layer:
                hold(pool, t.x_in[b], (p + 1) * (16 * t.loads), t.m.passed)
            t.nc.gpsimd.tensor_tensor(t.m.x[:, bass.ds(i * TT, TT), :], t.m.x[:, bass.ds(i * TT, TT), :],
                                      t.bo[:].unsqueeze(1).to_broadcast([P, TT, D]), ALU.add).then_inc(t.biased, 1)
        t.norm.gpsimd(pool, p)

    def scalar(t, act, p):
        for b in range(2):
            act.wait_ge(t.turned, p * 2 + b + 1)
            t.nc.scalar.copy(t.xT[b][:], t.pa[b][:]).then_inc(t.xT_ready, 1)

    def tensor(t, pe, p, xn):
        nc = t.nc
        for b in range(2):
            pe.wait_ge(t.divided, p * 2 + b + 1)
            to = t.pa[b][:].rearrange("p k (j d) -> p (k j) d", d=D)
            for j in range(TT):
                for c in range(DC):
                    last = nc.tensor.matmul(to[:, j, :], t.num[b][:, c, j * P:(j + 1) * P], t.wo[:, c, :],
                                            start=c == 0, stop=c == DC - 1)
            last.then_inc(t.projected, 1)
        for b in range(2):
            pe.wait_ge(t.norm.xn_ready, p * 2 + b + 1)
            turn_block(nc, t.m, t.pa[b], xn, b).then_inc(t.turned, 1)


def turn_block(nc, m, to, xn, b):
    for k in range(DC):
        for j in range(TT):
            last = nc.tensor.transpose(to[:, k, j * P:(j + 1) * P], xn[b][:, j, k * P:(k + 1) * P], m.ident[:])
    return last


def router(nc, m, d):
    with ExitStack() as ctx:
        t = Tail(nc, ctx, m, d, 0)

        def sb(name, shape, dt):
            return ctx.enter_context(nc.sbuf_tensor("r_" + name, shape, dt))

        def sem(name):
            return m.semaphore(nc, "r_" + name)

        wr = sb("wr", [P, DC, E1], FP32)
        br = sb("br", [1, E1], FP32)
        rank = sb("rank", [P, NT, E1], FP32)
        first_slot = sb("first_slot", [P, NT, E1], FP32)
        zero = sb("zero", [P, T // P * D], FP32)
        xn = [sb(f"xn{b}", [P, TT, D], FP32) for b in range(2)]
        rows = sb("rows", [P, NT, D], FP32)
        l, ex, prob, key, pick = (sb(n, [P, NT, E1], FP32) for n in ("l", "ex", "prob", "key", "pick"))
        col = sb("col", [P, 9, NT], FP32)
        pl = [ctx.enter_context(nc.psum_tensor(f"r_pl{b}", [P, TT * E1], FP32)) for b in range(2)]
        pp = ctx.enter_context(nc.psum_tensor("r_pp", [P, NT * E1], FP32))
        consts, own, zeroed = sem("consts"), sem("own"), sem("zeroed")
        logits, l_ready, lowered, expd = sem("logits"), sem("l_ready"), sem("lowered"), sem("expd")
        picked, counted, slotted = sem("picked"), sem("counted"), sem("slotted")
        scattered, kept = sem("scattered"), sem("kept")
        top, den, gate, best, pos, off, drop, keep, fs = range(9)
        CONSTS = 1 + 2 * E1
        block = ctx.enter_context(nc.Block())

        @block.sync
        def _(sp):
            sp.dma_start(wr[:], d["L0_ffn_Wr"].rearrange("(k p) n -> p k n", p=P)).then_inc(t.w_in, 16)
            sp.dma_start(br[:], d["L0_ffn_br"].rearrange("(a n) -> a n", a=1)).then_inc(t.w_in, 16)
            t.weights(sp)
            with sp.Fori(0, NB // 2) as p:
                t.load(sp, p)
            sp.wait_ge(consts, CONSTS)
            sp.dma_start(d["slots_in"].rearrange("(p n) d -> p (n d)", p=P), zero[:]).then_inc(zeroed, 16)
            sp.wait_ge(zeroed, 16)

        @block.gpsimd
        def _(pool):
            pool.wait_ge(t.b_in, 16)
            with pool.Fori(0, NB // 2) as p:
                t.gpsimd(pool, p)
            pool.wait_ge(zeroed, 16)
            for j in range(NT):
                pool.wait_ge(slotted, j + 1)
                nc.gpsimd.indirect_dma_start(
                    out=d["slots_in"], out_offset=bass.IndirectOffsetOnAxis(ap=m.slots[:, j:j + 1], axis=0),
                    in_=rows[:, j, :], in_offset=None, bounds_check=T - 1, oob_is_err=False,
                ).then_inc(scattered, 16)
            pool.wait_ge(scattered, 16 * NT)

        @block.scalar
        def _(act):
            with act.Fori(0, NB // 2) as p:
                t.scalar(act, p)
                for b in range(2):
                    nc.scalar.copy(rows[:, bass.ds((p * 2 + b) * TT, TT), :], xn[b][:]).then_inc(kept, 1)
                for b in range(2):
                    act.wait_ge(logits, p * 2 + b + 1)
                    nc.scalar.copy(l[:, bass.ds((p * 2 + b) * TT, TT), :],
                                   pl[b][:].rearrange("p (j e) -> p j e", e=E1)).then_inc(l_ready, 1)
            act.wait_ge(kept, NB + 2)
            act.wait_ge(lowered, 1)
            nc.scalar.activation(ex[:], l[:], ACT.Exp).then_inc(expd, 1)

        @block.vector
        def _(dve):
            link = Chain(dve, own)
            V = nc.vector

            def wide(c):
                return col[:, c, :].unsqueeze(2).to_broadcast([P, NT, E1])

            ppv = pp[:].rearrange("p (j e) -> p j e", e=E1)
            dve.sem_inc(kept, 2)
            t.invert(dve)
            V.memset(zero[:], 0.0).then_inc(consts, 1)
            for e in range(E1):
                V.memset(rank[:, :, e], float(E1 - e)).then_inc(consts, 1)
                V.memset(first_slot[:, :, e], float(CAP * e)).then_inc(consts, 1)
            dve.wait_ge(consts, CONSTS)
            with dve.Fori(0, NB // 2) as p:
                link.at(p * t.LINKS)
                dve.wait_ge(kept, (p + 1) * 2)
                t.vector(dve, link, p, xn)
            assert link.n == t.LINKS, link.n
            link.at(NB // 2 * t.LINKS)
            dve.wait_ge(l_ready, NB)
            link(V.tensor_reduce(col[:, top, :], l[:], AXIS.X, ALU.max))
            V.tensor_tensor(l[:], l[:], wide(top), ALU.subtract).then_inc(lowered, 1)
            dve.wait_ge(expd, 1)
            link(V.tensor_reduce(col[:, den, :], ex[:], AXIS.X, ALU.add))
            link(V.reciprocal(col[:, den, :], col[:, den, :]))
            link(V.tensor_tensor(prob[:], ex[:], wide(den), ALU.mult))
            link(V.tensor_reduce(col[:, gate, :], prob[:], AXIS.X, ALU.max))
            link(V.tensor_tensor(key[:], prob[:], wide(gate), ALU.is_equal))
            link(V.tensor_tensor(key[:], key[:], rank[:], ALU.mult))
            link(V.tensor_reduce(col[:, best, :], key[:], AXIS.X, ALU.max))
            V.tensor_tensor(pick[:], key[:], wide(best), ALU.is_equal).then_inc(picked, 1)
            dve.wait_ge(picked, 1)
            link(V.tensor_tensor(prob[:], first_slot[:], pick[:], ALU.mult))
            link(V.tensor_reduce(col[:, off, :], prob[:], AXIS.X, ALU.add))
            dve.wait_ge(counted, 1)
            link(V.tensor_tensor(key[:], ppv, pick[:], ALU.mult))
            link(V.tensor_reduce(col[:, pos, :], key[:], AXIS.X, ALU.add))
            V.tensor_scalar(col[:, drop, :], col[:, pos, :], float(CAP), float(4 * T), ALU.is_ge, ALU.mult)
            V.tensor_scalar(col[:, keep, :], col[:, pos, :], float(CAP), None, ALU.is_lt)
            link(V.tensor_tensor(col[:, fs, :], col[:, pos, :], col[:, off, :], ALU.add))
            link(V.tensor_tensor(m.slots[:], col[:, fs, :], col[:, drop, :], ALU.add))
            V.tensor_tensor(m.gates[:], col[:, gate, :], col[:, keep, :], ALU.mult)
            for j in range(NT):
                V.tensor_scalar(rows[:, j, :], rows[:, j, :], col[:, gate, j:j + 1], None, ALU.mult).then_inc(slotted, 1)

        @block.tensor
        def _(pe):
            pe.wait_ge(t.w_in, 16 * 3)
            with pe.Fori(0, NB // 2) as p:
                t.tensor(pe, p, xn)
                for b in range(2):
                    pe.wait_ge(t.xT_ready, p * 2 + b + 1)
                    for j in range(TT):
                        to = pl[b][:, j * E1:(j + 1) * E1]
                        for c in range(DC):
                            nc.tensor.matmul(to, t.xT[b][:, c, j * P:(j + 1) * P], wr[:, c, :],
                                             start=c == 0, stop=False)
                        last = nc.tensor.matmul(to, m.ones[0:1, :], br[:], start=False, stop=True)
                    last.then_inc(logits, 1)
            pe.wait_ge(picked, 1)
            nc.tensor.matmul(pp[:], m.upto[:], pick[:].rearrange("p j e -> p (j e)"), start=True, stop=False)
            for a in range(NT - 1):
                last = nc.tensor.matmul(pp[:, (a + 1) * E1:].rearrange("p (j e) -> p j e", e=E1), m.ones[:],
                                        pick[:, a:a + 1, :].to_broadcast([P, NT - 1 - a, E1]),
                                        start=False, stop=a == NT - 2)
            last.then_inc(counted, 1)


def experts(nc, m, d):
    with ExitStack() as ctx:
        def sb(name, shape, dt):
            return ctx.enter_context(nc.sbuf_tensor("f_" + name, shape, dt))

        def sem(name):
            return m.semaphore(nc, "f_" + name)

        SC = CAP // P
        w1, w2, b1, b2, xs, xsT, hT, eo, pT, ph, pe_ = [], [], [], [], [], [], [], [], [], [], []
        for b in range(2):
            w1.append(sb(f"w1{b}", [P, DC, D], FP32))
            w2.append(sb(f"w2{b}", [P, DC, D], FP32))
            b1.append(sb(f"b1{b}", [P, DC], FP32))
            b2.append(sb(f"b2{b}", [1, D], FP32))
            xs.append(sb(f"xs{b}", [P, SC, D], FP32))
            xsT.append(sb(f"xsT{b}", [P, DC, CAP], FP32))
            hT.append(sb(f"hT{b}", [P, DC, CAP], FP32))
            eo.append(sb(f"eo{b}", [P, SC, D], FP32))
            pT.append(ctx.enter_context(nc.psum_tensor(f"f_pT{b}", [P, DC * CAP], FP32)))
            ph.append(ctx.enter_context(nc.psum_tensor(f"f_ph{b}", [P, DC * CAP], FP32)))
            pe_.append(ctx.enter_context(nc.psum_tensor(f"f_pe{b}", [P, SC * D], FP32)))
        first_in = [sem(f"first_in{b}") for b in range(2)]
        second_in = [sem(f"second_in{b}") for b in range(2)]
        stored = [sem(f"stored{b}") for b in range(2)]
        turned, xsT_ready, hidden, hT_ready, made, copied = (
            sem("turned"), sem("xsT_ready"), sem("hidden"), sem("hT_ready"), sem("made"), sem("copied"))
        eo_free = sem("eo_free")
        block = ctx.enter_context(nc.Block())

        def weights(name, e):
            return d[name].rearrange("e k n -> (e k) n")[bass.ds(e * D, D), :].rearrange("(k p) n -> p k n", p=P)

        def both(eng, body):
            with eng.Fori(0, E1 // 2 - 1) as p:
                for b in range(2):
                    body(p, b, p * 2 + b)
            for b in range(2):
                body(E1 // 2 - 1, b, E1 - 2 + b)

        @block.sync
        def _(sp):
            sp.sem_inc(hidden, 2)
            sp.sem_inc(made, 2)

            def body(p, b, e):
                hold(sp, hidden, e + 1, m.passed)
                sp.dma_start(xs[b][:], d["slots_in"][bass.ds(e * CAP, CAP), :].rearrange("(k p) n -> p k n", p=P)
                             ).then_inc(first_in[b], 16)
                sp.dma_start(w1[b][:], weights("L0_ffn_W1", e)).then_inc(first_in[b], 16)
                hold(sp, made, e + 1, m.passed)
                sp.dma_start(w2[b][:], weights("L0_ffn_W2", e)).then_inc(second_in[b], 16)
                with nc.allow_non_contiguous_dma(reason="a bias as a column"):
                    sp.dma_start(b1[b][:], d["L0_ffn_b1"].rearrange("e n -> (e n)")[bass.ds(e * D, D)]
                                 .rearrange("(k p) -> p k", p=P)).then_inc(second_in[b], 16)
                sp.dma_start(b2[b][:], d["L0_ffn_b2"][bass.ds(e, 1), :]).then_inc(second_in[b], 16)
            both(sp, body)

        @block.gpsimd
        def _(pool):
            def body(p, b, e):
                hold(pool, copied, e + 1, m.passed)
                pool.dma_start(d["slots_out"][bass.ds(e * CAP, CAP), :].rearrange("(k p) n -> p k n", p=P), eo[b][:]
                               ).then_inc(stored[b], 16)
                hold(pool, stored[b], 16 * (p + 1), eo_free)
            pool.sem_inc(eo_free, 2)
            both(pool, body)

        @block.scalar
        def _(act):
            def body(p, b, e):
                act.wait_ge(hidden, e + 3)
                act.wait_ge(second_in[b], (p + 1) * (16 * 3))
                for k in range(DC):
                    ins = nc.scalar.activation(hT[b][:, k, :], ph[b][:, k * CAP:(k + 1) * CAP], ACT.Relu,
                                               bias=b1[b][:, k:k + 1])
                ins.then_inc(hT_ready, 1)
            both(act, body)

        @block.vector
        def _(dve):
            def take(b, e):
                dve.wait_ge(turned, e + 1)
                nc.vector.tensor_copy(xsT[b][:].rearrange("p k c -> p (k c)"), pT[b][:]).then_inc(xsT_ready, 1)

            def body(p, b, e):
                if not (isinstance(e, int) and e == E1 - 1):
                    take(1 - b, e + 1)
                dve.wait_ge(made, e + 3)
                dve.wait_ge(eo_free, e + 1)
                nc.vector.tensor_copy(eo[b][:].rearrange("p k c -> p (k c)"), pe_[b][:]).then_inc(copied, 1)
            take(0, 0)
            both(dve, body)

        @block.tensor
        def _(pe):
            def turn(p, b):
                pe.wait_ge(first_in[b], (p + 1) * (16 * 2))
                for k in range(DC):
                    for j in range(SC):
                        last = nc.tensor.transpose(pT[b][:, k * CAP + j * P:k * CAP + (j + 1) * P],
                                                   xs[b][:, j, k * P:(k + 1) * P], m.ident[:])
                last.then_inc(turned, 1)

            def body(p, b, e):
                pe.wait_ge(xsT_ready, e + 1)
                for k in range(DC):
                    for c in range(DC):
                        last = nc.tensor.matmul(ph[b][:, k * CAP:(k + 1) * CAP], w1[b][:, c, k * P:(k + 1) * P],
                                                xsT[b][:, c, :], start=c == 0, stop=c == DC - 1)
                last.then_inc(hidden, 1)
                if not (isinstance(e, int) and e == E1 - 1):
                    turn(p + b, 1 - b)
                pe.wait_ge(hT_ready, e + 1)
                pe.wait_ge(second_in[b], (p + 1) * (16 * 3))
                for j in range(SC):
                    to = pe_[b][:, j * D:(j + 1) * D]
                    for c in range(DC):
                        nc.tensor.matmul(to, hT[b][:, c, j * P:(j + 1) * P], w2[b][:, c, :], start=c == 0, stop=False)
                    last = nc.tensor.matmul(to, m.ones[0:1, :], b2[b][:], start=False, stop=True)
                last.then_inc(made, 1)
            turn(0, 0)
            both(pe, body)


def gather(nc, m, d):
    with ExitStack() as ctx:
        def sb(name, shape, dt=FP32):
            return ctx.enter_context(nc.sbuf_tensor("g_" + name, shape, dt))

        def sem(name):
            return m.semaphore(nc, "g_" + name)

        norm = PairNorm(nc, ctx, m, "g_")
        eo = sb("eo", [P, NT, D])
        xn, xT, kf, rest = ([sb(f"{n}{b}", shape) for b in range(2)] for n, shape in (
            ("xn", [P, TT, D]), ("xT", [P, DC, TB]), ("kf", [P, DC, TB]), ("rest", [P, DC, TB])))
        parts = [sb(f"parts{b}", [P, 3, DC, TB], BF16) for b in range(2)]
        bq = sb("bq", [P, DC])
        pa = [ctx.enter_context(nc.psum_tensor(f"g_pa{b}", [P, DC, TB], FP32)) for b in range(2)]
        pq = [ctx.enter_context(nc.psum_tensor(f"g_pq{b}", [P, DC, TB], FP32)) for b in range(2)]
        w_in, cleared, own = sem("w_in"), sem("cleared"), sem("own")
        eo_in = [sem(f"eo_in{p}") for p in range(NB // 2)]
        turned, xT_ready, proj, kf_ready, split_done = (
            sem("turned"), sem("xT_ready"), sem("proj"), sem("kf_ready"), sem("split_done"))
        parts_out = [sem(f"parts_out{b}") for b in range(2)]
        block = ctx.enter_context(nc.Block())

        @block.sync
        def _(sp):
            with nc.allow_non_contiguous_dma(reason="a bias as a column"):
                sp.dma_start(bq[:], d["L1_xattn_bq"].rearrange("(k p) -> p k", p=P)).then_inc(w_in, 16)
            for b in range(2):
                sp.sem_inc(parts_out[b], 16)
            with sp.Fori(0, NB // 2) as p:
                for b in range(2):
                    hold(sp, split_done, p * 2 + b + 1, m.passed)
                    sp.dma_start(d["q_parts"][1][:, bass.ds((p * 2 + b) * TB, TB)].rearrange("(q p) c -> p q c", p=P),
                                 parts[b][:].rearrange("p g k c -> p (g k) c")).then_inc(parts_out[b], 16)
            for b in range(2):
                sp.wait_ge(parts_out[b], 16 * (NB // 2 + 1))

        @block.gpsimd
        def _(pool):
            for p in range(NB // 2):
                pool.wait_ge(cleared, p + 1)
                for j in range(p * 2 * TT, (p + 1) * 2 * TT):
                    nc.gpsimd.indirect_dma_start(
                        out=eo[:, j, :], out_offset=None, in_=d["slots_out"],
                        in_offset=bass.IndirectOffsetOnAxis(ap=m.slots[:, j:j + 1], axis=0),
                        bounds_check=T - 1, oob_is_err=False).then_inc(eo_in[p], 16)
            for p in range(NB // 2):
                norm.gpsimd(pool, p)

        @block.scalar
        def _(act):
            act.wait_ge(w_in, 16)
            with act.Fori(0, NB // 2) as p:
                for b in range(2):
                    act.wait_ge(turned, p * 2 + b + 1)
                    nc.scalar.copy(xT[b][:], pa[b][:]).then_inc(xT_ready, 1)
                for b in range(2):
                    act.wait_ge(proj, p * 2 + b + 1)
                    for k in range(DC):
                        ins = nc.scalar.activation(kf[b][:, k, :], pq[b][:, k, :], ACT.Identity, bias=bq[:, k:k + 1])
                    ins.then_inc(kf_ready, 1)

        @block.vector
        def _(dve):
            link = Chain(dve, own)
            V = nc.vector
            LINKS = 2 + PairNorm.LINKS + 3 * 2
            for p in range(NB // 2):
                V.memset(eo[:, p * 2 * TT:(p + 1) * 2 * TT, :], 0.0).then_inc(cleared, 1)
            for p in range(NB // 2):
                link.at(p * LINKS)
                dve.wait_ge(eo_in[p], 16 * 2 * TT)
                ready = []
                for b in range(2):
                    for j in range(TT):
                        n = (p * 2 + b) * TT + j
                        x = m.x[:, n, :]
                        ins = V.scalar_tensor_tensor(out=x, in0=eo[:, n, :], scalar=m.gates[:, n:n + 1], in1=x,
                                                     op0=ALU.mult, op1=ALU.add)
                    ready.append(link.mark(ins))
                norm.vector(dve, link, p, ready, xn)
                marks = []
                for b in range(2):
                    dve.wait_ge(kf_ready, p * 2 + b + 1)
                    dve.wait_ge(parts_out[b], 16 * (p + 1))
                    marks.append(link.mark(V.tensor_copy(parts[b][:, 0], kf[b][:])))
                    link.wait(marks[-1])
                    marks.append(link.mark(V.tensor_tensor(rest[b][:], kf[b][:], parts[b][:, 0], ALU.subtract)))
                    link.wait(marks[-1])
                    marks.append(link.mark(V.tensor_copy(parts[b][:, 1], rest[b][:])))
                    link.wait(marks[-1])
                    V.tensor_tensor(parts[b][:, 2], rest[b][:], parts[b][:, 1], ALU.subtract).then_inc(split_done, 1)
            assert link.n == LINKS, link.n

        @block.tensor
        def _(pe):
            with pe.Fori(0, NB // 2) as p:
                for b in range(2):
                    pe.wait_ge(norm.xn_ready, p * 2 + b + 1)
                    turn_block(nc, m, pa[b], xn, b).then_inc(turned, 1)
                for b in range(2):
                    pe.wait_ge(xT_ready, p * 2 + b + 1)
                    for k in range(DC):
                        for c in range(DC):
                            last = nc.tensor.matmul(pq[b][:, k, :], m.wq1[:, c, k * P:(k + 1) * P], xT[b][:, c, :],
                                                    start=c == 0, stop=c == DC - 1)
                    last.then_inc(proj, 1)


class Path:

    def __init__(self, name, kts, pbufs, causal=False, row=False, masked=False, lead=4, rest=1):
        self.name, self.kts, self.causal, self.pbufs = name, kts, causal, pbufs
        self.row, self.masked = row, masked
        self.fills = 2 + 1 + U + (U // 2 if row else 0)
        self.rows = STACK + row
        self.c0 = kts[0] * P
        self.steps = [(kt, half, max(half * 2 * TB, kt * P if causal else 0)) for kt in kts for half in range(2)
                      if not causal or kt * P < (half + 1) * 2 * TB]
        self.pieces = []
        for i in range(NT):
            end = min(S, P * (i + 1)) if causal else S
            self.pieces += [(i, n, c, min(c + TB, end)) for n, c in enumerate(range(self.c0, end, TB))]
        self.ne = len(self.steps)
        self.nm = len(self.pieces) + 1
        assert (U * self.ne) % pbufs == 0 
        self.plan(lead, rest)

    def plan(self, lead, rest):
        cost = [(half + 1) * 2 * TB - q0 + 220 for _, half, q0 in self.steps]
        work = [end - c + 80 for _, _, c, end in self.pieces]
        done, at, share = 0, 0, []
        for n in range(self.nm):
            share.append(done / sum(work))
            done += work[n] if n < len(work) else 0
        self.slots = [[] for _ in range(self.ne)]
        shift = 1 - sum(cost[-lead:]) / sum(cost)
        edges = [sum(cost[:e + 1]) / sum(cost) for e in range(self.ne)]
        for k in (1, 2):
            for n in range(self.nm):
                when = shift - 1 + share[n] * (1 - rest / self.ne) + (k - 1)
                if n == self.nm - 1:
                    when = shift - 1e-6 + (k - 1)
                if 0 <= when < 1:
                    self.slots[next(e for e in range(self.ne) if when < edges[e])].append((k, n))
        self.early = [n for slot in self.slots for k, n in slot if k == 2]


def wait(eng, sem, value):
    if not (isinstance(value, int) and value <= 0):
        eng.wait_ge(sem, value)


def attend(nc, m, d, layer, paths, mask=None):
    with ExitStack() as ctx:
        def sb(name, shape, dt):
            return ctx.enter_context(nc.sbuf_tensor(f"t{layer}_" + name, shape, dt))

        q = [sb(f"q{b}", [ROWS, T], BF16) for b in range(U)]
        k = [sb(f"k{b}", [ROWS, KT * P], BF16) for b in range(U)]
        vo = [sb(f"vo{b}", [P, KT, 2 * DH], FP32) for b in range(2)]
        prob = [sb(f"prob{b}", [P, 2 * TB], FP32) for b in range(max(x.pbufs for x in paths))]
        osb = [sb(f"osb{b}", [P, TB], FP32) for b in range(2)]
        part_max = sb("part_max", [P, NT, 4], FP32)
        neg_max = sb("neg_max", [P, NT], FP32)
        neg_rest = sb("neg_rest", [P, NT], FP32)
        neg_cols = sb("neg_cols", [P, 2 * NT], BF16)
        neg_rows = sb("neg_rows", [2 * NT, P], BF16)
        mask_t = sb("mask_t", [P, len(paths[-1].kts), T], BF16) if mask is not None else None
        scores = [ctx.enter_context(nc.psum_tensor(f"t{layer}_s{b}", [P, 2 * TB], FP32)) for b in range(2)]
        mx = [ctx.enter_context(nc.psum_tensor(f"t{layer}_m{b}", [P, TB], FP32)) for b in range(MX)]
        out = ctx.enter_context(nc.psum_tensor(f"t{layer}_o", [P, TB], FP32))
        QFILL = U // 2
        NLOAD = 6

        class Sems:
            def __init__(s, name):
                def sem(n):
                    return m.semaphore(nc, f"t{layer}{name}_{n}")
                s.qk_in = [sem(f"qk_in{b}") for b in range(U)]
                s.neg_in = [sem(f"neg_in{b}") for b in range(U)]
                s.v_in = [sem(f"v_in{b}") for b in range(2)]
                s.scored = sem("scored")
                s.expd = sem("expd")
                s.used = sem("used")
                s.piece = sem("piece")
                s.taken = sem("taken")
                s.neg_cols = sem("neg_cols")
                s.neg_rows = sem("neg_rows")
                s.copied = sem("copied")
                s.stored = [sem(f"stored{b}") for b in range(2)]
                s.own = sem("own")
                s.mturned = sem("mturned")
                s.mcopied = sem("mcopied")
                s.ready = sem("ready")
                s.filled = sem("filled")

        sems = [Sems(x.name) for x in paths]
        block = ctx.enter_context(nc.Block())

        def choose(eng, run):
            if len(paths) == 1:
                run(paths[0], sems[0])
                return
            fast = eng.value_load(m.flag[0:1, 0:1], min_val=0, max_val=1)
            with eng.If(fast >= 1):
                run(paths[0], sems[0])
                eng.nop()
            with eng.Else():
                run(paths[1], sems[1])
                eng.nop()
            eng.nop()

        def heads(eng, body):
            for b in range(U):
                body(0, b)
            with eng.Fori(1, H // U - 1) as p:
                for b in range(U):
                    body(p, b)
            for b in range(U):
                body(H // U - 1, b)

        def after(p, b, n):
            p, b = p + (b + n) // U, (b + n) % U
            if isinstance(p, int) and not 0 <= p < H // U:
                return None
            return p, b

        def turn(p, b):
            return p * (U // 2) + b // 2

        @block.sync
        def _(sp):
            def run(path, s):
                def load(p, b):
                    rows = bass.ds(p * (U * DH) + b * DH, DH)
                    for g, (at, n) in enumerate(GROUPS):
                        to = slice(at * DH, (at + n) * DH)
                        sp.dma_start(q[b][to, :], d["q_parts"][layer].rearrange("(g r) c -> g r c", g=3)[0:n, rows, :]
                                     ).then_inc(s.qk_in[b], 16)
                        sp.dma_start(k[b][to, path.c0:S],
                                     d["k_parts"][layer].rearrange("(g r) c -> g r c", g=3)[g:g + 1, rows, path.c0:S]
                                     .to_broadcast([n, DH, S - path.c0])).then_inc(s.qk_in[b], 16)

                def neg(p, b):
                    sp.wait_ge(s.neg_rows, p * U + b + 1)
                    for r in range(2):
                        sp.dma_start(q[b][path.rows + r:path.rows + r + 1, :].rearrange("a (i c) -> a i c", c=P),
                                     neg_rows[r * NT:(r + 1) * NT, :]).then_inc(s.neg_in[b], 16)

                def store(p, b):
                    sp.wait_ge(s.copied, p * U + b + 1)
                    sp.dma_start(d["sums"][bass.ds(p * (U * P) + b * P, P), :], osb[b % 2][:]
                                 ).then_inc(s.stored[b % 2], 16)

                for b in range(2):
                    sp.sem_inc(s.stored[b], 16)
                for b in range(3):
                    load(0, b)
                neg(0, 0)

                def body(p, b):
                    if after(p, b, 3):
                        wait(sp, s.scored, (p * U + b) * path.ne)
                        load(*after(p, b, 3))
                    if after(p, b, -1):
                        store(*after(p, b, -1))
                    if after(p, b, 1):
                        neg(*after(p, b, 1))

                heads(sp, body)
                store(H // U - 1, U - 1)
                for b in range(2):
                    sp.wait_ge(s.stored[b], 16 * (H // 2 + 1))
            choose(sp, run)

        @block.gpsimd
        def _(pool):
            def run(path, s):
                link = Chain(pool, s.filled)
                if path.row:
                    for b in range(QFILL, U):
                        link(nc.gpsimd.memset(q[b][STACK:STACK + 1, :], 1.0))
                for b in range(2):
                    link(nc.gpsimd.memset(vo[b][:, :, DH:2 * DH], 1.0))
                pool.sem_inc(s.ready, 2 + (U - QFILL if path.row else 0))
                pool.wait_ge(s.ready, path.fills)

                def body(p, b):
                    wait(pool, s.used, (p * U + b - 1) * path.ne)
                    at = bass.ds(p * (U * DH) + b * DH, DH)
                    full = [kt for kt in path.kts if kt < KT - 1]
                    nc.gpsimd.tensor_copy(vo[b % 2][:, full[0]:full[-1] + 1, 0:DH],
                                          m.v[layer][:, full[0]:full[-1] + 1, at]).then_inc(s.v_in[b % 2], 1)
                    nc.gpsimd.tensor_copy(vo[b % 2][0:KLAST, KT - 1, 0:DH],
                                          m.v[layer][0:KLAST, KT - 1, at]).then_inc(s.v_in[b % 2], 1)
                heads(pool, body)
            choose(pool, run)

        @block.scalar
        def _(act):
            def run(path, s):
                def body(p, b):
                    base = p * (U * path.ne) + b * path.ne
                    for e, (kt, half, q0) in enumerate(path.steps):
                        n = b * path.ne + e
                        act.wait_ge(s.scored, base + e + 1)
                        wait(act, s.used, base + e + 1 - path.pbufs)
                        c = q0 - half * 2 * TB
                        rows = keys_of(kt)
                        nc.scalar.activation(prob[n % path.pbufs][0:rows, c:], scores[n % 2][0:rows, c:],
                                             ACT.Exp, scale=DH ** -0.5).then_inc(s.expd, 1)
                heads(act, body)
            choose(act, run)

        @block.vector
        def _(dve):
            def run(path, s):
                link = Chain(dve, s.own)
                nc.vector.memset(part_max[:], -3.0e38).then_inc(s.ready, 1)
                for b in range(U):
                    ins = nc.vector.memset(k[b][STACK:path.rows + 2, path.c0:S], 1.0)
                    if path.row:
                        link(ins)
                        if b < QFILL:
                            nc.vector.memset(q[b][STACK:STACK + 1, :], 1.0)
                        ins = nc.vector.tensor_copy(k[b][STACK:STACK + 1, path.c0:S], m.mask_row[STACK:STACK + 1, :])
                    ins.then_inc(s.ready, 1)
                dve.wait_ge(s.ready, path.fills)
                if path.masked:
                    for i, kt in enumerate(path.kts):
                        dve.wait_ge(s.mturned, i + 1)
                        rows = keys_of(kt)
                        nc.vector.tensor_copy(mask_t[0:rows, i, :], scores[i % 2][:].bitcast(BF16)[0:rows, :]
                                              ).then_inc(s.mcopied, 1)
                LINKS = 3

                def piece(p, b, n):
                    base = p * (U * path.nm) + b * path.nm
                    ps = mx[n % MX]
                    if n < path.nm - 1:
                        i, part, c, end = path.pieces[n]
                        dve.wait_ge(s.piece, base + n + 1)
                        nc.vector.tensor_reduce(part_max[:, i, part:part + 1], ps[:, 0:end - c], AXIS.X, ALU.max
                                                ).then_inc(s.taken, 1)
                        return
                    link.at((p * U + b) * LINKS + (U if path.row else 0))
                    dve.wait_ge(s.taken, base + n)
                    link(nc.vector.tensor_reduce(neg_max[:], part_max[:], AXIS.X, ALU.max, negate=True))
                    link(nc.vector.tensor_copy(neg_cols[:, 0:NT], neg_max[:]))
                    link(nc.vector.tensor_tensor(neg_rest[:], neg_max[:], neg_cols[:, 0:NT], ALU.subtract))
                    nc.vector.tensor_copy(neg_cols[:, NT:2 * NT], neg_rest[:]).then_inc(s.neg_cols, 1)
                    dve.wait_ge(s.piece, base + path.nm)
                    before = after(p, b, -1)
                    if before:
                        dve.wait_ge(s.neg_in[before[1]], 32 * (before[0] + 1))
                    nc.vector.tensor_copy(neg_rows[:], ps[:].bitcast(BF16)[0:2 * NT, 0:P]).then_inc(s.taken, 1)
                    dve.wait_ge(s.taken, base + path.nm)
                    dve.sem_inc(s.neg_rows, 1)

                def copy_sums(p, b):
                    dve.wait_ge(s.used, (p * U + b + 1) * path.ne)
                    dve.wait_ge(s.stored[b % 2], 16 * (turn(p, b) + 1))
                    nc.vector.tensor_copy(osb[b % 2][:], out[:]).then_inc(s.copied, 1)

                for n in range(path.nm):
                    piece(0, 0, n)
                for n in path.early:
                    piece(0, 1, n)

                def body(p, b):
                    for e, slot in enumerate(path.slots):
                        for k_, n in slot:
                            if after(p, b, k_):
                                piece(*after(p, b, k_), n)
                        if e == 1 and after(p, b, -1):
                            copy_sums(*after(p, b, -1))
                heads(dve, body)
                copy_sums(H // U - 1, U - 1)
            choose(dve, run)

        @block.tensor
        def _(pe):
            def run(path, s):
                pe.wait_ge(s.ready, path.fills)
                if path.masked:
                    for i, kt in enumerate(path.kts):
                        rows = keys_of(kt)
                        wait(pe, s.mcopied, i - 1)
                        for t in range(NT):
                            last = nc.tensor.transpose(scores[i % 2][:].bitcast(BF16)[0:rows, t * P:(t + 1) * P],
                                                       mask[:, t * S + kt * P:t * S + kt * P + rows], m.ident_bf[:])
                        last.then_inc(s.mturned, 1)
                    pe.wait_ge(s.mcopied, len(path.kts))

                def score(p, b, e):
                    kt, half, q0 = path.steps[e]
                    n = b * path.ne + e
                    base = p * (U * path.ne) + n
                    if e == 0:
                        pe.wait_ge(s.neg_in[b], 32 * (p + 1))
                    wait(pe, s.expd, base - 1)
                    rows = keys_of(kt)
                    c = q0
                    while c < (half + 1) * 2 * TB:
                        end = (c // TB + 1) * TB
                        at = c - half * 2 * TB
                        diag = path.causal and c == kt * P
                        ps = scores[n % 2]
                        last = nc.tensor.matmul(ps[0:rows, at:at + end - c],
                                                k[b][0:path.rows + 2, kt * P:kt * P + rows],
                                                q[b][0:path.rows + 2, c:end], start=True,
                                                stop=not path.masked and not diag)
                        if path.masked:
                            last = nc.tensor.matmul(ps[0:rows, at:at + end - c], m.neg_big[0:rows, 0:rows],
                                                    mask_t[0:rows, path.kts.index(kt), c:end], start=False, stop=True)
                        if diag:
                            last = nc.tensor.matmul(ps[0:rows, at:at + P], m.neg_big[0:rows, 0:rows],
                                                    m.late_key[0:rows, :], start=False, stop=True)
                        c = end
                    last.then_inc(s.scored, 1)

                def weigh(p, b, e):
                    kt, half, q0 = path.steps[e]
                    n = b * path.ne + e
                    pe.wait_ge(s.expd, p * (U * path.ne) + n + 1)
                    if e == 0:
                        pe.wait_ge(s.v_in[b % 2], 2 * (turn(p, b) + 1))
                        wait(pe, s.copied, p * U + b)
                    rows = keys_of(kt)
                    for j in (2 * half, 2 * half + 1):
                        c = max(q0, j * TB)
                        if c >= (j + 1) * TB:
                            continue
                        at = c - half * 2 * TB
                        final = kt == path.kts[-1] or (path.causal and kt == 4 * j + 3)
                        last = nc.tensor.matmul(out[32 * j:32 * j + 32, c - j * TB:TB], vo[b % 2][0:rows, kt, :],
                                                prob[n % path.pbufs][0:rows, at:at + (j + 1) * TB - c],
                                                start=kt == path.kts[0], stop=final)
                    last.then_inc(s.used, 1)

                def piece(p, b, n):
                    base = p * (U * path.nm) + b * path.nm
                    if n == 0:
                        pe.wait_ge(s.qk_in[b], (16 * NLOAD) * (p + 1))
                    prior = n - MX if n >= MX else (path.nm - 1 - n) // MX * MX + n - path.nm
                    wait(pe, s.taken, base + prior + 1)
                    ps = mx[n % MX]
                    if n == path.nm - 1:
                        pe.wait_ge(s.neg_cols, p * U + b + 1)
                        nc.tensor.transpose(ps[:].bitcast(BF16)[0:2 * NT, 0:P], neg_cols[:], m.ident_bf[:]
                                            ).then_inc(s.piece, 1)
                        return
                    i, _, c, end = path.pieces[n]
                    diag = path.causal and i < KT and end == min(S, P * (i + 1))
                    last = nc.tensor.matmul(ps[:, 0:end - c], q[b][0:path.rows, i * P:(i + 1) * P],
                                            k[b][0:path.rows, c:end], start=True, stop=not path.masked and not diag)
                    if path.masked:
                        last = nc.tensor.matmul(ps[:, 0:end - c], m.neg_big[:], mask[:, i * S + c:i * S + end],
                                                start=False, stop=True)
                    if diag:
                        last = nc.tensor.matmul(ps[:, i * P - c:end - c], m.neg_big[:], m.late_key_q[:, 0:end - i * P],
                                                start=False, stop=True)
                    last.then_inc(s.piece, 1)

                for n in range(path.nm):
                    piece(0, 0, n)
                for n in path.early:
                    piece(0, 1, n)

                def body(p, b):
                    for e in range(path.ne):
                        score(p, b, e)
                        if e >= 3:
                            for f in ((0, 1) if e == 3 else (e - 2,)):
                                weigh(p, b, f)
                        elif e < 2 and after(p, b, -1):
                            weigh(*after(p, b, -1), path.ne - 2 + e)
                        for k_, n in path.slots[e]:
                            if after(p, b, k_):
                                piece(*after(p, b, k_), n)
                heads(pe, body)
                for e in (path.ne - 2, path.ne - 1):
                    weigh(H // U - 1, U - 1, e)
            choose(pe, run)


def weights_of_experts(nc, m, d):
    with ExitStack() as ctx:
        t = Tail(nc, ctx, m, d, 1)

        def sb(name, shape, dt=FP32):
            return ctx.enter_context(nc.sbuf_tensor("w_" + name, shape, dt))

        def sem(name):
            return m.semaphore(nc, "w_" + name)

        G = TT * HM
        HC = HM // DC
        wm = sb("wm", [P, DC, D])
        bm = sb("bm", [P, DC])
        emb = sb("emb", [P, HC * E2])
        rank = sb("rank", [P, 2 * G, E2])
        xn, h, rest = ([sb(f"{n}{b}", shape) for b in range(2)] for n, shape in (
            ("xn", [P, TT, D]), ("h", [P, DC, TB]), ("rest", [P, DC, TB])))
        parts = [sb(f"parts{b}", [P, 3, DC, TB], BF16) for b in range(2)]
        l, w, key, first, second = (sb(n, [P, 2 * G, E2]) for n in ("l", "w", "key", "first", "second"))
        ex, low = key, l
        col = sb("col", [P, 5, 2 * G])
        wT = [sb(f"wT{b}", [P, TB]) for b in range(2)]
        ph = [ctx.enter_context(nc.psum_tensor(f"w_ph{b}", [P, DC, TB], FP32)) for b in range(2)]
        consts, own, hid, h_ready, split_done, parts_free = (
            sem("consts"), sem("own"), sem("hid"), sem("h_ready"), sem("split_done"), sem("parts_free"))
        logits, lowered, expd, weighed, w_turned, wT_ready, wT_free = (
            sem("logits"), sem("lowered"), sem("expd"), sem("weighed"), sem("w_turned"), sem("wT_ready"), sem("wT_free"))
        parts_out, wT_out = ([sem(f"{n}{b}") for b in range(2)] for n in ("parts_out", "wT_out"))
        top, den, best, best2, top2 = range(5)
        CONSTS = 1 + E2
        WEIGHTS = 2 + HC
        block = ctx.enter_context(nc.Block())

        @block.sync
        def _(sp):
            sp.dma_start(wm[:], d["L1_ffn_Wm"].rearrange("(k p) n -> p k n", p=P)).then_inc(t.w_in, 16)
            with nc.allow_non_contiguous_dma(reason="a bias as a column"):
                sp.dma_start(bm[:], d["L1_ffn_bm"].rearrange("(k p) -> p k", p=P)).then_inc(t.w_in, 16)
            t.weights(sp)
            sp.wait_ge(consts, CONSTS)
            for a in range(HC):
                sp.dma_start(emb[a * HD:(a + 1) * HD, a * E2:(a + 1) * E2], d["L1_ffn_expert_emb"]).then_inc(t.w_in, 16)
            with sp.Fori(0, NB // 2) as p:
                t.load(sp, p)

        @block.gpsimd
        def _(pool):
            nc.gpsimd.memset(emb[:], 0.0).then_inc(consts, 1)
            for e in range(E2):
                nc.gpsimd.memset(rank[:, :, e], float(E2 - e)).then_inc(consts, 1)
            pool.wait_ge(t.b_in, 16)
            pool.sem_inc(parts_free, 2)
            pool.sem_inc(wT_free, 2)
            with pool.Fori(0, NB // 2) as p:
                t.gpsimd(pool, p)
                for b in range(2):
                    hold(pool, split_done, p * 2 + b + 1, m.passed)
                    pool.dma_start(d["t_parts"][:, bass.ds((p * 2 + b) * TB, TB)].rearrange("(q p) c -> p q c", p=P),
                                   parts[b][:].rearrange("p g k c -> p (g k) c")).then_inc(parts_out[b], 16)
                for b in range(2):
                    hold(pool, wT_ready, p * 2 + b + 1, m.passed)
                    pool.dma_start(d["w_t"][bass.ds((p * 2 + b) * P, P), :], wT[b][:]).then_inc(wT_out[b], 16)
                for b in range(2):
                    hold(pool, parts_out[b], 16 * (p + 1), parts_free)
                    hold(pool, wT_out[b], 16 * (p + 1), wT_free)

        @block.scalar
        def _(act):
            act.wait_ge(t.w_in, 16 * WEIGHTS)
            with act.Fori(0, NB // 2) as p:
                t.scalar(act, p)
                for b in range(2):
                    act.wait_ge(hid, p * 2 + b + 1)
                    for k in range(DC):
                        ins = nc.scalar.activation(h[b][:, k, :], ph[b][:, k, :], ACT.Identity, bias=bm[:, k:k + 1])
                    ins.then_inc(h_ready, 1)
                act.wait_ge(lowered, p + 1)
                nc.scalar.activation(ex[:], l[:], ACT.Exp).then_inc(expd, 1)
                for b in range(2):
                    act.wait_ge(w_turned, p * 2 + b + 1)
                    act.wait_ge(wT_free, p * 2 + b + 1)
                    nc.scalar.copy(wT[b][:], ph[b][:, 1, :]).then_inc(wT_ready, 1)

        @block.vector
        def _(dve):
            link = Chain(dve, own)
            V = nc.vector
            LINKS = t.LINKS + 3 * 2 + 17

            def wide(c):
                return col[:, c, :].unsqueeze(2).to_broadcast([P, 2 * G, E2])

            def greatest(values, at, top_at, pick):
                link(V.tensor_reduce(col[:, top_at, :], values[:], AXIS.X, ALU.max))
                link(V.tensor_tensor(key[:], values[:], wide(top_at), ALU.is_equal))
                link(V.tensor_tensor(key[:], key[:], rank[:], ALU.mult))
                link(V.tensor_reduce(col[:, at, :], key[:], AXIS.X, ALU.max))
                link(V.tensor_tensor(pick[:], key[:], wide(at), ALU.is_equal))

            t.invert(dve)
            dve.wait_ge(consts, CONSTS)
            with dve.Fori(0, NB // 2) as p:
                link.at(p * LINKS)
                t.vector(dve, link, p, xn)
                for b in range(2):
                    dve.wait_ge(h_ready, p * 2 + b + 1)
                    dve.wait_ge(parts_free, p * 2 + b + 1)
                    link(V.tensor_copy(parts[b][:, 0], h[b][:]))
                    link(V.tensor_tensor(rest[b][:], h[b][:], parts[b][:, 0], ALU.subtract))
                    link(V.tensor_copy(parts[b][:, 1], rest[b][:]))
                    V.tensor_tensor(parts[b][:, 2], rest[b][:], parts[b][:, 1], ALU.subtract).then_inc(split_done, 1)
                pg = [t.pa[b][:, 0, :].rearrange("p (g e) -> p g e", e=E2) for b in range(2)]
                for b in range(2):
                    dve.wait_ge(logits, p * 2 + b + 1)
                    ins = V.tensor_reduce(col[:, top, b * G:(b + 1) * G], pg[b], AXIS.X, ALU.max)
                link(ins)
                for b in range(2):
                    of = slice(b * G, (b + 1) * G)
                    ins = V.tensor_tensor(l[:, of, :], pg[b],
                                          col[:, top, of].unsqueeze(2).to_broadcast([P, G, E2]), ALU.subtract)
                ins.then_inc(lowered, 1)
                dve.wait_ge(expd, p + 1)
                link(V.tensor_reduce(col[:, den, :], ex[:], AXIS.X, ALU.add))
                link(V.reciprocal(col[:, den, :], col[:, den, :]))
                link(V.tensor_tensor(w[:], ex[:], wide(den), ALU.mult))
                greatest(w, best, top, first)
                link(V.scalar_tensor_tensor(out=low[:], in0=first[:], scalar=-2.0, in1=w[:], op0=ALU.mult, op1=ALU.add))
                greatest(low, best2, top2, second)
                link(V.tensor_tensor(first[:], first[:], second[:], ALU.add))
                link(V.tensor_tensor(w[:], w[:], first[:], ALU.mult))
                dve.sem_inc(weighed, 1)
            assert link.n == LINKS, link.n

        @block.tensor
        def _(pe):
            pe.wait_ge(t.w_in, 16 * WEIGHTS)
            with pe.Fori(0, NB // 2) as p:
                t.tensor(pe, p, xn)
                for b in range(2):
                    pe.wait_ge(t.xT_ready, p * 2 + b + 1)
                    for k in range(DC):
                        for c in range(DC):
                            last = nc.tensor.matmul(ph[b][:, k, :], wm[:, c, k * P:(k + 1) * P], t.xT[b][:, c, :],
                                                    start=c == 0, stop=c == DC - 1)
                    last.then_inc(hid, 1)
                for b in range(2):
                    pe.wait_ge(h_ready, p * 2 + b + 1)
                    for j in range(TT):
                        for c in range(DC):
                            at = (j * HM + c * HC) * E2
                            last = nc.tensor.matmul(t.pa[b][:, 0, at:at + HC * E2], h[b][:, c, j * P:(j + 1) * P],
                                                    emb[:], start=True, stop=True)
                    last.then_inc(logits, 1)
                pe.wait_ge(weighed, p + 1)
                for b in range(2):
                    for j in range(TT):
                        at = (b * TT + j) * HM
                        last = nc.tensor.transpose(ph[b][:, 1, j * P:(j + 1) * P],
                                                   w[:, at:at + HM, :].rearrange("p h e -> p (h e)"), m.ident[:])
                    last.then_inc(w_turned, 1)


def head_experts(nc, m, d):
    with ExitStack() as ctx:
        def sb(name, shape, dt):
            return ctx.enter_context(nc.sbuf_tensor("x_" + name, shape, dt))

        def sem(name):
            return m.semaphore(nc, "x_" + name)

        HC = HM // DC
        K3 = 3 * HD
        HB = 4
        w1f = sb("w1f", [K3, E2, F2], FP32)
        w1r = sb("w1r", [K3, E2, F2], FP32)
        w1m = sb("w1m", [K3, E2, F2], BF16)
        w1 = [sb(f"w1{n}", [K3, E2, F2], BF16) for n in range(2)]
        b1 = sb("b1", [F2, E2], FP32)
        w2 = sb("w2", [F2, E2, HD], FP32)
        b2 = sb("b2", [P, E2], FP32)
        wo = sb("wo", [P, DC, D], FP32)
        bo = sb("bo", [1, D], FP32)
        xt = [[sb(f"xt{c}{n}", [K3, HC, TB], BF16) for n in range(2)] for c in range(DC)]
        wb = [sb(f"wb{c}", [P, E2, TB], FP32) for c in range(DC)]
        hm = [sb(f"hm{n}", [F2, 2 * TB], FP32) for n in range(HB)]
        weighed_ = [sb(f"we{n}", [P, TB], FP32) for n in range(2)]
        acc = [sb(f"acc{c}", [P, TB], FP32) for c in range(DC)]
        pu = [ctx.enter_context(nc.psum_tensor(f"x_pu{n}", [F2, 2 * TB], FP32)) for n in range(2)]
        pe_ = [ctx.enter_context(nc.psum_tensor(f"x_pe{n}", [P, TB], FP32)) for n in range(2)]
        po = ctx.enter_context(nc.psum_tensor("x_po", [P, TT * D], FP32))
        w_in, w1_ready, own = sem("w_in"), sem("w1_ready"), sem("own")
        t_in = [sem(f"t_in{c}") for c in range(DC)]
        up, active, down, taken, summed = sem("up"), sem("active"), sem("down"), sem("taken"), sem("summed")
        projected, added, out_done = sem("projected"), sem("added"), sem("out_done")
        LOADS = 6 + HC
        N = E2 * 2
        WEIGHTS = 3 + 1 + 1 + HC + 2
        block = ctx.enter_context(nc.Block())

        def blocks(eng, body):
            body(0, True)
            with eng.Fori(1, NB) as i:
                body(i, False)

        @block.sync
        def _(sp):
            for n in range(3):
                sp.dma_start(w1f[n * HD:(n + 1) * HD, :, :], d["L1_ffn_W1"].rearrange("e k f -> k e f")).then_inc(w_in, 16)
            with nc.allow_non_contiguous_dma(reason="biases as columns"):
                sp.dma_start(b1[:], d["L1_ffn_b1"].rearrange("e f -> f e")).then_inc(w_in, 16)
                for a in range(HC):
                    sp.dma_start(b2[a * HD:(a + 1) * HD, :], d["L1_ffn_b2"].rearrange("e f -> f e")).then_inc(w_in, 16)
            sp.dma_start(w2[:], d["L1_ffn_W2"].rearrange("e f o -> f e o")).then_inc(w_in, 16)
            sp.dma_start(wo[:], d["L1_ffn_Wo"].rearrange("(k p) n -> p k n", p=P)).then_inc(w_in, 16)
            sp.dma_start(bo[:], d["L1_ffn_bo"].rearrange("(a n) -> a n", a=1)).then_inc(w_in, 16)

            def body(i, first):
                for c in range(DC):
                    if not first:
                        hold(sp, summed, (i - 1) * DC + c + 1, m.passed)
                    for n, parts in enumerate(((0, 1, 2), (0, 1, 0))):
                        for r, g in enumerate(parts):
                            src = d["t_parts"][g * D + c * P:g * D + (c + 1) * P, bass.ds(i * TB, TB)]
                            sp.dma_start(xt[c][n][r * HD:(r + 1) * HD, :, :], src.rearrange("(a r) c -> r a c", a=HC)
                                         ).then_inc(t_in[c], 16)
                    for a in range(HC):
                        rows = bass.ds(i * P + (c * HC + a) * E2, E2)
                        src = d["w_t"][rows, :].rearrange("(o e) c -> o (e c)", o=1).to_broadcast([HD, E2 * TB])
                        sp.dma_start(wb[c][a * HD:(a + 1) * HD, :, :].rearrange("p e c -> p (e c)"), src
                                     ).then_inc(t_in[c], 16)
                if not first:
                    store(i - 1)

            def store(i):
                hold(sp, added, i + 1, m.passed)
                sp.dma_start(d["out_rows"][bass.ds(i * TB, TB), :].rearrange("(j p) d -> p j d", p=P),
                             m.x[:, bass.ds(i * TT, TT), :]).then_inc(out_done, 16)
            blocks(sp, body)
            store(NB - 1)
            sp.wait_ge(out_done, 16 * NB)

        @block.gpsimd
        def _(pool):
            pool.nop()

        @block.scalar
        def _(act):
            act.wait_ge(w_in, 16 * WEIGHTS)

            def body(i, first):
                for c in range(DC):
                    for n in range(N):
                        base = i * (DC * N) + (c * N + n)
                        act.wait_ge(up, base + 1)
                        if not (first and c * N + n < HB):
                            act.wait_ge(down, base + 1 - HB)
                        nc.scalar.activation(hm[n % HB][:], pu[n % 2][:], ACT.Gelu, bias=b1[:, n // 2:n // 2 + 1]
                                             ).then_inc(active, 1)
            blocks(act, body)

        @block.vector
        def _(dve):
            link = Chain(dve, own)
            V = nc.vector
            dve.wait_ge(w_in, 16 * WEIGHTS)
            link(V.tensor_copy(w1[0][:], w1f[:]))
            link(V.tensor_tensor(w1r[:], w1f[:], w1[0][:], ALU.subtract))
            link(V.tensor_copy(w1m[:], w1r[:]))
            V.tensor_copy(w1[1][0:2 * HD], w1m[0:2 * HD]).then_inc(w1_ready, 1)
            V.tensor_tensor(w1[1][2 * HD:K3], w1r[2 * HD:K3], w1m[2 * HD:K3], ALU.subtract).then_inc(w1_ready, 1)
            START = link.n
            CH = 2 * E2 - 1

            def result(i):
                dve.wait_ge(projected, i + 1)
                V.tensor_tensor(x_block(m, i), x_block(m, i), po[:], ALU.add).then_inc(added, 1)

            def body(i, first):
                for c in range(DC):
                    link.at(i * (DC * CH) + (START + c * CH))
                    if c == 1 and not first:
                        result(i - 1)
                    for e in range(E2):
                        dve.wait_ge(down, i * (DC * N) + (c * N + 2 * e + 2))
                        if e == 0:
                            dve.wait_ge(t_in[c], (i + 1) * (16 * LOADS))
                            if not first:
                                dve.wait_ge(projected, i)
                        to = weighed_[e % 2] if e else acc[c]
                        ins = V.scalar_tensor_tensor(out=to[:], in0=pe_[e % 2][:], scalar=b2[:, e:e + 1],
                                                     in1=wb[c][:, e, :], op0=ALU.add, op1=ALU.mult)
                        link(ins)
                        dve.sem_inc(taken, 1)
                        if e:
                            link(V.tensor_tensor(acc[c][:], acc[c][:], to[:], ALU.add))
                    dve.sem_inc(summed, 1)
            blocks(dve, body)
            result(NB - 1)

        @block.tensor
        def _(pe):
            pe.wait_ge(w1_ready, 2)

            def project(i):
                pe.wait_ge(summed, (i + 1) * DC)
                if not isinstance(i, int) or i > 0:
                    pe.wait_ge(added, i)
                for j in range(TT):
                    to = po[:, j * D:(j + 1) * D]
                    for c in range(DC):
                        nc.tensor.matmul(to, acc[c][:, j * P:(j + 1) * P], wo[:, c, :], start=c == 0, stop=False)
                    last = nc.tensor.matmul(to, m.ones[0:1, :], bo[:], start=False, stop=True)
                last.then_inc(projected, 1)

            def lower(i, c, n):
                base = i * (DC * N) + (c * N + n)
                pe.wait_ge(active, base + 1)
                e, pair = n // 2, n % 2
                if pair == 0 and not (isinstance(i, int) and i == 0 and c == 0 and e < 2):
                    pe.wait_ge(taken, i * (DC * E2) + (c * E2 + e - 1))
                for a in range(2):
                    g = 2 * pair + a
                    last = nc.tensor.matmul(pe_[e % 2][g * HD:(g + 1) * HD, :], w2[:, e, :],
                                            hm[n % HB][:, a * TB:(a + 1) * TB], start=True, stop=True)
                last.then_inc(down, 1)

            def body(i, first):
                for c in range(DC):
                    for n in range(N):
                        base = i * (DC * N) + (c * N + n)
                        if n == 0:
                            pe.wait_ge(t_in[c], (i + 1) * (16 * LOADS))
                        if not (first and c == 0 and n < 2):
                            pe.wait_ge(active, base - 1)
                        e, pair = n // 2, n % 2
                        for a in range(2):
                            for s in range(2):
                                last = nc.tensor.matmul(pu[n % 2][:, a * TB:(a + 1) * TB], w1[s][:, e, :],
                                                        xt[c][s][:, 2 * pair + a, :], start=s == 0, stop=s == 1)
                        last.then_inc(up, 1)
                        if n >= 2:
                            lower(i, c, n - 2)
                        elif c:
                            lower(i, c - 1, N - 2 + n)
                        elif not first:
                            lower(i - 1, DC - 1, N - 2 + n)
                        if n == 3 and c == 0 and not first:
                            project(i - 1)
            blocks(pe, body)
            for n in (N - 2, N - 1):
                lower(NB - 1, DC - 1, n)
            project(NB - 1)


_SCRATCH = (("q_parts0", (3 * D, T), BF16), ("q_parts1", (3 * D, T), BF16), ("k_parts0", (3 * D, S), BF16),
            ("k_parts1", (3 * D, S), BF16), ("sums", (H * P, TB), FP32),
            ("inverses", (H * NB, TB), FP32), ("t_parts", (3 * D, T), BF16), ("w_t", (NB * HM * E2, TB), FP32),
            ("slots_in", (T, D), FP32), ("slots_out", (T, D), FP32))


def program(nc, d, out):
    d = dict(d)
    for name, shape, dt in _SCRATCH:
        d[name] = nc.dram_tensor(name, shape, dt, kind="Internal").ap()
    for n in ("q_parts", "k_parts"):
        d[n] = [d[n + "0"], d[n + "1"]]
    d["x_rows"] = d["x"].rearrange("a t d -> (a t) d")
    d["out_rows"] = out.rearrange("a t d -> (a t) d")
    fast = Path("f", list(range(FAST_FROM, KT)), 4, row=True, lead=3, rest=0.7)
    full = Path("a", list(range(KT)), 4, masked=True)
    causal = Path("c", list(range(KT)), 4, causal=True, lead=6)
    with ExitStack() as ctx:
        m = place_shared(nc, ctx)
        with nc.sbuf_tensor("mask", [P, NT * S], BF16) as mask:
            prepare(nc, m, d, mask)
            attend(nc, m, d, 0, [fast, full], mask)
        m.x = ctx.enter_context(nc.sbuf_tensor("x", [P, NT, D], FP32))
        m.clear_semaphores(nc)
        router(nc, m, d)
        experts(nc, m, d)
        gather(nc, m, d)
        m.clear_semaphores(nc)
        attend(nc, m, d, 1, [causal])
        weights_of_experts(nc, m, d)
        head_experts(nc, m, d)


_INS = ['x', 'ctx_1024', 'mask_Bx1xSxS2_bk1'] + [
    f'L{l}_xattn_{n}' for l in range(2) for n in ('Wq', 'bq', 'Wk', 'bk', 'Wv', 'bv', 'Wo', 'bo')] + [
    f'L0_ffn_{n}' for n in ('Wr', 'br', 'W1', 'b1', 'W2', 'b2')] + [
    f'L1_ffn_{n}' for n in ('Wm', 'bm', 'expert_emb', 'W1', 'b1', 'W2', 'b2', 'Wo', 'bo')]


def kernel(**inputs):
    import numpy as np
    import concourse.bacc as bacc
    from concourse.bass_utils import run_bass_kernel_spmd

    nc = bacc.Bacc("TRN2", target_bir_lowering=False, num_devices=1)
    arrays, d = {}, {}
    for name in _INS:
        a = np.ascontiguousarray(inputs[name])
        arrays["in_" + name] = a
        d[name] = nc.dram_tensor("in_" + name, a.shape, mybir.dt.from_np(a.dtype), kind="ExternalInput").ap()
    d["mask"] = d["mask_Bx1xSxS2_bk1"]
    out = nc.dram_tensor("out_0", (1, T, D), FP32, kind="ExternalOutput").ap()
    program(nc, d, out)
    return run_bass_kernel_spmd(nc, [arrays], core_ids=[0]).results[0]["out_0"]
```
